# Optimizing a Trainium2 kernel written in Bass

```python
import numpy as np
import jax
import jax.numpy as jnp

def _softmax(x, axis=-1):
    return jax.nn.softmax(x, axis=axis)
def _gelu(x):
    return jax.nn.gelu(x, approximate=True)
def _silu(x):
    return jax.nn.silu(x)
def _sigmoid(x):
    return jax.nn.sigmoid(x)
def _layernorm(x, axis=-1, eps=1e-5):
    m = jnp.mean(x, axis=axis, keepdims=True)
    v = jnp.var(x, axis=axis, keepdims=True)
    return (x - m) / jnp.sqrt(v + eps)
def _scatter_add(tgt, idx, src, axis=0):
    return tgt.at[idx].add(src)
def _segment_sum(src, seg, n):
    return jax.ops.segment_sum(src, seg, n)

kernel_name = 'mk_metaformer_d2_conv_nhwc256_2bb8c1'

def setup_inputs(seed: int = 0):
    np.random.seed(seed)
    _w = jnp.asarray
    def _rec_inputs():
        import jax
        import jax.numpy as jnp
        _gk = jax.random.key(seed)
        x = -0.000929 + 1 * jax.random.normal(jax.random.fold_in(_gk, 1), (4, 32, 32, 256), jnp.float32)
        return x
    x = _rec_inputs()
    def _L0_conv_setup():
        import jax, jax.numpy as jnp
        import numpy as np
        DIM = 256
        INNER = 512
        NH = 8
        DH = INNER // NH
        NB = INNER // 4
        BS = 4
        K = 4
        EPS = 1e-06
        LN_EPS = 1e-05

        def _mlstm_forward(x, W_up, conv_w, conv_b, Wq, Wk, Wv, W_i, b_i, W_f, b_f, norm_w, skip, W_down):
            B, H, W, C = x.shape
            S = H * W
            xs = x.reshape(B, S, C)
            up = xs @ W_up.T
            x_m, z = (up[..., :INNER], up[..., INNER:])
            xp = jnp.pad(x_m, ((0, 0), (K - 1, 0), (0, 0)))
            x_conv = conv_b + sum((xp[:, k:k + S, :] * conv_w[:, 0, k] for k in range(K)))
            x_act = jax.nn.silu(x_conv)
            xa = x_act.reshape(B, S, NB, BS)
            q = jnp.einsum('bsnd,nod->bsno', xa, Wq).reshape(B, S, INNER)
            k = jnp.einsum('bsnd,nod->bsno', xa, Wk).reshape(B, S, INNER)
            xv = x_m.reshape(B, S, NB, BS)
            v = jnp.einsum('bsnd,nod->bsno', xv, Wv).reshape(B, S, INNER)
            gate_in = jnp.concatenate([q, k, v], axis=-1)
            ig = (gate_in @ W_i.T + b_i).transpose(0, 2, 1)
            fg = (gate_in @ W_f.T + b_f).transpose(0, 2, 1)
            qh = q.reshape(B, S, NH, DH).transpose(0, 2, 1, 3)
            kh = k.reshape(B, S, NH, DH).transpose(0, 2, 1, 3) / np.sqrt(DH)
            vh = v.reshape(B, S, NH, DH).transpose(0, 2, 1, 3)
            lf = jax.nn.log_sigmoid(fg)
            lc = jnp.cumsum(lf, axis=-1)
            M = lc[..., :, None] - lc[..., None, :]
            mask = jnp.tril(jnp.ones((S, S), dtype=bool))
            logD = jnp.where(mask, M + ig[..., None, :], -jnp.inf)
            m = jnp.max(logD, axis=-1, keepdims=True)
            D = jnp.exp(logD - m)
            Cmat = jnp.einsum('bhid,bhjd->bhij', qh, kh) * D
            norm = jnp.maximum(jnp.abs(Cmat.sum(-1, keepdims=True)), jnp.exp(-m))
            h_cell = jnp.einsum('bhij,bhjd->bhid', Cmat / (norm + EPS), vh)
            mu = h_cell.mean(-1, keepdims=True)
            var = h_cell.var(-1, keepdims=True)
            hn = (h_cell - mu) / jnp.sqrt(var + LN_EPS)
            hn = hn * norm_w.reshape(NH, 1, DH)
            h = hn.transpose(0, 2, 1, 3).reshape(B, S, INNER)
            h = h + skip * x_act
            h = h * jax.nn.silu(z)
            out = h @ W_down.T
            return out.reshape(B, H, W, C)
        key = jax.random.key(seed)
        ks = jax.random.split(key, 14)
        f32 = jnp.float32
        return {'x': jax.random.normal(ks[0], (4, 32, 32, DIM), f32), 'W_up': jax.random.normal(ks[1], (2 * INNER, DIM), f32) * 0.05, 'conv_w': jax.random.normal(ks[2], (INNER, 1, K), f32) * 0.3, 'conv_b': jax.random.normal(ks[3], (INNER,), f32) * 0.05, 'Wq': jax.random.normal(ks[4], (NB, BS, BS), f32) * 0.3, 'Wk': jax.random.normal(ks[5], (NB, BS, BS), f32) * 0.3, 'Wv': jax.random.normal(ks[6], (NB, BS, BS), f32) * 0.3, 'W_i': jax.random.normal(ks[7], (NH, 3 * INNER), f32) * 0.02, 'b_i': jax.random.normal(ks[8], (NH,), f32) * 0.1, 'W_f': jax.random.normal(ks[9], (NH, 3 * INNER), f32) * 0.02, 'b_f': jax.random.normal(ks[10], (NH,), f32) * 0.1, 'norm_w': jnp.ones((INNER,), f32), 'skip': jax.random.normal(ks[11], (INNER,), f32) * 0.1, 'W_down': jax.random.normal(ks[12], (DIM, INNER), f32) * 0.05}
    _L0_conv_all = _L0_conv_setup()
    _L0_conv_in = {k: v for k, v in _L0_conv_all.items() if k in ('W_up', 'conv_w', 'conv_b', 'Wq', 'Wk', 'Wv', 'W_i', 'b_i', 'W_f', 'b_f', 'norm_w', 'skip', 'W_down', )}
    del _L0_conv_all

    def _L0_ffn_setup():
        import math
        import jax, jax.numpy as jnp
        import numpy as np
        CAPACITY_FACTOR = 1.25
        TOP_K = 2
        LN_EPS = 1e-05

        def _layer_norm(x, gamma, beta):
            mu = jnp.mean(x, axis=-1, keepdims=True)
            var = jnp.var(x, axis=-1, keepdims=True)
            return (x - mu) * jax.lax.rsqrt(var + LN_EPS) * gamma + beta
        key = jax.random.key(seed)
        ks = jax.random.split(key, 4)
        B, S, D, F, E = (8, 4096, 256, 512, 8)
        x = jax.random.normal(ks[0], (B, S, D), dtype=jnp.float32)
        Wr = jax.random.normal(ks[1], (D, E), dtype=jnp.float32) / np.sqrt(D)
        br = jnp.zeros((E,), jnp.float32)
        W1 = jax.random.normal(ks[2], (E, D, F), dtype=jnp.float32) / np.sqrt(D)
        b1 = jnp.zeros((E, F), jnp.float32)
        W2 = jax.random.normal(ks[3], (E, F, D), dtype=jnp.float32) / np.sqrt(F)
        b2 = jnp.zeros((E, D), jnp.float32)
        gamma = jnp.ones((D,), jnp.float32)
        beta = jnp.zeros((D,), jnp.float32)
        return {'x': x, 'Wr': Wr, 'br': br, 'W1': W1, 'b1': b1, 'W2': W2, 'b2': b2, 'gamma': gamma, 'beta': beta}
    _L0_ffn_all = _L0_ffn_setup()
    _L0_ffn_in = {k: v for k, v in _L0_ffn_all.items() if k in ('Wr', 'br', 'W1', 'b1', 'W2', 'b2', 'gamma', 'beta', )}
    del _L0_ffn_all

    def _L1_conv_setup():
        import jax, jax.numpy as jnp
        import numpy as np
        NEG_SLOPE = 0.01
        LN_EPS = 1e-05
        L2_EPS = 1e-12
        key = jax.random.key(seed)
        ks = jax.random.split(key, 8)
        B, T, N, C = (16, 32, 64, 256)
        local_feat = jax.random.normal(ks[0], (B, T, N, C), dtype=jnp.float32)
        global_feat = jax.random.normal(ks[1], (B, C), dtype=jnp.float32)
        pos = jax.random.normal(ks[2], (B, T * N, 3), dtype=jnp.float32)
        adj_w = jax.random.normal(ks[3], (C, C), dtype=jnp.float32) * (1.0 / np.sqrt(C))
        affine_w = jax.random.normal(ks[4], (C, C), dtype=jnp.float32) * np.sqrt(2.0 / C)
        affine_b = jnp.zeros((C,), dtype=jnp.float32)
        ln_g = jnp.ones((C,), dtype=jnp.float32)
        ln_b = jnp.zeros((C,), dtype=jnp.float32)
        return {'local_feat': local_feat, 'global_feat': global_feat, 'pos': pos, 'adj_w': adj_w, 'affine_w': affine_w, 'affine_b': affine_b, 'ln_g': ln_g, 'ln_b': ln_b}
    _L1_conv_all = _L1_conv_setup()
    _L1_conv_in = {k: v for k, v in _L1_conv_all.items() if k in ('global_feat', 'pos', 'adj_w', 'affine_w', 'affine_b', 'ln_g', 'ln_b', )}
    del _L1_conv_all

    def _L1_ffn_setup():
        import math
        import jax, jax.numpy as jnp
        import numpy as np
        CAPACITY_FACTOR = 1.25
        TOP_K = 2
        LN_EPS = 1e-05

        def _layer_norm(x, gamma, beta):
            mu = jnp.mean(x, axis=-1, keepdims=True)
            var = jnp.var(x, axis=-1, keepdims=True)
            return (x - mu) * jax.lax.rsqrt(var + LN_EPS) * gamma + beta
        key = jax.random.key(seed)
        ks = jax.random.split(key, 4)
        B, S, D, F, E = (8, 4096, 256, 512, 8)
        x = jax.random.normal(ks[0], (B, S, D), dtype=jnp.float32)
        Wr = jax.random.normal(ks[1], (D, E), dtype=jnp.float32) / np.sqrt(D)
        br = jnp.zeros((E,), jnp.float32)
        W1 = jax.random.normal(ks[2], (E, D, F), dtype=jnp.float32) / np.sqrt(D)
        b1 = jnp.zeros((E, F), jnp.float32)
        W2 = jax.random.normal(ks[3], (E, F, D), dtype=jnp.float32) / np.sqrt(F)
        b2 = jnp.zeros((E, D), jnp.float32)
        gamma = jnp.ones((D,), jnp.float32)
        beta = jnp.zeros((D,), jnp.float32)
        return {'x': x, 'Wr': Wr, 'br': br, 'W1': W1, 'b1': b1, 'W2': W2, 'b2': b2, 'gamma': gamma, 'beta': beta}
    _L1_ffn_all = _L1_ffn_setup()
    _L1_ffn_in = {k: v for k, v in _L1_ffn_all.items() if k in ('Wr', 'br', 'W1', 'b1', 'W2', 'b2', 'gamma', 'beta', )}
    del _L1_ffn_all

    return {
        "x": x,
        "L0_conv_W_up": _L0_conv_in["W_up"],
        "L0_conv_conv_w": _L0_conv_in["conv_w"],
        "L0_conv_conv_b": _L0_conv_in["conv_b"],
        "L0_conv_Wq": _L0_conv_in["Wq"],
        "L0_conv_Wk": _L0_conv_in["Wk"],
        "L0_conv_Wv": _L0_conv_in["Wv"],
        "L0_conv_W_i": _L0_conv_in["W_i"],
        "L0_conv_b_i": _L0_conv_in["b_i"],
        "L0_conv_W_f": _L0_conv_in["W_f"],
        "L0_conv_b_f": _L0_conv_in["b_f"],
        "L0_conv_norm_w": _L0_conv_in["norm_w"],
        "L0_conv_skip": _L0_conv_in["skip"],
        "L0_conv_W_down": _L0_conv_in["W_down"],
        "L0_ffn_Wr": _L0_ffn_in["Wr"],
        "L0_ffn_br": _L0_ffn_in["br"],
        "L0_ffn_W1": _L0_ffn_in["W1"],
        "L0_ffn_b1": _L0_ffn_in["b1"],
        "L0_ffn_W2": _L0_ffn_in["W2"],
        "L0_ffn_b2": _L0_ffn_in["b2"],
        "L0_ffn_gamma": _L0_ffn_in["gamma"],
        "L0_ffn_beta": _L0_ffn_in["beta"],
        "L1_conv_global_feat": _L1_conv_in["global_feat"],
        "L1_conv_pos": _L1_conv_in["pos"],
        "L1_conv_adj_w": _L1_conv_in["adj_w"],
        "L1_conv_affine_w": _L1_conv_in["affine_w"],
        "L1_conv_affine_b": _L1_conv_in["affine_b"],
        "L1_conv_ln_g": _L1_conv_in["ln_g"],
        "L1_conv_ln_b": _L1_conv_in["ln_b"],
        "L1_ffn_Wr": _L1_ffn_in["Wr"],
        "L1_ffn_br": _L1_ffn_in["br"],
        "L1_ffn_W1": _L1_ffn_in["W1"],
        "L1_ffn_b1": _L1_ffn_in["b1"],
        "L1_ffn_W2": _L1_ffn_in["W2"],
        "L1_ffn_b2": _L1_ffn_in["b2"],
        "L1_ffn_gamma": _L1_ffn_in["gamma"],
        "L1_ffn_beta": _L1_ffn_in["beta"],
    }

def reference(x, L0_conv_W_up, L0_conv_conv_w, L0_conv_conv_b, L0_conv_Wq, L0_conv_Wk, L0_conv_Wv, L0_conv_W_i, L0_conv_b_i, L0_conv_W_f, L0_conv_b_f, L0_conv_norm_w, L0_conv_skip, L0_conv_W_down, L0_ffn_Wr, L0_ffn_br, L0_ffn_W1, L0_ffn_b1, L0_ffn_W2, L0_ffn_b2, L0_ffn_gamma, L0_ffn_beta, L1_conv_global_feat, L1_conv_pos, L1_conv_adj_w, L1_conv_affine_w, L1_conv_affine_b, L1_conv_ln_g, L1_conv_ln_b, L1_ffn_Wr, L1_ffn_br, L1_ffn_W1, L1_ffn_b1, L1_ffn_W2, L1_ffn_b2, L1_ffn_gamma, L1_ffn_beta):
    import jax
    import jax.numpy as jnp
    def _L0_conv_ref(x, W_up, conv_w, conv_b, Wq, Wk, Wv, W_i, b_i, W_f, b_f, norm_w, skip, W_down):
        import jax, jax.numpy as jnp
        import numpy as np
        DIM = 256
        INNER = 512
        NH = 8
        DH = INNER // NH
        NB = INNER // 4
        BS = 4
        K = 4
        EPS = 1e-06
        LN_EPS = 1e-05

        def _mlstm_forward(x, W_up, conv_w, conv_b, Wq, Wk, Wv, W_i, b_i, W_f, b_f, norm_w, skip, W_down):
            B, H, W, C = x.shape
            S = H * W
            xs = x.reshape(B, S, C)
            up = xs @ W_up.T
            x_m, z = (up[..., :INNER], up[..., INNER:])
            xp = jnp.pad(x_m, ((0, 0), (K - 1, 0), (0, 0)))
            x_conv = conv_b + sum((xp[:, k:k + S, :] * conv_w[:, 0, k] for k in range(K)))
            x_act = jax.nn.silu(x_conv)
            xa = x_act.reshape(B, S, NB, BS)
            q = jnp.einsum('bsnd,nod->bsno', xa, Wq).reshape(B, S, INNER)
            k = jnp.einsum('bsnd,nod->bsno', xa, Wk).reshape(B, S, INNER)
            xv = x_m.reshape(B, S, NB, BS)
            v = jnp.einsum('bsnd,nod->bsno', xv, Wv).reshape(B, S, INNER)
            gate_in = jnp.concatenate([q, k, v], axis=-1)
            ig = (gate_in @ W_i.T + b_i).transpose(0, 2, 1)
            fg = (gate_in @ W_f.T + b_f).transpose(0, 2, 1)
            qh = q.reshape(B, S, NH, DH).transpose(0, 2, 1, 3)
            kh = k.reshape(B, S, NH, DH).transpose(0, 2, 1, 3) / np.sqrt(DH)
            vh = v.reshape(B, S, NH, DH).transpose(0, 2, 1, 3)
            lf = jax.nn.log_sigmoid(fg)
            lc = jnp.cumsum(lf, axis=-1)
            M = lc[..., :, None] - lc[..., None, :]
            mask = jnp.tril(jnp.ones((S, S), dtype=bool))
            logD = jnp.where(mask, M + ig[..., None, :], -jnp.inf)
            m = jnp.max(logD, axis=-1, keepdims=True)
            D = jnp.exp(logD - m)
            Cmat = jnp.einsum('bhid,bhjd->bhij', qh, kh) * D
            norm = jnp.maximum(jnp.abs(Cmat.sum(-1, keepdims=True)), jnp.exp(-m))
            h_cell = jnp.einsum('bhij,bhjd->bhid', Cmat / (norm + EPS), vh)
            mu = h_cell.mean(-1, keepdims=True)
            var = h_cell.var(-1, keepdims=True)
            hn = (h_cell - mu) / jnp.sqrt(var + LN_EPS)
            hn = hn * norm_w.reshape(NH, 1, DH)
            h = hn.transpose(0, 2, 1, 3).reshape(B, S, INNER)
            h = h + skip * x_act
            h = h * jax.nn.silu(z)
            out = h @ W_down.T
            return out.reshape(B, H, W, C)
        return _mlstm_forward(x, W_up, conv_w, conv_b, Wq, Wk, Wv, W_i, b_i, W_f, b_f, norm_w, skip, W_down)

    def _L0_ffn_ref(x, Wr, br, W1, b1, W2, b2, gamma, beta):
        import math
        import jax, jax.numpy as jnp
        import numpy as np
        CAPACITY_FACTOR = 1.25
        TOP_K = 2
        LN_EPS = 1e-05

        def _layer_norm(x, gamma, beta):
            mu = jnp.mean(x, axis=-1, keepdims=True)
            var = jnp.var(x, axis=-1, keepdims=True)
            return (x - mu) * jax.lax.rsqrt(var + LN_EPS) * gamma + beta
        B, S, D = x.shape
        E = Wr.shape[1]
        N = B * S
        K = TOP_K
        logits = jnp.mean(x, axis=1) @ Wr + br
        routing_weights = jax.nn.softmax(logits, axis=-1)
        capacity = float(math.ceil(N * CAPACITY_FACTOR / E))
        expected_loads = routing_weights.sum(axis=0) * (N / B)
        scale = jnp.where(expected_loads > capacity, capacity / expected_loads, 1.0)
        routing_weights = jax.nn.softmax(routing_weights * scale, axis=-1)
        rw_tok = jnp.broadcast_to(routing_weights[:, None, :], (B, S, E)).reshape(N, E)
        top_w, top_i = jax.lax.top_k(rw_tok, K)
        top_w = jax.nn.softmax(top_w, axis=-1)
        xf = x.reshape(N, D)
        h = jax.nn.gelu(jnp.einsum('nd,edf->enf', xf, W1) + b1[:, None, :], approximate=False)
        y = jnp.einsum('enf,efd->end', h, W2) + b2[:, None, :]
        w_dense = jnp.zeros((N, E), x.dtype).at[jnp.arange(N)[:, None], top_i].add(top_w)
        out = jnp.einsum('ne,end->nd', w_dense, y).reshape(B, S, D)
        out = _layer_norm(out + x, gamma, beta)
        return out

    def _L1_conv_ref(local_feat, global_feat, pos, adj_w, affine_w, affine_b, ln_g, ln_b):
        import jax, jax.numpy as jnp
        import numpy as np
        NEG_SLOPE = 0.01
        LN_EPS = 1e-05
        L2_EPS = 1e-12
        B, T, N, C = local_feat.shape
        x = local_feat.reshape(B, T * N, C)
        nrm = jnp.sqrt(jnp.sum(x * x, axis=-1, keepdims=True))
        nf = x / jnp.maximum(nrm, L2_EPS)
        A = jnp.einsum('bnc,cd,bmd->bnm', nf, adj_w, nf)
        A = 5.0 * (A - jnp.max(A, axis=-1, keepdims=True))
        A = jax.nn.softmax(A, axis=-1)
        h = jnp.einsum('bmc,dc->bmd', x, affine_w) + affine_b
        h = jnp.einsum('bnm,bmc->bnc', A, h)
        mu = jnp.mean(h, axis=-1, keepdims=True)
        var = jnp.mean(jnp.square(h - mu), axis=-1, keepdims=True)
        h = (h - mu) / jnp.sqrt(var + LN_EPS) * ln_g + ln_b
        h = jnp.where(h >= 0, h, NEG_SLOPE * h)
        return h.reshape(B, T, N, C)

    def _L1_ffn_ref(x, Wr, br, W1, b1, W2, b2, gamma, beta):
        import math
        import jax, jax.numpy as jnp
        import numpy as np
        CAPACITY_FACTOR = 1.25
        TOP_K = 2
        LN_EPS = 1e-05

        def _layer_norm(x, gamma, beta):
            mu = jnp.mean(x, axis=-1, keepdims=True)
            var = jnp.var(x, axis=-1, keepdims=True)
            return (x - mu) * jax.lax.rsqrt(var + LN_EPS) * gamma + beta
        B, S, D = x.shape
        E = Wr.shape[1]
        N = B * S
        K = TOP_K
        logits = jnp.mean(x, axis=1) @ Wr + br
        routing_weights = jax.nn.softmax(logits, axis=-1)
        capacity = float(math.ceil(N * CAPACITY_FACTOR / E))
        expected_loads = routing_weights.sum(axis=0) * (N / B)
        scale = jnp.where(expected_loads > capacity, capacity / expected_loads, 1.0)
        routing_weights = jax.nn.softmax(routing_weights * scale, axis=-1)
        rw_tok = jnp.broadcast_to(routing_weights[:, None, :], (B, S, E)).reshape(N, E)
        top_w, top_i = jax.lax.top_k(rw_tok, K)
        top_w = jax.nn.softmax(top_w, axis=-1)
        xf = x.reshape(N, D)
        h = jax.nn.gelu(jnp.einsum('nd,edf->enf', xf, W1) + b1[:, None, :], approximate=False)
        y = jnp.einsum('enf,efd->end', h, W2) + b2[:, None, :]
        w_dense = jnp.zeros((N, E), x.dtype).at[jnp.arange(N)[:, None], top_i].add(top_w)
        out = jnp.einsum('ne,end->nd', w_dense, y).reshape(B, S, D)
        out = _layer_norm(out + x, gamma, beta)
        return out

    def _gn(v, G=32, eps=1e-5):
        B_, H_, W_, C_ = v.shape
        g = v.reshape(B_, H_, W_, G, C_ // G)
        m = jnp.mean(g, axis=(1, 2, 4), keepdims=True)
        s = jnp.var(g, axis=(1, 2, 4), keepdims=True)
        return ((g - m) / jnp.sqrt(s + eps)).reshape(v.shape)

    def _ln_c(v, eps=1e-6):
        m = jnp.mean(v, axis=-1, keepdims=True)
        s = jnp.var(v, axis=-1, keepdims=True)
        return (v - m) / jnp.sqrt(s + eps)

    def _ln_t(v, eps=1e-5):
        m = jnp.mean(v, axis=-1, keepdims=True)
        s = jnp.var(v, axis=-1, keepdims=True)
        return (v - m) / jnp.sqrt(s + eps)

    def _to_tokens(v):
        B_, H_, W_, C_ = v.shape
        return v.reshape(B_, H_ * W_, C_)
    def _from_tokens(t, like):
        return t.reshape(like.shape)

    x = x + _L0_conv_ref(_ln_c(x), L0_conv_W_up, L0_conv_conv_w, L0_conv_conv_b, L0_conv_Wq, L0_conv_Wk, L0_conv_Wv, L0_conv_W_i, L0_conv_b_i, L0_conv_W_f, L0_conv_b_f, L0_conv_norm_w, L0_conv_skip, L0_conv_W_down)
    t = _to_tokens(x)
    t = t + _L0_ffn_ref(_ln_t(t), L0_ffn_Wr, L0_ffn_br, L0_ffn_W1, L0_ffn_b1, L0_ffn_W2, L0_ffn_b2, L0_ffn_gamma, L0_ffn_beta)
    x = _from_tokens(t, x)
    x = x + _L1_conv_ref(_ln_c(x), L1_conv_global_feat, L1_conv_pos, L1_conv_adj_w, L1_conv_affine_w, L1_conv_affine_b, L1_conv_ln_g, L1_conv_ln_b)
    t = _to_tokens(x)
    t = t + _L1_ffn_ref(_ln_t(t), L1_ffn_Wr, L1_ffn_br, L1_ffn_W1, L1_ffn_b1, L1_ffn_W2, L1_ffn_b2, L1_ffn_gamma, L1_ffn_beta)
    x = _from_tokens(t, x)
    return x


_drawn_inputs = setup_inputs


def setup_inputs(seed=0):
    import zlib

    import numpy as np

    out = dict(_drawn_inputs(seed))
    spreads = {'L0_conv_norm_w': (1.0, 0.2),
     'L0_ffn_br': (0.0, 0.1),
     'L0_ffn_b1': (0.0, 0.1),
     'L0_ffn_b2': (0.0, 0.1),
     'L0_ffn_gamma': (1.0, 0.2),
     'L0_ffn_beta': (0.0, 0.1),
     'L1_conv_affine_b': (0.0, 0.1),
     'L1_conv_ln_g': (1.0, 0.2),
     'L1_conv_ln_b': (0.0, 0.1),
     'L1_ffn_br': (0.0, 0.8),
     'L1_ffn_b1': (0.0, 0.601),
     'L1_ffn_b2': (0.0, 0.418),
     'L1_ffn_gamma': (1.0, 0.2),
     'L1_ffn_beta': (0.0, 0.268)}
    factors = {'L0_conv_b_i': 5.663, 'L0_conv_b_f': 5.307, 'L0_conv_skip': 4.263, 'L0_ffn_Wr': 8.0}
    for name, (base, spread) in spreads.items():
        noise = np.random.default_rng([zlib.crc32(name.encode()), seed]).standard_normal(out[name].shape)
        drawn = base * np.exp(spread * noise) if base else spread * noise
        out[name] = jnp.asarray(drawn.astype(out[name].dtype))
    for name, factor in factors.items():
        out[name] = (out[name] * factor).astype(out[name].dtype)
    return out
```

```python
from contextlib import ExitStack, contextmanager

import numpy as np

import concourse.bass as bass
from concourse import mybir

F32 = mybir.dt.float32
F16 = mybir.dt.float16
BF16 = mybir.dt.bfloat16
U32 = mybir.dt.uint32
I32 = mybir.dt.int32
ALU = mybir.AluOpType
ACT = mybir.ActivationFunctionType
AX_X = mybir.AxisListType.X

P = 128
B = 4
S = 1024
C = 256
KC = C // P
NT = S // P
HALF = S // 2
INNER = 512
MC = INNER // P
NH = 8
DH = INNER // NH
TAPS = 4
VW = DH + 1
NE = 8
TOPK = 2
FF = 512
FC = FF // P
CAPACITY = float(-(-B * S * 1.25 // NE))
GROW = 72

PC_TAP, PC_CB, PC_NW, PC_SKIP = 0, TAPS, TAPS + 1, TAPS + 2
PC_N = TAPS + 3


def slot_head(slot):
    return 4 * (slot // 4) + 2 * (slot % 2) + (slot // 2) % 2


def row(t, i):
    return t[:, bass.ds(i, 1), :].rearrange("p o f -> p (o f)")


def inverse_root(dve, out, x, t):
    dve.tensor_scalar(t.bitcast(I32), x.bitcast(I32), 1, None, ALU.arith_shift_right)
    dve.drain()
    dve.tensor_scalar(out.bitcast(I32), t.bitcast(I32), -1.0, float(0x5F3759DF), ALU.mult, ALU.add)
    dve.drain()
    for _ in range(3):
        dve.tensor_tensor(t, out, out, ALU.mult)
        dve.drain()
        dve.scalar_tensor_tensor(out=t, in0=t, scalar=-0.5, in1=x, op0=ALU.mult, op1=ALU.mult)
        dve.drain()
        dve.scalar_tensor_tensor(out=out, in0=t, scalar=1.5, in1=out, op0=ALU.add, op1=ALU.mult)
        dve.drain()


def product3(pe, out, a, b, start, stop):
    pe.matmul(out, a[0], b[0], start=start, stop=False)
    pe.matmul(out, a[0], b[1], start=False, stop=False)
    return pe.matmul(out, a[1], b[0], start=False, stop=stop)


@contextmanager
def cleared(nc, sems):
    yield
    with nc.Block() as block:
        @block.sync
        def _(sp):
            for s in sems:
                sp.sem_clear(s)


def mixer0(nc, X, K, A, usum):
    sems = []
    with ExitStack() as ctx, cleared(nc, sems), ExitStack() as stage:
        def sb(name, shape, dt=F32):
            return ctx.enter_context(nc.sbuf_tensor("m0_" + name, shape, dt))

        def sem(name):
            sems.append(ctx.enter_context(nc.semaphore(name)))
            return sems[-1]

        ps = [ctx.enter_context(nc.psum_tensor(f"m0_ps{i}", [P, HALF], F32)) for i in range(8)]

        wup = sb("wup", [P, 2, KC, 2 * INNER], F16)
        wdn = sb("wdn", [P, 2, MC, C], F16)
        gk = sb("gk", [P, 2, MC, P], F16)
        wv = sb("wv", [P, 2, MC, P], F16)
        ga = sb("ga", [P, 2, MC, 40], F16)
        gv = sb("gv", [P, 2, MC, 40], F16)
        pc = sb("pc", [P, MC, PC_N])
        gb = sb("gb", [40, 1])
        sel = sb("sel", [GROW, NH, P], BF16)
        pair_sel = sb("pair_sel", [NH, MC, P])
        negmask = sb("negmask", [P, 4, P], BF16)
        ident16 = sb("ident16", [P, P], BF16)
        region_a = sb("region_a", [P, NT * NH * VW])
        region_b = sb("region_b", [P, MC * S])
        sz = sb("sz", [P, MC, S])
        xa = sb("xa", [P, MC, S])
        region_e = sb("region_e", [P, MC * S])
        region_f = sb("region_f", [P, MC * S])
        vext = sb("vext", [P, NT, NH * VW])
        region_h = sb("region_h", [P, NT * C])
        kt = sb("kt", [P, 2, 4 * DH])
        tmp = sb("tmp", [P, 4 * VW])
        state = sb("state", [P, MC, 2 * VW])
        stack = sb("stack", [P, S])
        part_a = sb("part_a", [GROW, S], BF16)
        part_n = sb("part_n", [GROW, S], BF16)
        mid16 = sb("mid16", [NH, 2, S], BF16)
        cols = sb("cols", [P, NT, GROW])
        dec_row = sb("dec_row", [NH, NT])
        dec = sb("dec", [P, MC, NT])
        st6 = sb("st6", [P, NT, 6])
        mv = sb("mv", [P, NT, 2])
        rstd = sb("rstd", [P, NT])
        lnv = sb("lnv", [P, NT])
        sm = sb("sm", [P, 8, NT * NH])

        XW = TAPS - 1 + S
        xm32 = region_a[:, 0:MC * XW].rearrange("p (m t) -> p m t", m=MC)
        rows_a = region_a[0:NH, 0:4 * S].rearrange("p (r t) -> p r t", r=4)
        num = region_a[:, :].rearrange("p (n w) -> p n w", n=NT)
        num4 = region_a[:, :].rearrange("p (n v) -> p n v", v=VW)
        b16 = region_b[:, :].bitcast(F16).rearrange("p (a m t) -> p a m t", a=2, m=MC)
        ktok = region_b[:, :].rearrange("p (n c) -> p n c", n=NT)
        xa16 = region_e[:, :].bitcast(F16).rearrange("p (a m t) -> p a m t", a=2, m=MC)
        sq = region_e[:, :].rearrange("p (n d) -> p n d", d=DH)
        conv = region_f[:, :].rearrange("p (m t) -> p m t", m=MC)
        xn16 = region_f[:, 0:KC * S].bitcast(F16).rearrange("p (a k t) -> p a k t", a=2, k=KC)
        kf16 = region_f[:, :].bitcast(F16).rearrange("p (a m t) -> p a m t", a=2, m=MC)
        cen = region_f[:, :].rearrange("p (n d) -> p n d", d=DH)
        cen_t = region_f[:, :].rearrange("p (n c) -> p n c", n=NT)
        xn = region_h[:, :].rearrange("p (n c) -> p n c", n=NT)
        rows_h = region_h[0:NH, :].rearrange("p (r t) -> p r t", r=2)
        dbuf = region_h[:, 0:2 * HALF].rearrange("p (r t) -> p r t", r=2)
        pbuf = region_h[:, 2 * HALF:4 * HALF].rearrange("p (r t) -> p r t", r=2)
        hbuf = region_h[:, :].rearrange("p (r t) -> p r t", r=4)
        s_wup = xa[:, :, :].rearrange("p m t -> p (m t)")[:, 0:KC * 2 * INNER].rearrange("p (k n) -> p k n", k=KC)
        s_wdn = sz[:, 0, :].rearrange("p (m n) -> p m n", m=MC)
        s_blk = region_b[:, 0:4 * MC * P].rearrange("p (w m c) -> p w m c", w=4, m=MC)
        s_sel = region_f[0:GROW, 0:NH * P].rearrange("p (h t) -> p h t", h=NH)
        s_neg = region_f[:, NH * P:NH * P + 4 * P].rearrange("p (h t) -> p h t", h=4)
        s_wg = region_e[:, 0:3 * MC * 40].rearrange("p (w m c) -> p w m c", w=3, m=MC)

        w_in, blk_in, small_in = sem("m0_w_in"), sem("m0_blk_in"), sem("m0_small_in")
        fold_full, fold_hi, w_hi, w_ready = sem("m0_fold_full"), sem("m0_fold_hi"), sem("m0_w_hi"), sem("m0_w_ready")
        init_done = sem("m0_init_done")
        batch_done = sem("m0_batch_done")
        x_in = sem("m0_x_in")
        stats, rstd_ok = sem("m0_stats"), sem("m0_rstd")
        xn_ready, xt_full, xt_hi, xt_lo = sem("m0_xn"), sem("m0_xt_full"), sem("m0_xt_hi"), sem("m0_xt_lo")
        up_full, up_act, up_lo = sem("m0_up_full"), sem("m0_up_act"), sem("m0_up_lo")
        conv_init, conv_done = sem("m0_conv_init"), sem("m0_conv_done")
        xa_hi, xa_lo = sem("m0_xa_hi"), sem("m0_xa_lo")
        gates_full, gates_read = sem("m0_gates_full"), sem("m0_gates_read")
        gate_abs, gate_log, gate_args = sem("m0_gate_abs"), sem("m0_gate_log"), sem("m0_gate_args")
        mid_ready, gate_exp, parts_ready = sem("m0_mid"), sem("m0_gate_exp"), sem("m0_parts")
        v_full, v_read = sem("m0_v_full"), sem("m0_v_read")
        kf_full, kf_hi, kf_lo = sem("m0_kf_full"), sem("m0_kf_hi"), sem("m0_kf_lo")
        kt_full, kt_read = sem("m0_kt_full"), sem("m0_kt_read")
        cols_full, cols_ready = sem("m0_cols_full"), sem("m0_cols")
        s_full, d_full, d_ready, p_ready = sem("m0_s_full"), sem("m0_d_full"), sem("m0_d"), sem("m0_p")
        kw_ready, av_full, comb_done = sem("m0_kw"), sem("m0_av_full"), sem("m0_comb")
        st_full, st_done = sem("m0_st_full"), sem("m0_st")
        cen_ready, sq_ready = sem("m0_cen"), sem("m0_sq")
        skx_ready, hn_ready = sem("m0_skx"), sem("m0_hn")
        ht_full, h32_ready, h_hi, h_lo = sem("m0_ht_full"), sem("m0_h32"), sem("m0_h_hi"), sem("m0_h_lo")
        dn_full = sem("m0_dn_full")
        u_stats, u_rstd, u_ready, us_full = sem("m0_u_stats"), sem("m0_u_rstd"), sem("m0_u"), sem("m0_us_full")

        NQ = 2 * NT
        NS = NQ - 2

        def unit_cols(q):
            return q // 2, q % 2

        block = stage.enter_context(nc.Block())

        @block.sync
        def _(sp):
            sp.dma_start(s_blk, A["blocks"]).then_inc(blk_in, 16)
            sp.dma_start(s_wg, A["w_gates"]).then_inc(blk_in, 16)
            sp.dma_start(s_wup, A["w_up"].rearrange("(k p) n -> p k n", p=P)).then_inc(w_in, 16)
            sp.dma_start(s_wdn, A["w_down"].rearrange("(m p) n -> p m n", p=P)).then_inc(w_in, 16)
            sp.dma_start(pc[:, :, :], A["chan"]).then_inc(small_in, 16)
            sp.dma_start(gb[:, :], A["gate_bias"]).then_inc(small_in, 16)
            sp.dma_start(s_sel, A["sel"]).then_inc(small_in, 16)
            sp.dma_start(pair_sel[:, :, :], A["pair_sel"]).then_inc(small_in, 16)
            sp.dma_start(s_neg, A["negmask"]).then_inc(small_in, 16)
            for b in range(B):
                sp.dma_start(X[:, b * NT:(b + 1) * NT, :],
                             A["x"][b * S:(b + 1) * S, :].rearrange("(n p) c -> p n c", p=P)).then_inc(x_in, 16)
                sp.wait_ge(x_in, b * 16 + 16)

        @block.tensor
        def _(pe):
            pe.wait_ge(blk_in, 32)
            for m in range(MC):
                pe.matmul(ps[0][:, m * P:(m + 1) * P], s_blk[:, 1, m, :], s_blk[:, 0, m, :], start=True, stop=True)
            for m in range(MC):
                o = ps[1][:, m * 40:(m + 1) * 40]
                pe.matmul(o, s_blk[:, 0, m, :], s_wg[:, 0, m, :], start=True, stop=False)
                pe.matmul(o, s_blk[:, 1, m, :], s_wg[:, 1, m, :], start=False, stop=True)
            for m in range(MC):
                last = pe.matmul(ps[2][:, m * 40:(m + 1) * 40], s_blk[:, 2, m, :], s_wg[:, 2, m, :],
                                 start=True, stop=True)
            last.then_inc(fold_full, 1)
            pe.wait_ge(w_ready, 1)
            pe.wait_ge(small_in, 80)
            pe.drain().then_inc(batch_done, 1)
            with pe.Fori(0, B) as b:
                pe.wait_ge(batch_done, b * 4 + 4)
                for g in range(4):
                    half, k = g // 2, g % 2
                    pe.wait_ge(xn_ready, b * NT + 4 * half + 4)
                    for j in range(4):
                        t = pe.transpose(ps[g][:, j * P:(j + 1) * P], xn[:, 4 * half + j, k * P:(k + 1) * P],
                                         K["ident"])
                    t.then_inc(xt_full, 1)
                for u in range(16):
                    half, m = u // 8, u % 8
                    if m in (0, 4):
                        pe.wait_ge(xt_lo, b * 4 + (2 * half + 2 if u < 4 else 4))
                    if u >= 8:
                        pe.wait_ge(up_act, b * 16 + u - 7)
                        if m < 4:
                            pe.wait_ge(up_lo, b * 8 + m + 1)
                    for k in range(KC):
                        t = product3(pe, ps[(4 + u) % 8][:, :],
                                     [wup[:, a, k, m * P:(m + 1) * P] for a in (0, 1)],
                                     [xn16[:, a, k, half * HALF:(half + 1) * HALF] for a in (0, 1)],
                                     k == 0, k == KC - 1)
                    t.then_inc(up_full, 1)
                pe.wait_ge(up_act, b * 16 + 16)
                pe.wait_ge(up_lo, b * 8 + 8)
                pe.wait_ge(xa_lo, b * MC + MC)
                r = 0
                for half in range(2):
                    t0 = slice(half * HALF, (half + 1) * HALF)
                    for m in range(MC):
                        product3(pe, ps[r][0:40, :], [ga[:, a, m, :] for a in (0, 1)],
                                 [xa16[:, a, m, t0] for a in (0, 1)], m == 0, False)
                        t = product3(pe, ps[r][0:40, :], [gv[:, a, m, :] for a in (0, 1)],
                                     [b16[:, a, m, t0] for a in (0, 1)], False, m == MC - 1)
                    t.then_inc(gates_full, 1)
                    r += 1
                for n in range(NT):
                    if r >= 8:
                        pe.wait_ge(gates_read, b * 2 + r - 7)
                    for m in range(MC):
                        t = product3(pe, ps[r % 8][:, m * P:(m + 1) * P],
                                     [b16[:, a, m, n * P:(n + 1) * P] for a in (0, 1)],
                                     [wv[:, a, m, :] for a in (0, 1)], True, True)
                    t.then_inc(v_full, 1)
                    r += 1
                for j in range(8):
                    m, half = j // 2, j % 2
                    pe.wait_ge(v_read, b * NT + j + 1)
                    t = product3(pe, ps[r % 8][:, :], [gk[:, a, m, :] for a in (0, 1)],
                                 [xa16[:, a, m, half * HALF:(half + 1) * HALF] for a in (0, 1)], True, True)
                    t.then_inc(kf_full, 1)
                    r += 1
                for n in range(NT):
                    pe.wait_ge(kf_lo, b * 8 + n + 1)
                    for m in range(MC):
                        t = product3(pe, ps[r % 8][:, m * P:(m + 1) * P],
                                     [xa16[:, a, m, n * P:(n + 1) * P] for a in (0, 1)],
                                     [gk[:, a, m, :] for a in (0, 1)], True, True)
                    t.then_inc(kt_full, 1)
                    r += 1
                pe.wait_ge(kt_read, b * NT + NT)
                pe.wait_ge(gate_exp, b * 4 + 4)
                for g in range(2):
                    for j in range(4):
                        n = 4 * g + j
                        t = pe.transpose(ps[2 + g][:, j * P:j * P + GROW], stack[0:GROW, n * P:(n + 1) * P],
                                         K["ident"][0:GROW, 0:GROW])
                    t.then_inc(cols_full, 1)
                for m in range(MC):
                    t = pe.matmul(ps[4][:, m * NT:(m + 1) * NT], pair_sel[:, m, :], dec_row[:, :],
                                  start=True, stop=True)
                t.then_inc(cols_full, 1)
                pe.wait_ge(parts_ready, b * 4 + 4)
                pe.wait_ge(cols_ready, b * 3 + 3)

                def scores(q):
                    c, hf = unit_cols(q)
                    t0 = slice(c * P, (c + 1) * P)
                    if q >= 2:
                        pe.wait_ge(p_ready, b * NQ + q - 1)
                    for pr in range(2):
                        for par in range(2):
                            rows = slice(64 * par, 64 * par + 64)
                            m = 2 * hf + pr
                            t = product3(pe, ps[2 * (q % 2) + par][:, pr * P:(pr + 1) * P],
                                         [kf16[rows, a, m, t0] for a in (0, 1)],
                                         [xa16[rows, a, m, t0] for a in (0, 1)], True, True)
                    t.then_inc(s_full, 1)

                def log_weights(q):
                    c, hf = unit_cols(q)
                    t0 = slice(c * P, (c + 1) * P)
                    if q >= 1:
                        pe.wait_ge(d_ready, b * NQ + q)
                    pe.matmul(ps[4][:, :], ident16[:, :], negmask[:, :, :].rearrange("p h t -> p (h t)"),
                              start=True, stop=False)
                    pe.matmul(ps[4][:, :], part_a[:, t0],
                              sel[:, 4 * hf:4 * hf + 4, :].rearrange("p h t -> p (h t)"), start=False, stop=False)
                    for s in range(4):
                        t = pe.matmul(ps[4][:, s * P:(s + 1) * P], sel[:, 4 * hf + s, :], part_n[:, t0],
                                      start=False, stop=(s == 3))
                    t.then_inc(d_full, 1)

                scores(0)
                log_weights(0)
                for q in range(NQ):
                    c, hf = unit_cols(q)
                    t0 = slice(c * P, (c + 1) * P)
                    if q + 1 < NQ:
                        scores(q + 1)
                        log_weights(q + 1)
                    pe.wait_ge(p_ready, b * NQ + q + 1)
                    if q >= 1:
                        pe.wait_ge(comb_done, b * NQ + q)
                    for s in range(4):
                        h = slot_head(4 * hf + s)
                        t = pe.matmul(ps[5][:, (h % 4) * VW:(h % 4 + 1) * VW], pbuf[:, q % 2, s * P:(s + 1) * P],
                                      vext[:, c, h * VW:(h + 1) * VW], start=True, stop=True)
                    if c > 0:
                        pe.wait_ge(st_done, b * NS + q - 1)
                        for pr in range(2):
                            t = pe.matmul(ps[6][:, pr * 2 * VW:(pr + 1) * 2 * VW], xa[:, 2 * hf + pr, t0],
                                          state[:, 2 * hf + pr, :], start=True, stop=True)
                    t.then_inc(av_full, 1)
                    if c < NT - 1:
                        pe.wait_ge(kw_ready, b * NS + q + 1)
                        if q >= 1:
                            pe.wait_ge(st_done, b * NS + q)
                        for pr in range(2):
                            m = 2 * hf + pr
                            t = pe.matmul(ps[7][:, pr * 2 * VW:(pr + 1) * 2 * VW], kt[:, q % 2, pr * P:(pr + 1) * P],
                                          vext[:, c, m * 2 * VW:(m + 1) * 2 * VW], start=True, stop=True)
                        t.then_inc(st_full, 1)
                pe.wait_ge(hn_ready, b + 1)
                for g in range(8):
                    half, m = g // 4, g % 4
                    for j in range(4):
                        t = pe.transpose(ps[g][:, j * P:(j + 1) * P], cen_t[:, 4 * half + j, m * P:(m + 1) * P],
                                         K["ident"])
                    t.then_inc(ht_full, 1)
                for n in range(NT):
                    if n % 4 == 0:
                        pe.wait_ge(h_lo, b * 8 + n + 4)
                    for m in range(MC):
                        t = product3(pe, ps[n][:, 0:C], [b16[:, a, m, n * P:(n + 1) * P] for a in (0, 1)],
                                     [wdn[:, a, m, :] for a in (0, 1)], m == 0, m == MC - 1)
                    t.then_inc(dn_full, 1)
                pe.wait_ge(u_ready, b + 1)
                for k in range(KC):
                    for n in range(NT):
                        t = pe.matmul(ps[0][:, k:k + 1], xn[:, n, k * P:(k + 1) * P], K["ones"],
                                      start=(n == 0), stop=(n == NT - 1))
                t.then_inc(us_full, 1)
                pe.drain().then_inc(batch_done, 1)

        @block.scalar
        def _(act):
            act.wait_ge(w_in, 32)
            act.activation(wup[:, 0, :, :], s_wup, ACT.Identity)
            act.activation(wdn[:, 0, :, :], s_wdn, ACT.Identity)
            act.wait_ge(blk_in, 32)
            act.activation(wv[:, 0, :, :], s_blk[:, 3, :, :], ACT.Identity).then_inc(w_hi, 1)
            act.wait_ge(fold_full, 1)
            act.activation(gk[:, 0, :, :].rearrange("p m c -> p (m c)"), ps[0][:, :], ACT.Identity, scale=DH ** -0.5)
            act.activation(ga[:, 0, :, :].rearrange("p m c -> p (m c)"), ps[1][:, 0:MC * 40], ACT.Identity)
            act.activation(gv[:, 0, :, :].rearrange("p m c -> p (m c)"), ps[2][:, 0:MC * 40],
                           ACT.Identity).then_inc(fold_hi, 1)
            act.wait_ge(small_in, 80)
            act.activation(sel[:, :, :], s_sel, ACT.Identity)
            act.activation(negmask[:, :, :], s_neg, ACT.Identity)
            act.activation(ident16[:, :], K["ident"], ACT.Identity)
            act.wait_ge(init_done, 1)
            act.drain().then_inc(batch_done, 1)
            with act.Fori(0, B) as b:
                act.wait_ge(batch_done, b * 4 + 4)
                for g in range(4):
                    half, k = g // 2, g % 2
                    act.wait_ge(xt_full, b * 4 + g + 1)
                    act.activation(xn16[:, 0, k, half * HALF:(half + 1) * HALF], ps[g][:, :],
                                   ACT.Identity).then_inc(xt_hi, 1)
                for u in range(16):
                    half, m = u // 8, u % 8
                    src = ps[(4 + u) % 8][:, :]
                    act.wait_ge(up_full, b * 16 + u + 1)
                    if m < 4:
                        act.activation(xm32[:, m, TAPS - 1 + half * HALF:TAPS - 1 + (half + 1) * HALF], src,
                                       ACT.Identity)
                        act.activation(b16[:, 0, m, half * HALF:(half + 1) * HALF], src,
                                       ACT.Identity).then_inc(up_act, 1)
                    else:
                        act.activation(sz[:, m - 4, half * HALF:(half + 1) * HALF], src,
                                       ACT.Silu).then_inc(up_act, 1)
                act.drain()
                for m in range(MC):
                    act.activation(conv[:, m, :], xm32[:, m, TAPS - 1:TAPS - 1 + S], ACT.Identity,
                                   bias=pc[:, m, PC_CB:PC_CB + 1],
                                   scale=pc[:, m, TAPS - 1:TAPS]).then_inc(conv_init, 1)
                for m in range(MC):
                    act.wait_ge(conv_done, b * MC + m + 1)
                    act.activation(xa16[:, 0, m, :], conv[:, m, :], ACT.Silu)
                    act.activation(xa[:, m, :], conv[:, m, :], ACT.Silu).then_inc(xa_hi, 1)
                act.wait_ge(gate_abs, b + 1)
                act.activation(rows_a[:, 1, :], rows_a[:, 1, :], ACT.Exp)
                act.drain()
                act.activation(rows_a[:, 1, :], rows_a[:, 1, :], ACT.Ln,
                               bias=K["ones"][0:NH, :]).then_inc(gate_log, 1)
                for n in range(NT):
                    act.wait_ge(v_full, b * NT + n + 1)
                    act.activation(vext[:, n, :].rearrange("p (h v) -> p h v", v=VW)[:, :, 0:DH],
                                   ps[(2 + n) % 8][:, :].rearrange("p (h v) -> p h v", v=DH),
                                   ACT.Identity).then_inc(v_read, 1)
                for j in range(8):
                    m, half = j // 2, j % 2
                    act.wait_ge(kf_full, b * 8 + j + 1)
                    act.activation(kf16[:, 0, m, half * HALF:(half + 1) * HALF], ps[(10 + j) % 8][:, :],
                                   ACT.Identity).then_inc(kf_hi, 1)
                for n in range(NT):
                    act.wait_ge(kt_full, b * NT + n + 1)
                    act.activation(ktok[:, n, :], ps[(18 + n) % 8][:, :], ACT.Identity).then_inc(kt_read, 1)
                act.wait_ge(mid_ready, b * 2 + 2)
                act.activation(part_n[32:32 + NH, :], mid16[:, 0, :], ACT.Identity).then_inc(parts_ready, 1)
                act.activation(part_a[32:32 + NH, :], mid16[:, 1, :], ACT.Identity).then_inc(parts_ready, 1)
                act.wait_ge(gate_args, b + 1)
                act.activation(stack[0:NH, :], rows_h[:, 0, :], ACT.Exp).then_inc(gate_exp, 1)
                act.activation(stack[32:32 + NH, :], rows_h[:, 1, :], ACT.Exp).then_inc(gate_exp, 1)
                act.activation(stack[64:64 + NH, :], rows_a[:, 1, :], ACT.Exp).then_inc(gate_exp, 1)
                act.activation(dec_row[:, :], dec_row[:, :], ACT.Exp).then_inc(gate_exp, 1)
                for q in range(NQ):
                    act.wait_ge(d_full, b * NQ + q + 1)
                    if q >= 2:
                        act.wait_ge(p_ready, b * NQ + q - 1)
                    else:
                        act.wait_ge(cols_ready, b * 3 + 3)
                    act.activation(dbuf[:, q % 2, :], ps[4][:, :], ACT.Exp).then_inc(d_ready, 1)
                act.wait_ge(av_full, b * NQ + NQ)
                for m in range(MC):
                    t = act.activation(xa[:, m, :], xa[:, m, :], ACT.Identity, scale=pc[:, m, PC_SKIP:PC_SKIP + 1])
                t.then_inc(skx_ready, 1)
                act.wait_ge(cen_ready, b + 1)
                act.activation(sq, cen, ACT.Square).then_inc(sq_ready, 1)
                for g in range(8):
                    half, m = g // 4, g % 4
                    act.wait_ge(h32_ready, b * 8 + g + 1)
                    act.activation(b16[:, 0, m, half * HALF:(half + 1) * HALF], hbuf[:, g % 4, :],
                                   ACT.Identity).then_inc(h_hi, 1)
                act.drain().then_inc(batch_done, 1)

        @block.gpsimd
        def _(pool):
            pool.memset(stack[:, :], 0.0)
            pool.memset(part_a[:, :], 0.0)
            pool.memset(part_n[:, :], 0.0)
            pool.memset(state[:, :, :], 0.0)
            pool.memset(vext[:, :, :], 1.0)
            pool.drain().then_inc(init_done, 1)
            pool.wait_ge(small_in, 80)
            pool.drain().then_inc(batch_done, 1)
            with pool.Fori(0, B) as b:
                pool.wait_ge(batch_done, b * 4 + 4)
                pool.wait_ge(stats, b + 1)
                pool.tensor_tensor(rstd[:, :], lnv[:, :], K["neg_half"], ALU.pow).then_inc(rstd_ok, 1)
                pool.wait_ge(kt_read, b * NT + NT)
                pool.wait_ge(cols_ready, b * 3 + 3)
                for q in range(NS):
                    c, hf = unit_cols(q)
                    if q >= 2:
                        pool.wait_ge(st_full, b * NS + q - 1)
                    pool.tensor_tensor(kt[:, q % 2, :].rearrange("p (h d) -> p h d", h=4),
                                       ktok[:, c, hf * 4 * DH:(hf + 1) * 4 * DH].rearrange("p (h d) -> p h d", h=4),
                                       cols[:, c, 64 + 4 * hf:68 + 4 * hf].unsqueeze(2).broadcast_to([P, 4, DH]),
                                       ALU.mult).then_inc(kw_ready, 1)
                pool.wait_ge(u_stats, b + 1)
                pool.tensor_tensor(rstd[:, :], lnv[:, :], K["neg_half"], ALU.pow).then_inc(u_rstd, 1)
                pool.drain().then_inc(batch_done, 1)

        @block.vector
        def _(dve):
            dve.wait_ge(w_hi, 1)
            dve.tensor_tensor(wup[:, 1, :, :], s_wup, wup[:, 0, :, :], ALU.subtract)
            dve.tensor_tensor(wdn[:, 1, :, :], s_wdn, wdn[:, 0, :, :], ALU.subtract)
            dve.tensor_tensor(wv[:, 1, :, :], s_blk[:, 3, :, :], wv[:, 0, :, :], ALU.subtract)
            dve.wait_ge(fold_hi, 1)
            dve.scalar_tensor_tensor(out=gk[:, 1, :, :].rearrange("p m c -> p (m c)"), in0=ps[0][:, :],
                                     scalar=DH ** -0.5, in1=gk[:, 0, :, :].rearrange("p m c -> p (m c)"),
                                     op0=ALU.mult, op1=ALU.subtract)
            dve.tensor_tensor(ga[:, 1, :, :].rearrange("p m c -> p (m c)"), ps[1][:, 0:MC * 40],
                              ga[:, 0, :, :].rearrange("p m c -> p (m c)"), ALU.subtract)
            dve.tensor_tensor(gv[:, 1, :, :].rearrange("p m c -> p (m c)"), ps[2][:, 0:MC * 40],
                              gv[:, 0, :, :].rearrange("p m c -> p (m c)"), ALU.subtract).then_inc(w_ready, 1)
            dve.wait_ge(small_in, 80)
            dve.drain().then_inc(batch_done, 1)

            def moments(b, eps, out_sem):
                for n in range(NT):
                    dve.bn_stats(st6[:, n, :], row(X, b * NT + n))
                dve.drain()
                for n in range(NT):
                    dve.bn_aggr(mv[:, n, :], st6[:, n, :])
                dve.drain()
                dve.tensor_scalar(lnv[:, :], mv[:, :, 1], eps, None, ALU.add).then_inc(out_sem, 1)

            def normalise(b, n):
                return dve.tensor_scalar(xn[:, n, :], row(X, b * NT + n), mv[:, n, 0:1], rstd[:, n:n + 1],
                                         ALU.subtract, ALU.mult)

            with dve.Fori(0, B) as b:
                dve.wait_ge(batch_done, b * 4 + 4)
                dve.wait_ge(x_in, b * 16 + 16)
                moments(b, 1e-6, stats)
                dve.wait_ge(rstd_ok, b + 1)
                for n in range(NT):
                    normalise(b, n).then_inc(xn_ready, 1)
                for g in range(4):
                    half, k = g // 2, g % 2
                    t0 = slice(half * HALF, (half + 1) * HALF)
                    dve.wait_ge(xt_hi, b * 4 + g + 1)
                    dve.tensor_tensor(xn16[:, 1, k, t0], ps[g][:, :], xn16[:, 0, k, t0],
                                      ALU.subtract).then_inc(xt_lo, 1)
                for m in range(MC):
                    dve.memset(xm32[:, m, 0:TAPS - 1], 0.0)
                for u in range(16):
                    half, m = u // 8, u % 8
                    if m >= 4:
                        continue
                    t0 = slice(half * HALF, (half + 1) * HALF)
                    dve.wait_ge(up_act, b * 16 + u + 1)
                    dve.tensor_tensor(b16[:, 1, m, t0], ps[(4 + u) % 8][:, :], b16[:, 0, m, t0],
                                      ALU.subtract).then_inc(up_lo, 1)
                for j in range(TAPS - 1):
                    dve.drain()
                    for m in range(MC):
                        if j == 0:
                            dve.wait_ge(conv_init, b * MC + m + 1)
                        t = dve.scalar_tensor_tensor(out=conv[:, m, :], in0=xm32[:, m, j:j + S],
                                                     scalar=pc[:, m, j:j + 1], in1=conv[:, m, :],
                                                     op0=ALU.mult, op1=ALU.add)
                        if j == TAPS - 2:
                            t.then_inc(conv_done, 1)
                for m in range(MC):
                    dve.wait_ge(xa_hi, b * MC + m + 1)
                    dve.tensor_tensor(xa16[:, 1, m, :], xa[:, m, :], xa16[:, 0, m, :],
                                      ALU.subtract).then_inc(xa_lo, 1)
                F, L, CUM, I = (rows_a[:, r, :] for r in range(4))
                for half in range(2):
                    t0 = slice(half * HALF, (half + 1) * HALF)
                    dve.wait_ge(gates_full, b * 2 + half + 1)
                    dve.tensor_scalar(F[:, t0], ps[half][32:32 + NH, :], gb[32:32 + NH, :], None, ALU.add)
                    dve.tensor_scalar(I[:, t0], ps[half][0:NH, :], gb[0:NH, :], None,
                                      ALU.add).then_inc(gates_read, 1)
                dve.drain()
                dve.scalar_tensor_tensor(out=L, in0=F, scalar=-1.0, in1=F, op0=ALU.mult,
                                         op1=ALU.min).then_inc(gate_abs, 1)
                for j in range(8):
                    m, half = j // 2, j % 2
                    t0 = slice(half * HALF, (half + 1) * HALF)
                    if j == 2:
                        dve.wait_ge(gate_log, b + 1)
                        dve.scalar_tensor_tensor(out=F, in0=F, scalar=0.0, in1=L, op0=ALU.min, op1=ALU.subtract)
                        dve.drain()
                        dve.tensor_tensor_scan(CUM, F, F, 0.0, ALU.add, ALU.bypass)
                        dve.drain()
                        dve.tensor_tensor(I, I, CUM, ALU.subtract)
                        dve.drain()
                        dve.tensor_tensor_scan(F, I, I, -3.0e38, ALU.max, ALU.bypass)
                        dve.drain()
                    dve.wait_ge(kf_hi, b * 8 + j + 1)
                    dve.tensor_tensor(kf16[:, 1, m, t0], ps[(10 + j) % 8][:, :], kf16[:, 0, m, t0],
                                      ALU.subtract).then_inc(kf_lo, 1)
                for i, (src, sign, part) in enumerate(((F, -1.0, part_n), (I, 1.0, part_a))):
                    dve.tensor_scalar(part[0:NH, :], src, sign, None, ALU.mult)
                    dve.drain()
                    dve.scalar_tensor_tensor(out=L, in0=src, scalar=sign, in1=part[0:NH, :], op0=ALU.mult,
                                             op1=ALU.subtract)
                    dve.drain()
                    dve.tensor_copy(mid16[:, i, :], L).then_inc(mid_ready, 1)
                    dve.drain()
                    dve.tensor_tensor(part[64:64 + NH, :], L, mid16[:, i, :], ALU.subtract).then_inc(parts_ready, 1)
                Fc = F.rearrange("p (n t) -> p n t", n=NT)
                Ic = I.rearrange("p (n t) -> p n t", n=NT)
                Lc = L.rearrange("p (n t) -> p n t", n=NT)
                ends = Fc[:, :, P - 1:P]
                dve.scalar_tensor_tensor(out=rows_h[:, 0, :], in0=CUM, scalar=-1.0, in1=F, op0=ALU.mult,
                                         op1=ALU.subtract)
                Dc = rows_h[:, 1, :].rearrange("p (n t) -> p n t", n=NT)
                dve.memset(Dc[:, 0, :], 0.0)
                dve.tensor_tensor(Dc[:, 1:NT, :], ends[:, 0:NT - 1, :].broadcast_to([NH, NT - 1, P]), Fc[:, 1:NT, :],
                                  ALU.subtract)
                dve.drain()
                dve.tensor_tensor(Lc, Ic, ends.broadcast_to([NH, NT, P]), ALU.subtract)
                dve.memset(dec_row[:, 0:1], 0.0)
                dve.tensor_tensor(dec_row[:, 1:NT], Fc[:, 0:NT - 1, P - 1], Fc[:, 1:NT, P - 1],
                                  ALU.subtract)
                dve.drain().then_inc(gate_args, 1)
                for g in range(2):
                    dve.wait_ge(cols_full, b * 3 + g + 1)
                    dve.tensor_copy(cols[:, 4 * g:4 * g + 4, :],
                                    ps[2 + g][:, :].rearrange("p (n r) -> p n r", n=4)[:, :, 0:GROW]
                                    ).then_inc(cols_ready, 1)
                dve.wait_ge(cols_full, b * 3 + 3)
                dve.tensor_copy(dec[:, :, :].rearrange("p m n -> p (m n)"), ps[4][:, 0:MC * NT]
                                ).then_inc(cols_ready, 1)

                def weigh(q):
                    dve.wait_ge(s_full, b * NQ + q + 1)
                    dve.wait_ge(d_ready, b * NQ + q + 1)
                    if q >= 2:
                        dve.wait_ge(av_full, b * NQ + q - 1)
                    for par in range(2):
                        t1 = slice(par * 2 * P, (par + 1) * 2 * P)
                        t = dve.tensor_tensor(pbuf[:, q % 2, t1], ps[2 * (q % 2) + par][:, 0:2 * P],
                                              dbuf[:, q % 2, t1], ALU.mult)
                    t.then_inc(p_ready, 1)

                weigh(0)
                for q in range(NQ):
                    c, hf = unit_cols(q)
                    if q + 1 < NQ:
                        weigh(q + 1)
                    dst = num[:, c, hf * 4 * VW:(hf + 1) * 4 * VW]
                    dve.wait_ge(av_full, b * NQ + q + 1)
                    if c == 0:
                        dve.tensor_copy(dst, ps[5][:, 0:4 * VW]).then_inc(comb_done, 1)
                    else:
                        dve.tensor_tensor(tmp[:, :].rearrange("p (h v) -> p h v", h=4),
                                          ps[6][:, 0:4 * VW].rearrange("p (h v) -> p h v", h=4),
                                          cols[:, c, 32 + 4 * hf:36 + 4 * hf].unsqueeze(2).broadcast_to([P, 4, VW]),
                                          ALU.mult)
                        dve.drain()
                        dve.tensor_tensor(dst, tmp[:, :], ps[5][:, 0:4 * VW], ALU.add).then_inc(comb_done, 1)
                    if c < NT - 1:
                        dve.wait_ge(st_full, b * NS + q + 1)
                        for pr in range(2):
                            m = 2 * hf + pr
                            for par in range(2):
                                rows = slice(64 * par, 64 * par + 64)
                                own = state[rows, m, par * VW:(par + 1) * VW]
                                new = ps[7][rows, (2 * pr + par) * VW:(2 * pr + par + 1) * VW]
                                if c == 0:
                                    t = dve.tensor_copy(own, new)
                                else:
                                    t = dve.scalar_tensor_tensor(out=own, in0=own, scalar=dec[rows, m, c:c + 1],
                                                                 in1=new, op0=ALU.mult, op1=ALU.add)
                        t.then_inc(st_done, 1)
                dve.drain()
                den = num4[:, :, DH]
                v0, v1, v2, v3, v4, v5, v6, v7 = (sm[:, i, :] for i in range(8))
                dve.scalar_tensor_tensor(out=v0, in0=den, scalar=-1.0, in1=den, op0=ALU.mult, op1=ALU.max)
                dve.tensor_reduce(v1, num4[:, :, 0:DH], AX_X, ALU.add)
                dve.drain()
                dve.tensor_tensor(v2.rearrange("p (n h) -> p n h", n=NT), v0.rearrange("p (n h) -> p n h", n=NT),
                                  cols[:, :, 0:NH], ALU.max)
                dve.tensor_scalar(v1, v1, 1.0 / DH, None, ALU.mult)
                dve.drain()
                dve.tensor_tensor(cen, num4[:, :, 0:DH], v1.unsqueeze(2).broadcast_to([P, NT * NH, DH]),
                                  ALU.subtract).then_inc(cen_ready, 1)
                dve.tensor_scalar(v2, v2, 1e-6, None, ALU.add)
                dve.drain()
                dve.reciprocal(v3, v2)
                dve.drain()
                dve.wait_ge(sq_ready, b + 1)
                dve.tensor_reduce(v4, sq, AX_X, ALU.add)
                dve.drain()
                dve.scalar_tensor_tensor(out=v4, in0=v4, scalar=1.0 / DH, in1=v3, op0=ALU.mult, op1=ALU.mult)
                dve.drain()
                dve.tensor_tensor(v4, v4, v3, ALU.mult)
                dve.drain()
                dve.tensor_scalar(v4, v4, 1e-5, None, ALU.add)
                dve.drain()
                inverse_root(dve, v6, v4, v5)
                dve.tensor_tensor(v7, v6, v3, ALU.mult)
                dve.drain()
                dve.tensor_tensor(cen, cen, v7.unsqueeze(2).broadcast_to([P, NT * NH, DH]),
                                  ALU.mult).then_inc(hn_ready, 1)
                dve.wait_ge(skx_ready, b + 1)

                def low_part(g):
                    half, m = g // 4, g % 4
                    t0 = slice(half * HALF, (half + 1) * HALF)
                    dve.wait_ge(h_hi, b * 8 + g + 1)
                    dve.tensor_tensor(b16[:, 1, m, t0], hbuf[:, g % 4, :], b16[:, 0, m, t0],
                                      ALU.subtract).then_inc(h_lo, 1)

                for g in range(8):
                    half, m = g // 4, g % 4
                    t0 = slice(half * HALF, (half + 1) * HALF)
                    dve.wait_ge(ht_full, b * 8 + g + 1)
                    dve.scalar_tensor_tensor(out=hbuf[:, g % 4, :], in0=ps[g][:, :],
                                             scalar=pc[:, m, PC_NW:PC_NW + 1], in1=xa[:, m, t0],
                                             op0=ALU.mult, op1=ALU.add)
                    dve.drain()
                    dve.tensor_tensor(hbuf[:, g % 4, :], hbuf[:, g % 4, :], sz[:, m, t0],
                                      ALU.mult).then_inc(h32_ready, 1)
                    if g >= 1:
                        low_part(g - 1)
                low_part(7)
                for n in range(NT):
                    dve.wait_ge(dn_full, b * NT + n + 1)
                    dve.tensor_tensor(row(X, b * NT + n), row(X, b * NT + n), ps[n][:, 0:C], ALU.add)
                dve.drain()
                moments(b, 1e-5, u_stats)
                dve.wait_ge(u_rstd, b + 1)
                for n in range(NT):
                    t = normalise(b, n)
                t.then_inc(u_ready, 1)
                dve.wait_ge(us_full, b + 1)
                dve.tensor_copy(usum[:, :, bass.ds(b, 1)].rearrange("p k o -> p (k o)"), ps[0][:, 0:KC])
                dve.drain().then_inc(batch_done, 1)


def build(nc, A, out):
    with ExitStack() as ctx:
        def sb(name, shape, dt=F32):
            return ctx.enter_context(nc.sbuf_tensor(name, shape, dt))

        def sem(name):
            return ctx.enter_context(nc.semaphore(name))

        X = sb("X", [P, B * NT, C])
        ident = sb("ident", [P, P])
        consts = sb("consts", [P, 17])
        usum = sb("usum", [P, KC, B])
        K = {"ident": ident[:, :], "ones": consts[:, 0:1], "neg_half": consts[:, 1:1 + NT],
             "half": consts[:, 1 + NT:1 + 2 * NT]}
        c_in = sem("c_in")
        c_set = sem("c_set")
        with nc.Block() as block:
            @block.sync
            def _(sp):
                sp.dma_start(ident[:, :], A["ident"]).then_inc(c_in, 16)
                sp.wait_ge(c_in, 16)

            @block.vector
            def _(dve):
                dve.memset(consts[:, 0:1], 1.0)
                dve.memset(consts[:, 1:1 + NT], -0.5)
                dve.memset(consts[:, 1 + NT:1 + 2 * NT], 0.5).then_inc(c_set, 1)
                dve.wait_ge(c_set, 1)
        mixer0(nc, X, K, A, usum)
        experts(nc, X, K, A, usum, 0)
        mixer1(nc, X, K, A, usum)
        experts(nc, X, K, A, usum, 1, out)


def experts(nc, X, K, A, usum, layer, out=None):
    L = f"e{layer}_"
    sems = []
    with ExitStack() as ctx, cleared(nc, sems), ExitStack() as stage:
        def sb(name, shape, dt=F32):
            return ctx.enter_context(nc.sbuf_tensor(L + name, shape, dt))

        def sem(name):
            sems.append(ctx.enter_context(nc.semaphore(name)))
            return sems[-1]

        ps = [ctx.enter_context(nc.psum_tensor(f"{L}ps{i}", [P, HALF], F32)) for i in range(8)]
        wr = sb("wr", [P, KC, NE])
        br = sb("br", [B, NE])
        ones4 = sb("ones4", [B, P])
        own = sb("own", [B, B, TOPK])
        gam, bet = sb("gam", [P, C]), sb("bet", [P, C])
        lg, rw, ex = sb("lg", [B, NE]), sb("rw", [B, NE]), sb("ex", [B, NE])
        sc = sb("sc", [B, 12])
        top, idx = sb("top", [B, NE]), sb("idx", [B, NE], U32)
        wexp = sb("wexp", [B, B, TOPK])
        idx_row = sb("idx_row", [1, B * TOPK], U32)
        wcol = sb("wcol", [P, B, TOPK])
        s1, s2 = sb("s1", [P, TOPK, KC, FF]), sb("s2", [P, TOPK, FC, C])
        sb1, sb2 = sb("sb1", [P, TOPK, FC]), sb("sb2", [P, TOPK, C])
        w1, w2 = sb("w1", [P, TOPK, 2, KC, FF], F16), sb("w2", [P, TOPK, 2, FC, C], F16)
        b1, b2 = sb("b1", [P, TOPK, FC]), sb("b2", [P, C])
        u = sb("u", [P, NT, C])
        y = sb("y", [P, NT, C])
        uf = sb("uf", [P, 2, KC, S], F16)
        g32 = sb("g32", [P, 4, HALF])
        hp = sb("hp", [P, 2, 2, TOPK * FC, HALF], F16)
        st6, mv = sb("st6", [P, NT, 6]), sb("mv", [P, NT, 2])
        lnv, rstd = sb("lnv", [P, NT]), sb("rstd", [P, NT])
        yst, ymv = sb("yst", [P, NT, 6]), sb("ymv", [P, NT, 2])
        yvar, yrstd = sb("yvar", [P, NT]), sb("yrstd", [P, NT])

        names = ("small_in lg_full sm_max sm_exp r_rw ld_full sm_max2 sm_exp2 r_top r_exp r_wexp wc_full idx_ok "
                 "idx_in w1_in w2_in w2_scaled w1_hi w2_hi w1_split w2_split wc_read u_stats u_rstd u_ready ut_full uf_hi "
                 "uf_lo h_full g_ready h_lo ub_ready y_full y_read y_stats y_rstd z_ready z_done x_out").split()
        (small_in, lg_full, sm_max, sm_exp, r_rw, ld_full, sm_max2, sm_exp2, r_top, r_exp, r_wexp, wc_full, idx_ok,
         idx_in, w1_in, w2_in, w2_scaled, w1_hi, w2_hi, w1_split, w2_split, wc_read, u_stats, u_rstd, u_ready, ut_full, uf_hi,
         uf_lo, h_full, g_ready, h_lo, ub_ready, y_full, y_read, y_stats, y_rstd, z_ready, z_done,
         x_out) = (sem(L + n) for n in names)
        NU = TOPK * FC
        N2 = 2 * NU

        block = stage.enter_context(nc.Block())

        @block.sync
        def _(sp):
            sp.dma_start(wr[:, :, :], A[L + "wr"]).then_inc(small_in, 16)
            sp.dma_start(br[:, :], A[L + "br"].broadcast_to([B, NE])).then_inc(small_in, 16)
            sp.dma_start(ones4[:, :], A["ones4"]).then_inc(small_in, 16)
            sp.dma_start(own[:, :, :], A["own"]).then_inc(small_in, 16)
            sp.dma_start(gam[:, :], A[L + "gamma"].broadcast_to([P, C])).then_inc(small_in, 16)
            sp.dma_start(bet[:, :], A[L + "beta"].broadcast_to([P, C])).then_inc(small_in, 16)
            sp.wait_ge(idx_ok, 1)
            sp.dma_start(idx_row[:, :], idx[:, 0:TOPK]).then_inc(idx_in, 16)
            sp.wait_ge(idx_in, 16)

            def experts_of(b):
                return [sp.value_load(idx_row[0:1, bass.ds(b * TOPK + s, 1)], min_val=0, max_val=NE - 1)
                        for s in range(TOPK)]

            def load_first(chosen):
                for s, e in enumerate(chosen):
                    sp.dma_start(s1[:, s, :, :], A[L + "w1"][bass.ds(e, 1), :, :].rearrange(
                        "o (k p) f -> p (o k) f", p=P)).then_inc(w1_in, 16)
                    sp.dma_start(sb1[:, s, :], A[L + "b1"][bass.ds(e, 1), :, :].rearrange(
                        "o p f -> p (o f)")).then_inc(w1_in, 16)

            def load_second(chosen):
                for s, e in enumerate(chosen):
                    sp.dma_start(s2[:, s, :, :], A[L + "w2"][bass.ds(e, 1), :, :].rearrange(
                        "o (k p) f -> p (o k) f", p=P)).then_inc(w2_in, 16)
                    sp.dma_start(sb2[:, s, :], A[L + "b2"][bass.ds(e, 1), :].broadcast_to([P, C])).then_inc(w2_in, 16)

            def store(b):
                if out is not None:
                    sp.wait_ge(z_done, b * NT + NT)
                    sp.dma_start(out[bass.ds(b * S, S), :].rearrange("(n p) c -> p n c", p=P),
                                 X[:, bass.ds(b * NT, NT), :]).then_inc(x_out, 16)

            def reload(b):
                chosen = experts_of(b + 1)
                sp.wait_ge(w1_split, b + 1)
                load_first(chosen)
                sp.wait_ge(w2_split, b + 1)
                load_second(chosen)

            chosen = experts_of(0)
            load_first(chosen)
            load_second(chosen)
            reload(0)
            with sp.Fori(1, B - 1) as b:
                reload(b)
                store(b - 1)
            store(B - 2)
            store(B - 1)
            if out is not None:
                sp.wait_ge(x_out, 16 * B)

        @block.tensor
        def _(pe):
            pe.wait_ge(small_in, 96)
            for k in range(KC):
                t = pe.matmul(ps[0][0:B, 0:NE], usum[:, k, :], wr[:, k, :], start=(k == 0), stop=(k == KC - 1))
            t.then_inc(lg_full, 1)
            pe.wait_ge(r_rw, 1)
            pe.matmul(ps[1][0:B, 0:NE], ones4[:, 0:B], rw[:, :], start=True, stop=True).then_inc(ld_full, 1)
            pe.wait_ge(r_wexp, 1)
            pe.matmul(ps[4][:, 0:B * TOPK], ones4[:, :], wexp[:, :, :].rearrange("b c s -> b (c s)"),
                      start=True, stop=True).then_inc(wc_full, 1)

            def turn(b, half):
                pe.wait_ge(u_ready, b * NT + 4 * half + 4)
                for k in range(KC):
                    g = 2 * half + k
                    for j in range(4):
                        t = pe.transpose(ps[g][:, j * P:(j + 1) * P], u[:, 4 * half + j, k * P:(k + 1) * P],
                                         K["ident"])
                    t.then_inc(ut_full, 1)

            def compute(b, first, last):
                pe.wait_ge(w1_split, b + 1)
                for half in range(2):
                    pe.wait_ge(uf_lo, b * 4 + (4 if half else 2))
                    for j in range(NU):
                        i = half * NU + j
                        s, f = j // FC, j % FC
                        if i == 2:
                            pe.wait_ge(uf_lo, b * 4 + 4)
                        if i >= 4:
                            pe.wait_ge(g_ready, b * N2 + i - 3)
                        for k in range(KC):
                            t = product3(pe, ps[i % 4][:, :], [w1[:, s, a, k, f * P:(f + 1) * P] for a in (0, 1)],
                                         [uf[:, a, k, half * HALF:(half + 1) * HALF] for a in (0, 1)],
                                         k == 0, k == KC - 1)
                        t.then_inc(h_full, 1)
                pe.wait_ge(w2_split, b + 1)
                for n in range(NT):
                    half = n // 4
                    if n % 4 == 0:
                        pe.wait_ge(h_lo, b * N2 + (half + 1) * NU)
                    if n >= 4 or not first:
                        pe.wait_ge(y_read, b * NT + n - 3)
                    for j in range(NU):
                        s, f = j // FC, j % FC
                        t = product3(pe, ps[4 + n % 4][:, 0:C],
                                     [hp[:, half, a, j, (n % 4) * P:(n % 4 + 1) * P] for a in (0, 1)],
                                     [w2[:, s, a, f, :] for a in (0, 1)], j == 0, j == NU - 1)
                    t.then_inc(y_full, 1)
                    if n == 3 and not last:
                        pe.wait_ge(g_ready, b * N2 + N2)
                        turn(b + 1, 0)
                    if n == 5 and not last:
                        turn(b + 1, 1)

            turn(0, 0)
            turn(0, 1)
            pe.wait_ge(wc_read, 1)
            compute(0, True, False)
            with pe.Fori(1, B - 1) as b:
                compute(b, False, False)
            compute(B - 1, False, True)

        @block.scalar
        def _(act):
            act.wait_ge(sm_max, 1)
            act.activation(ex[:, :], lg[:, :], ACT.Exp, bias=sc[:, 0:1], accum_out=sc[:, 1:2]).then_inc(sm_exp, 1)
            act.wait_ge(sm_max2, 1)
            act.activation(ex[:, :], lg[:, :], ACT.Exp, bias=sc[:, 3:4], accum_out=sc[:, 4:5]).then_inc(sm_exp2, 1)
            act.wait_ge(r_top, 1)
            act.activation(sc[:, 7:8], sc[:, 6:7], ACT.Exp).then_inc(r_exp, 1)

            def turn_parts(b, half):
                for k in range(KC):
                    act.wait_ge(ut_full, b * 4 + 2 * half + k + 1)
                    act.activation(uf[:, 0, k, half * HALF:(half + 1) * HALF], ps[2 * half + k][:, :],
                                   ACT.Identity).then_inc(uf_hi, 1)

            def first_weights(b):
                act.drain()
                act.wait_ge(w1_in, b * 64 + 64)
                act.activation(b1[:, :, :], sb1[:, :, :], ACT.Identity)
                for s in range(TOPK):
                    act.activation(w1[:, s, 0, :, :], s1[:, s, :, :], ACT.Identity).then_inc(w1_hi, 1)
                act.drain()

            def hidden(b, i):
                s, f = (i % NU) // FC, i % FC
                act.wait_ge(h_full, b * N2 + i + 1)
                if i >= 4:
                    act.wait_ge(h_lo, b * N2 + i - 3)
                act.activation(hp[:, i // NU, 0, i % NU, :], ps[i % 4][:, :], ACT.Gelu, bias=b1[:, s, f:f + 1])
                act.activation(g32[:, i % 4, :], ps[i % 4][:, :], ACT.Gelu,
                               bias=b1[:, s, f:f + 1]).then_inc(g_ready, 1)

            def compute(b, last):
                for i in range(N2):
                    hidden(b, i)
                    if i in (1, 3):
                        s = i // 2
                        act.wait_ge(w2_scaled, b * TOPK + s + 1)
                        act.activation(w2[:, s, 0, :, :], s2[:, s, :, :], ACT.Identity).then_inc(w2_hi, 1)
                if not last:
                    first_weights(b + 1)
                    for half in range(2):
                        turn_parts(b + 1, half)

            first_weights(0)
            for half in range(2):
                turn_parts(0, half)
            with act.Fori(0, B - 1) as b:
                compute(b, False)
            compute(B - 1, True)

        @block.gpsimd
        def _(pool):
            pool.wait_ge(small_in, 96)

            def tail(b):
                pool.wait_ge(y_stats, b + 1)
                pool.tensor_tensor(yrstd[:, :], yvar[:, :], K["neg_half"], ALU.pow).then_inc(y_rstd, 1)
                for n in range(NT):
                    pool.wait_ge(z_ready, b * NT + n + 1)
                    pool.tensor_tensor(y[:, n, :], y[:, n, :], gam[:, :], ALU.mult)
                for n in range(NT):
                    if n == 0:
                        pool.drain()
                    pool.tensor_tensor(y[:, n, :], y[:, n, :], bet[:, :], ALU.add)
                pool.drain()
                for n in range(NT):
                    pool.tensor_tensor(row(X, b * NT + n), row(X, b * NT + n), y[:, n, :], ALU.add).then_inc(z_done, 1)
                pool.drain()

            def front(b):
                pool.wait_ge(u_stats, b + 1)
                pool.tensor_tensor(rstd[:, :], lnv[:, :], K["neg_half"], ALU.pow).then_inc(u_rstd, 1)

            def with_bias(b):
                pool.wait_ge(w2_split, b + 1)
                for n in range(NT):
                    pool.tensor_tensor(y[:, n, :], u[:, n, :], b2[:, :], ALU.add).then_inc(ub_ready, 1)

            front(0)
            with_bias(0)
            front(1)
            with pool.Fori(1, B - 1) as b:
                tail(b - 1)
                with_bias(b)
                front(b + 1)
            tail(B - 2)
            with_bias(B - 1)
            tail(B - 1)

        @block.vector
        def _(dve):
            dve.wait_ge(small_in, 96)
            dve.wait_ge(lg_full, 1)
            dve.scalar_tensor_tensor(out=lg[:, :], in0=ps[0][0:B, 0:NE], scalar=1.0 / S, in1=br[:, :],
                                     op0=ALU.mult, op1=ALU.add)
            dve.drain()
            dve.tensor_reduce(sc[:, 8:9], lg[:, :], AX_X, ALU.max)
            dve.drain()
            dve.tensor_scalar(sc[:, 0:1], sc[:, 8:9], -1.0, None, ALU.mult).then_inc(sm_max, 1)
            dve.wait_ge(sm_exp, 1)
            dve.reciprocal(sc[:, 2:3], sc[:, 1:2])
            dve.drain()
            dve.tensor_scalar(rw[:, :], ex[:, :], sc[:, 2:3], None, ALU.mult).then_inc(r_rw, 1)
            dve.wait_ge(ld_full, 1)
            dve.tensor_scalar(lg[:, :], ps[1][0:B, 0:NE], float(S), None, ALU.mult)
            dve.drain()
            dve.reciprocal(lg[:, :], lg[:, :])
            dve.drain()
            dve.tensor_scalar(lg[:, :], lg[:, :], CAPACITY, 1.0, ALU.mult, ALU.min)
            dve.drain()
            dve.tensor_tensor(lg[:, :], lg[:, :], rw[:, :], ALU.mult)
            dve.drain()
            dve.tensor_reduce(sc[:, 9:10], lg[:, :], AX_X, ALU.max)
            dve.drain()
            dve.tensor_scalar(sc[:, 3:4], sc[:, 9:10], -1.0, None, ALU.mult).then_inc(sm_max2, 1)
            dve.wait_ge(sm_exp2, 1)
            dve.reciprocal(sc[:, 5:6], sc[:, 4:5])
            dve.drain()
            dve.tensor_scalar(rw[:, :], ex[:, :], sc[:, 5:6], None, ALU.mult)
            dve.drain()
            dve.max(top[:, :], rw[:, :])
            dve.drain()
            dve.max_index(idx[:, :], top[:, :], rw[:, :]).then_inc(idx_ok, 1)
            dve.tensor_tensor(sc[:, 6:7], top[:, 1:2], top[:, 0:1], ALU.subtract).then_inc(r_top, 1)
            dve.wait_ge(r_exp, 1)
            dve.tensor_scalar(sc[:, 8:9], sc[:, 7:8], 1.0, None, ALU.add)
            dve.drain()
            dve.reciprocal(sc[:, 10:11], sc[:, 8:9])
            dve.drain()
            dve.tensor_tensor(sc[:, 11:12], sc[:, 10:11], sc[:, 7:8], ALU.mult)
            dve.drain()
            dve.tensor_tensor(wexp[:, :, :], own[:, :, :],
                              sc[:, 10:12].unsqueeze(1).broadcast_to([B, B, TOPK]), ALU.mult).then_inc(r_wexp, 1)
            dve.wait_ge(wc_full, 1)
            dve.tensor_copy(wcol[:, :, :].rearrange("p b s -> p (b s)"), ps[4][:, 0:B * TOPK]).then_inc(wc_read, 1)
            dve.drain()

            def weight(b, s):
                return wcol[:, bass.ds(b, 1), s:s + 1].rearrange("p o s -> p (o s)")

            def front_stats(b):
                for n in range(NT):
                    dve.bn_stats(st6[:, n, :], row(X, b * NT + n))
                dve.drain()
                for n in range(NT):
                    dve.bn_aggr(mv[:, n, :], st6[:, n, :])
                dve.drain()
                dve.tensor_scalar(lnv[:, :], mv[:, :, 1], 1e-5, None, ALU.add).then_inc(u_stats, 1)

            def front_norm(b):
                dve.wait_ge(u_rstd, b + 1)
                for n in range(NT):
                    dve.tensor_scalar(u[:, n, :], row(X, b * NT + n), mv[:, n, 0:1], rstd[:, n:n + 1],
                                      ALU.subtract, ALU.mult).then_inc(u_ready, 1)

            def first_weights(b, s):
                dve.wait_ge(w1_hi, b * TOPK + s + 1)
                t = dve.tensor_tensor(w1[:, s, 1, :, :], s1[:, s, :, :], w1[:, s, 0, :, :], ALU.subtract)
                if s == TOPK - 1:
                    t.then_inc(w1_split, 1)

            def turn_parts(b, half):
                t0 = slice(half * HALF, (half + 1) * HALF)
                for k in range(KC):
                    dve.wait_ge(uf_hi, b * 4 + 2 * half + k + 1)
                    dve.tensor_tensor(uf[:, 1, k, t0], ps[2 * half + k][:, :], uf[:, 0, k, t0],
                                      ALU.subtract).then_inc(uf_lo, 1)

            def scale_second(b):
                dve.wait_ge(w2_in, b * 64 + 64)
                for s in range(TOPK):
                    dve.tensor_scalar(s2[:, s, :, :], s2[:, s, :, :], weight(b, s), None,
                                      ALU.mult).then_inc(w2_scaled, 1)
                dve.tensor_scalar(b2[:, :], sb2[:, 0, :], weight(b, 0), None, ALU.mult)
                dve.drain()
                dve.scalar_tensor_tensor(out=b2[:, :], in0=sb2[:, 1, :], scalar=weight(b, 1), in1=b2[:, :],
                                         op0=ALU.mult, op1=ALU.add)

            def second_weights(b, s):
                dve.wait_ge(w2_hi, b * TOPK + s + 1)
                t = dve.tensor_tensor(w2[:, s, 1, :, :], s2[:, s, :, :], w2[:, s, 0, :, :], ALU.subtract)
                if s == TOPK - 1:
                    t.then_inc(w2_split, 1)

            def low_hidden(b, i):
                half, j = i // NU, i % NU
                dve.wait_ge(g_ready, b * N2 + i + 1)
                dve.tensor_tensor(hp[:, half, 1, j, :], g32[:, i % 4, :], hp[:, half, 0, j, :],
                                  ALU.subtract).then_inc(h_lo, 1)

            def sum_rows(b, n):
                dve.wait_ge(ub_ready, b * NT + n + 1)
                dve.wait_ge(y_full, b * NT + n + 1)
                dve.tensor_tensor(y[:, n, :], y[:, n, :], ps[4 + n % 4][:, 0:C], ALU.add).then_inc(y_read, 1)
                dve.drain()
                dve.bn_stats(yst[:, n, :], y[:, n, :])

            def sum_stats(b):
                dve.drain()
                for n in range(NT):
                    dve.bn_aggr(ymv[:, n, :], yst[:, n, :])
                dve.drain()
                dve.tensor_scalar(yvar[:, :], ymv[:, :, 1], 1e-5, None, ALU.add).then_inc(y_stats, 1)

            def sum_norm(b, n):
                dve.tensor_scalar(y[:, n, :], y[:, n, :], ymv[:, n, 0:1], yrstd[:, n:n + 1],
                                  ALU.subtract, ALU.mult).then_inc(z_ready, 1)

            def compute(b, first, last):
                scale_second(b)
                for i in range(N2):
                    low_hidden(b, i)
                    if i == 0 and not first:
                        dve.wait_ge(y_rstd, b)
                        for n in range(NT):
                            sum_norm(b - 1, n)
                    if i in (3, 5):
                        second_weights(b, (i - 3) // 2)
                    if i == 12 and not last:
                        front_stats(b + 1)
                if not last:
                    dve.wait_ge(ub_ready, b * NT + NT)
                    front_norm(b + 1)
                for n in range(NT):
                    sum_rows(b, n)
                    if not last:
                        if n in (1, 2):
                            first_weights(b + 1, n - 1)
                        if n in (4, 6):
                            turn_parts(b + 1, n // 2 - 2)
                sum_stats(b)

            front_stats(0)
            front_norm(0)
            for s in range(TOPK):
                first_weights(0, s)
            for half in range(2):
                turn_parts(0, half)
            compute(0, True, False)
            with dve.Fori(1, B - 1) as b:
                compute(b, False, False)
            compute(B - 1, False, True)
            dve.wait_ge(y_rstd, B)
            for n in range(NT):
                sum_norm(B - 1, n)


def mixer1(nc, X, K, A, usum):
    sems = []
    with ExitStack() as ctx, cleared(nc, sems), ExitStack() as stage:
        def sb(name, shape, dt=F32):
            return ctx.enter_context(nc.sbuf_tensor("m1_" + name, shape, dt))

        def sem(name):
            sems.append(ctx.enter_context(nc.semaphore(name)))
            return sems[-1]

        ps = [ctx.enter_context(nc.psum_tensor(f"m1_ps{i}", [P, HALF], F32)) for i in range(4)]
        pa = [ctx.enter_context(nc.psum_tensor(f"m1_pa{i}", [P, 2 * HALF], F32)) for i in range(2)]
        wst = sb("wst", [P, 2, KC, C])
        wadj, waff = sb("wadj", [P, 2, KC, C], F16), sb("waff", [P, 2, KC, C], F16)
        aff_b, ln_g, ln_b = sb("aff_b", [P, C]), sb("ln_g", [P, C]), sb("ln_b", [P, C])
        nf = sb("nf", [P, NT, C])
        nf16 = sb("nf16", [P, 2, KC, S], F16)
        g16 = sb("g16", [P, 2, KC, S], F16)
        h32 = sb("h32", [P, 3, C])
        h16 = sb("h16", [P, 2, NT, C], F16)
        pr = sb("pr", [P, 2, S])
        pt16 = sb("pt16", [P, 2, 2, NT, P], F16)
        y = sb("y", [P, 2, C])
        st6, mv = sb("st6", [P, NT, 6]), sb("mv", [P, NT, 2])
        sm = sb("sm", [P, 8, NT])
        mx, nmx = sb("mx", [P, 2]), sb("nmx", [P, 2])
        ssum = sb("ssum", [P, 2])
        yst, ymv, ys = sb("yst", [P, 2, 6]), sb("ymv", [P, 2, 2]), sb("ys", [P, 2, 4])
        names = ("w_in w_hi w_ready batch_done x_stats x_rstd n2_ready n_scale nf_ready nt_full nf_hi nf_lo "
                 "gf_full gf_hi gf_lo hf_full h_ready h_hi h_lo a_full mx_ready p_ready pt_full pt_hi pt_lo o_full "
                 "y_stats y_rstd y_norm y_aff x_done u_stats u_rstd u_ready us_full").split()
        (w_in, w_hi, w_ready, batch_done, x_stats, x_rstd, n2_ready, n_scale, nf_ready, nt_full, nf_hi, nf_lo,
         gf_full, gf_hi, gf_lo, hf_full, h_ready, h_hi, h_lo, a_full, mx_ready, p_ready, pt_full, pt_hi, pt_lo,
         o_full, y_stats, y_rstd, y_norm, y_aff, x_done, u_stats, u_rstd, u_ready,
         us_full) = (sem("m1_" + n) for n in names)
        block = stage.enter_context(nc.Block())

        @block.sync
        def _(sp):
            sp.dma_start(wst[:, 0, :, :], A["adj"].rearrange("(k p) n -> p k n", p=P)).then_inc(w_in, 16)
            sp.dma_start(wst[:, 1, :, :], A["affine"].rearrange("(k p) n -> p k n", p=P)).then_inc(w_in, 16)
            sp.dma_start(aff_b[:, :], A["affine_b"].broadcast_to([P, C])).then_inc(w_in, 16)
            sp.dma_start(ln_g[:, :], A["ln_g"].broadcast_to([P, C])).then_inc(w_in, 16)
            sp.dma_start(ln_b[:, :], A["ln_b"].broadcast_to([P, C])).then_inc(w_in, 16)
            sp.wait_ge(w_in, 80)

        @block.tensor
        def _(pe):
            pe.wait_ge(w_ready, 1)
            pe.drain().then_inc(batch_done, 1)
            with pe.Fori(0, B) as b:
                pe.wait_ge(batch_done, b * 4 + 4)
                for g in range(4):
                    half, k = g // 2, g % 2
                    pe.wait_ge(nf_ready, b * NT + 4 * half + 4)
                    for j in range(4):
                        t = pe.transpose(ps[g][:, j * P:(j + 1) * P], nf[:, 4 * half + j, k * P:(k + 1) * P],
                                         K["ident"])
                    t.then_inc(nt_full, 1)
                for i in range(4):
                    half, d = i // 2, i % 2
                    pe.wait_ge(nf_lo, b * 4 + (2 * half + 2 if i < 2 else 4))
                    for k in range(KC):
                        t = product3(pe, ps[i][:, :], [wadj[:, a, k, d * P:(d + 1) * P] for a in (0, 1)],
                                     [nf16[:, a, k, half * HALF:(half + 1) * HALF] for a in (0, 1)],
                                     k == 0, k == KC - 1)
                    t.then_inc(gf_full, 1)
                for n in range(NT):
                    if n < 4:
                        pe.wait_ge(gf_lo, b * 4 + n + 1)
                    else:
                        pe.wait_ge(h_ready, b * NT + n - 3)
                    for k in range(KC):
                        t = product3(pe, ps[n % 4][:, 0:C], [nf16[:, a, k, n * P:(n + 1) * P] for a in (0, 1)],
                                     [waff[:, a, k, :] for a in (0, 1)], k == 0, k == KC - 1)
                    t.then_inc(hf_full, 1)

                def logits(n):
                    if n >= 2:
                        pe.wait_ge(p_ready, b * NT + n - 1)
                    for half in range(2):
                        for k in range(KC):
                            t = product3(pe, pa[n % 2][:, half * HALF:(half + 1) * HALF],
                                         [g16[:, a, k, n * P:(n + 1) * P] for a in (0, 1)],
                                         [nf16[:, a, k, half * HALF:(half + 1) * HALF] for a in (0, 1)],
                                         k == 0, k == KC - 1)
                    t.then_inc(a_full, 1)

                def turn(n):
                    pe.wait_ge(p_ready, b * NT + n + 1)
                    for g in range(2):
                        if n >= 1:
                            pe.wait_ge(pt_lo, b * 2 * NT + 2 * n + g - 1)
                        for j in range(4):
                            t = pe.transpose(ps[g][:, j * P:(j + 1) * P], pr[:, n % 2, (4 * g + j) * P:(4 * g + j + 1) * P],
                                             K["ident"])
                        t.then_inc(pt_full, 1)

                def mix(n):
                    pe.wait_ge(pt_lo, b * 2 * NT + 2 * n + 2)
                    if n == 0:
                        pe.wait_ge(h_lo, b * NT + NT)
                    if n >= 2:
                        pe.wait_ge(y_norm, b * NT + n - 1)
                    for m in range(NT):
                        t = product3(pe, ps[2 + n % 2][:, 0:C], [pt16[:, n % 2, a, m, :] for a in (0, 1)],
                                     [h16[:, a, m, :] for a in (0, 1)], m == 0, m == NT - 1)
                    t.then_inc(o_full, 1)

                pe.wait_ge(h_ready, b * NT + NT)
                logits(0)
                for n in range(NT):
                    if n + 1 < NT:
                        logits(n + 1)
                    turn(n)
                    if n >= 1:
                        mix(n - 1)
                mix(NT - 1)
                pe.wait_ge(u_ready, b + 1)
                for k in range(KC):
                    for n in range(NT):
                        t = pe.matmul(ps[0][:, k:k + 1], nf[:, n, k * P:(k + 1) * P], K["ones"],
                                      start=(n == 0), stop=(n == NT - 1))
                t.then_inc(us_full, 1)
                pe.drain().then_inc(batch_done, 1)

        @block.scalar
        def _(act):
            act.wait_ge(w_in, 80)
            act.activation(wadj[:, 0, :, :], wst[:, 0, :, :], ACT.Identity)
            act.activation(waff[:, 0, :, :], wst[:, 1, :, :], ACT.Identity).then_inc(w_hi, 1)
            act.drain().then_inc(batch_done, 1)

            with act.Fori(0, B) as b:
                act.wait_ge(batch_done, b * 4 + 4)
                for g in range(4):
                    half, k = g // 2, g % 2
                    act.wait_ge(nt_full, b * 4 + g + 1)
                    act.activation(nf16[:, 0, k, half * HALF:(half + 1) * HALF], ps[g][:, :],
                                   ACT.Identity).then_inc(nf_hi, 1)
                for i in range(4):
                    half, d = i // 2, i % 2
                    act.wait_ge(gf_full, b * 4 + i + 1)
                    act.activation(g16[:, 0, d, half * HALF:(half + 1) * HALF], ps[i][:, :],
                                   ACT.Identity).then_inc(gf_hi, 1)
                for n in range(NT):
                    act.wait_ge(h_ready, b * NT + n + 1)
                    act.activation(h16[:, 0, n, :], h32[:, n % 3, :], ACT.Identity).then_inc(h_hi, 1)
                for n in range(NT):
                    act.wait_ge(mx_ready, b * NT + n + 1)
                    if n >= 2:
                        act.wait_ge(pt_full, b * 2 * NT + 2 * n - 2)
                        act.wait_ge(y_stats, b * NT + n - 1)
                    act.activation(pr[:, n % 2, :], pa[n % 2][:, :], ACT.Exp, bias=nmx[:, n % 2:n % 2 + 1],
                                   scale=5.0, accum_out=ssum[:, n % 2:n % 2 + 1]).then_inc(p_ready, 1)
                    if n >= 2:
                        act.wait_ge(o_full, b * NT + n - 1)
                    for g in range(2):
                        act.wait_ge(pt_full, b * 2 * NT + 2 * n + g + 1)
                        act.activation(pt16[:, n % 2, 0, 4 * g:4 * g + 4, :].rearrange("p m t -> p (m t)"),
                                       ps[g][:, :], ACT.Identity).then_inc(pt_hi, 1)
                act.drain().then_inc(batch_done, 1)

        @block.gpsimd
        def _(pool):
            pool.wait_ge(w_in, 80)
            pool.drain().then_inc(batch_done, 1)
            with pool.Fori(0, B) as b:
                pool.wait_ge(batch_done, b * 4 + 4)
                pool.wait_ge(x_stats, b + 1)
                pool.tensor_tensor(sm[:, 1, :], sm[:, 0, :], K["neg_half"], ALU.pow).then_inc(x_rstd, 1)
                pool.wait_ge(n2_ready, b + 1)
                pool.tensor_tensor(sm[:, 4, :], sm[:, 2, :], K["neg_half"], ALU.pow)
                pool.tensor_tensor(sm[:, 5, :], sm[:, 2, :], K["half"], ALU.pow).then_inc(n_scale, 1)
                for n in range(NT):
                    pool.wait_ge(y_stats, b * NT + n + 1)
                    pool.tensor_tensor(ys[:, n % 2, 3:4], ys[:, n % 2, 1:2], K["neg_half"][:, 0:1],
                                       ALU.pow).then_inc(y_rstd, 1)
                    pool.wait_ge(y_norm, b * NT + n + 1)
                    pool.tensor_tensor(y[:, n % 2, :], y[:, n % 2, :], ln_g[:, :], ALU.mult)
                    pool.drain()
                    pool.tensor_tensor(y[:, n % 2, :], y[:, n % 2, :], ln_b[:, :], ALU.add).then_inc(y_aff, 1)
                pool.wait_ge(u_stats, b + 1)
                pool.tensor_tensor(sm[:, 7, :], sm[:, 0, :], K["neg_half"], ALU.pow).then_inc(u_rstd, 1)
                pool.drain().then_inc(batch_done, 1)

        @block.vector
        def _(dve):
            dve.wait_ge(w_hi, 1)
            dve.tensor_tensor(wadj[:, 1, :, :], wst[:, 0, :, :], wadj[:, 0, :, :], ALU.subtract)
            dve.tensor_tensor(waff[:, 1, :, :], wst[:, 1, :, :], waff[:, 0, :, :], ALU.subtract)
            dve.drain().then_inc(w_ready, 1)
            dve.drain().then_inc(batch_done, 1)

            def moments(b, eps, out_sem):
                for n in range(NT):
                    dve.bn_stats(st6[:, n, :], row(X, b * NT + n))
                dve.drain()
                for n in range(NT):
                    dve.bn_aggr(mv[:, n, :], st6[:, n, :])
                dve.drain()
                dve.tensor_scalar(sm[:, 0, :], mv[:, :, 1], eps, None, ALU.add).then_inc(out_sem, 1)

            def row_max(b, n):
                dve.wait_ge(a_full, b * NT + n + 1)
                if n >= 2:
                    dve.wait_ge(p_ready, b * NT + n - 1)
                dve.tensor_reduce(mx[:, n % 2:n % 2 + 1], pa[n % 2][:, :], AX_X, ALU.max)
                dve.drain()
                dve.tensor_scalar(nmx[:, n % 2:n % 2 + 1], mx[:, n % 2:n % 2 + 1], -5.0, None,
                                  ALU.mult).then_inc(mx_ready, 1)

            def low_weights(b, n):
                for g in range(2):
                    dve.wait_ge(pt_hi, b * 2 * NT + 2 * n + g + 1)
                    dve.tensor_tensor(pt16[:, n % 2, 1, 4 * g:4 * g + 4, :].rearrange("p m t -> p (m t)"), ps[g][:, :],
                                      pt16[:, n % 2, 0, 4 * g:4 * g + 4, :].rearrange("p m t -> p (m t)"),
                                      ALU.subtract).then_inc(pt_lo, 1)

            def out_stats(b, n):
                i = n % 2
                dve.wait_ge(o_full, b * NT + n + 1)
                dve.bn_stats(yst[:, i, :], ps[2 + i][:, 0:C])
                dve.tensor_scalar(ys[:, i, 0:1], ssum[:, i:i + 1], ssum[:, i:i + 1], 1e-5, ALU.mult, ALU.mult)
                dve.drain()
                dve.bn_aggr(ymv[:, i, :], yst[:, i, :])
                dve.drain()
                dve.tensor_tensor(ys[:, i, 1:2], ymv[:, i, 1:2], ys[:, i, 0:1], ALU.add).then_inc(y_stats, 1)

            def out_norm(b, n):
                i = n % 2
                dve.wait_ge(y_rstd, b * NT + n + 1)
                dve.tensor_scalar(y[:, i, :], ps[2 + i][:, 0:C], ymv[:, i, 0:1], ys[:, i, 3:4],
                                  ALU.subtract, ALU.mult).then_inc(y_norm, 1)

            def out_add(b, n):
                i = n % 2
                dve.wait_ge(y_aff, b * NT + n + 1)
                dve.scalar_tensor_tensor(out=y[:, i, :], in0=y[:, i, :], scalar=0.01, in1=y[:, i, :],
                                         op0=ALU.mult, op1=ALU.max)
                dve.drain()
                dve.tensor_tensor(row(X, b * NT + n), row(X, b * NT + n), y[:, i, :], ALU.add)

            with dve.Fori(0, B) as b:
                dve.wait_ge(batch_done, b * 4 + 4)
                moments(b, 1e-6, x_stats)
                dve.wait_ge(x_rstd, b + 1)
                dve.tensor_tensor(sm[:, 2, :], mv[:, :, 1], sm[:, 1, :], ALU.mult)
                dve.drain()
                dve.tensor_tensor(sm[:, 2, :], sm[:, 2, :], sm[:, 1, :], ALU.mult)
                dve.drain()
                dve.tensor_scalar(sm[:, 2, :], sm[:, 2, :], float(C), 1e-24, ALU.mult, ALU.max).then_inc(n2_ready, 1)
                dve.wait_ge(n_scale, b + 1)
                dve.tensor_tensor(sm[:, 4, :], sm[:, 4, :], sm[:, 1, :], ALU.mult)
                dve.drain()
                for n in range(NT):
                    dve.tensor_scalar(nf[:, n, :], row(X, b * NT + n), mv[:, n, 0:1], sm[:, 4, n:n + 1],
                                      ALU.subtract, ALU.mult).then_inc(nf_ready, 1)
                for g in range(4):
                    half, k = g // 2, g % 2
                    t0 = slice(half * HALF, (half + 1) * HALF)
                    dve.wait_ge(nf_hi, b * 4 + g + 1)
                    dve.tensor_tensor(nf16[:, 1, k, t0], ps[g][:, :], nf16[:, 0, k, t0],
                                      ALU.subtract).then_inc(nf_lo, 1)
                for i in range(4):
                    half, d = i // 2, i % 2
                    t0 = slice(half * HALF, (half + 1) * HALF)
                    dve.wait_ge(gf_hi, b * 4 + i + 1)
                    dve.tensor_tensor(g16[:, 1, d, t0], ps[i][:, :], g16[:, 0, d, t0],
                                      ALU.subtract).then_inc(gf_lo, 1)
                for n in range(NT + 1):
                    if n < NT:
                        dve.wait_ge(hf_full, b * NT + n + 1)
                        if n >= 3:
                            dve.wait_ge(h_lo, b * NT + n - 2)
                        dve.scalar_tensor_tensor(out=h32[:, n % 3, :], in0=ps[n % 4][:, 0:C], scalar=sm[:, 5, n:n + 1],
                                                 in1=aff_b[:, :], op0=ALU.mult, op1=ALU.add).then_inc(h_ready, 1)
                    if n >= 1:
                        dve.wait_ge(h_hi, b * NT + n)
                        dve.tensor_tensor(h16[:, 1, n - 1, :], h32[:, (n - 1) % 3, :], h16[:, 0, n - 1, :],
                                          ALU.subtract).then_inc(h_lo, 1)
                row_max(b, 0)
                for n in range(NT):
                    if n + 1 < NT:
                        row_max(b, n + 1)
                    low_weights(b, n)
                    if n >= 1:
                        out_stats(b, n - 1)
                        out_norm(b, n - 1)
                    if n >= 2:
                        out_add(b, n - 2)
                out_stats(b, NT - 1)
                out_add(b, NT - 2)
                out_norm(b, NT - 1)
                out_add(b, NT - 1)
                dve.drain()
                moments(b, 1e-5, u_stats)
                dve.wait_ge(u_rstd, b + 1)
                for n in range(NT):
                    t = dve.tensor_scalar(nf[:, n, :], row(X, b * NT + n), mv[:, n, 0:1], sm[:, 7, n:n + 1],
                                          ALU.subtract, ALU.mult)
                t.then_inc(u_ready, 1)
                dve.wait_ge(us_full, b + 1)
                dve.tensor_copy(usum[:, :, bass.ds(b, 1)].rearrange("p k o -> p (k o)"), ps[0][:, 0:KC])
                dve.drain().then_inc(batch_done, 1)


def block_diagonal(w):
    w = np.asarray(w)
    full = np.zeros((MC, P // 4, 4, P // 4, 4), w.dtype)
    blocks = w.reshape(MC, P // 4, 4, 4)
    for n in range(P // 4):
        full[:, n, :, n, :] = blocks[:, n]
    return full.reshape(MC, P, P).transpose(1, 0, 2)


def arrange(inputs):
    i = {k: np.asarray(v) for k, v in inputs.items()}
    f = np.float32
    c = np.ascontiguousarray
    a = {"x": i["x"].reshape(B * S, C)}
    a["w_up"] = c(i["L0_conv_W_up"].T)
    a["w_down"] = c(i["L0_conv_W_down"].T)
    wq, wk, wv = i["L0_conv_Wq"], i["L0_conv_Wk"], i["L0_conv_Wv"]
    a["blocks"] = c(np.stack([block_diagonal(w) for w in (wq, wk, wv, wv.transpose(0, 2, 1))], axis=1))
    gates = np.zeros((3 * MC, P, 40), f)
    gates[:, :, 0:NH] = i["L0_conv_W_i"].T.reshape(3 * MC, P, NH)
    gates[:, :, 32:32 + NH] = i["L0_conv_W_f"].T.reshape(3 * MC, P, NH)
    a["w_gates"] = c(gates.reshape(3, MC, P, 40).transpose(2, 0, 1, 3))
    gb = np.zeros((40, 1), f)
    gb[0:NH, 0] = i["L0_conv_b_i"]
    gb[32:32 + NH, 0] = i["L0_conv_b_f"]
    a["gate_bias"] = gb
    chan = np.concatenate([i["L0_conv_conv_w"][:, 0, :], i["L0_conv_conv_b"][:, None],
                           i["L0_conv_norm_w"][:, None], i["L0_conv_skip"][:, None]], axis=1)
    a["chan"] = c(chan.reshape(MC, P, PC_N).transpose(1, 0, 2))
    sel = np.zeros((GROW, NH, P), f)
    for slot in range(NH):
        for g in range(3):
            sel[32 * g + slot_head(slot), slot, :] = 1
    a["sel"] = sel
    pair_sel = np.zeros((NH, MC, P), f)
    for h in range(NH):
        pair_sel[h, h // 2, DH * (h % 2):DH * (h % 2) + DH] = 1
    a["pair_sel"] = pair_sel
    later = np.tril(np.ones((P, P)), -1)
    a["negmask"] = np.repeat((later * -1e30)[:, None, :], 4, axis=1).astype(f)
    a["ident"] = np.eye(P, dtype=f)
    a["ones4"] = np.ones((B, P), f)
    a["own"] = np.repeat(np.eye(B, dtype=f)[:, :, None], TOPK, axis=2)
    for layer in range(2):
        src, dst = f"L{layer}_ffn_", f"e{layer}_"
        a[dst + "wr"] = c(i[src + "Wr"].reshape(KC, P, NE).transpose(1, 0, 2))
        a[dst + "w1"], a[dst + "w2"], a[dst + "b2"] = i[src + "W1"], i[src + "W2"], i[src + "b2"]
        a[dst + "b1"] = c(i[src + "b1"].reshape(NE, FC, P).transpose(0, 2, 1))
        for name in ("br", "gamma", "beta"):
            a[dst + name] = i[src + name][None, :]
    a["adj"] = i["L1_conv_adj_w"]
    a["affine"] = c(i["L1_conv_affine_w"].T)
    for name in ("affine_b", "ln_g", "ln_b"):
        a[name] = i["L1_conv_" + name][None, :]
    return a


def kernel(**inputs):
    import concourse.bacc as bacc
    from concourse.bass_utils import run_bass_kernel_spmd as run

    nc = bacc.Bacc("TRN2", target_bir_lowering=False, num_devices=1)
    arrays, aps = {}, {}
    for name, a in arrange(inputs).items():
        arrays["in_" + name] = a
        aps[name] = nc.dram_tensor("in_" + name, a.shape, mybir.dt.from_np(a.dtype), kind="ExternalInput").ap()
    out = nc.dram_tensor("out_0", (B * S, C), F32, kind="ExternalOutput").ap()
    build(nc, aps, out)
    r = run(nc, [arrays], core_ids=[0])
    return r.results[0]["out_0"].reshape(B, S // 32, 32, C)
```

```python
from contextlib import ExitStack, contextmanager

import numpy as np

import concourse.bass as bass
from concourse import mybir

F32 = mybir.dt.float32
F16 = mybir.dt.float16
BF16 = mybir.dt.bfloat16
U32 = mybir.dt.uint32
I32 = mybir.dt.int32
ALU = mybir.AluOpType
ACT = mybir.ActivationFunctionType
AX_X = mybir.AxisListType.X

P = 128
B = 4
S = 1024
C = 256
KC = C // P
NT = S // P
HALF = S // 2
INNER = 512
MC = INNER // P
NH = 8
DH = INNER // NH
TAPS = 4
VW = DH + 1
NE = 8
TOPK = 2
FF = 512
FC = FF // P
CAPACITY = float(-(-B * S * 1.25 // NE))
GROW = 72

PC_TAP, PC_CB, PC_NW, PC_SKIP = 0, TAPS, TAPS + 1, TAPS + 2
PC_N = TAPS + 3


def slot_head(slot):
    return 4 * (slot // 4) + 2 * (slot % 2) + (slot // 2) % 2


def row(t, i):
    return t[:, bass.ds(i, 1), :].rearrange("p o f -> p (o f)")


def inverse_root(dve, out, x, t):
    dve.tensor_scalar(t.bitcast(I32), x.bitcast(I32), 1, None, ALU.arith_shift_right)
    dve.drain()
    dve.tensor_scalar(out.bitcast(I32), t.bitcast(I32), -1.0, float(0x5F3759DF), ALU.mult, ALU.add)
    dve.drain()
    for _ in range(3):
        dve.tensor_tensor(t, out, out, ALU.mult)
        dve.drain()
        dve.scalar_tensor_tensor(out=t, in0=t, scalar=-0.5, in1=x, op0=ALU.mult, op1=ALU.mult)
        dve.drain()
        dve.scalar_tensor_tensor(out=out, in0=t, scalar=1.5, in1=out, op0=ALU.add, op1=ALU.mult)
        dve.drain()


def product3(pe, out, a, b, start, stop):
    pe.matmul(out, a[0], b[0], start=start, stop=False)
    pe.matmul(out, a[0], b[1], start=False, stop=False)
    return pe.matmul(out, a[1], b[0], start=False, stop=stop)


@contextmanager
def cleared(nc, sems):
    yield
    with nc.Block() as block:
        @block.sync
        def _(sp):
            for s in sems:
                sp.sem_clear(s)


def mixer0(nc, X, K, A, usum):
    sems = []
    with ExitStack() as ctx, cleared(nc, sems), ExitStack() as stage:
        def sb(name, shape, dt=F32):
            return ctx.enter_context(nc.sbuf_tensor("m0_" + name, shape, dt))

        def sem(name):
            sems.append(ctx.enter_context(nc.semaphore(name)))
            return sems[-1]

        ps = [ctx.enter_context(nc.psum_tensor(f"m0_ps{i}", [P, HALF], F32)) for i in range(8)]

        wup = sb("wup", [P, 2, KC, 2 * INNER], F16)
        wdn = sb("wdn", [P, 2, MC, C], F16)
        gk = sb("gk", [P, 2, MC, P], F16)
        wv = sb("wv", [P, 2, MC, P], F16)
        ga = sb("ga", [P, 2, MC, 40], F16)
        gv = sb("gv", [P, 2, MC, 40], F16)
        pc = sb("pc", [P, MC, PC_N])
        gb = sb("gb", [40, 1])
        sel = sb("sel", [GROW, NH, P], BF16)
        pair_sel = sb("pair_sel", [NH, MC, P])
        negmask = sb("negmask", [P, 4, P], BF16)
        ident16 = sb("ident16", [P, P], BF16)
        region_a = sb("region_a", [P, NT * NH * VW])
        region_b = sb("region_b", [P, MC * S])
        sz = sb("sz", [P, MC, S])
        xa = sb("xa", [P, MC, S])
        region_e = sb("region_e", [P, MC * S])
        region_f = sb("region_f", [P, MC * S])
        vext = sb("vext", [P, NT, NH * VW])
        region_h = sb("region_h", [P, NT * C])
        kt = sb("kt", [P, 2, 4 * DH])
        tmp = sb("tmp", [P, 4 * VW])
        state = sb("state", [P, MC, 2 * VW])
        stack = sb("stack", [P, S])
        part_a = sb("part_a", [GROW, S], BF16)
        part_n = sb("part_n", [GROW, S], BF16)
        sq_buf = sb("sq_buf", [P, S])
        cols = sb("cols", [P, NT, GROW])
        dec_row = sb("dec_row", [NH, NT])
        dec = sb("dec", [P, MC, NT])
        st6 = sb("st6", [P, NT, 6])
        mv = sb("mv", [P, NT, 2])
        rstd = sb("rstd", [P, NT])
        lnv = sb("lnv", [P, NT])
        xbias, ust, umv = sb("xbias", [P, NT]), sb("ust", [P, NT, 6]), sb("umv", [P, NT, 2])
        uvar, urstd, xneg = sb("uvar", [P, NT]), sb("urstd", [P, NT]), sb("xneg", [P, NT])
        sm = sb("sm", [P, 5, NT * NH])

        XW = TAPS - 1 + S
        xm32 = region_a[:, 0:MC * XW].rearrange("p (m t) -> p m t", m=MC)
        rows_a = region_a[0:NH, 0:4 * S].rearrange("p (r t) -> p r t", r=4)
        num = region_a[:, :].rearrange("p (n w) -> p n w", n=NT)
        num4 = region_a[:, :].rearrange("p (n v) -> p n v", v=VW)
        b16 = region_b[:, :].bitcast(F16).rearrange("p (a m t) -> p a m t", a=2, m=MC)
        ktok = region_b[:, :].rearrange("p (n c) -> p n c", n=NT)
        cen = region_b[:, :].rearrange("p (n d) -> p n d", d=DH)
        xa16 = region_e[:, :].bitcast(F16).rearrange("p (a m t) -> p a m t", a=2, m=MC)
        xn16 = region_f[:, 0:KC * S].bitcast(F16).rearrange("p (a k t) -> p a k t", a=2, k=KC)
        kf16 = region_f[:, :].bitcast(F16).rearrange("p (a m t) -> p a m t", a=2, m=MC)
        xn = region_h[:, :].rearrange("p (n c) -> p n c", n=NT)
        rows_h = region_h[0:NH, :].rearrange("p (r t) -> p r t", r=2)
        dbuf = region_h[:, 0:2 * HALF].rearrange("p (r t) -> p r t", r=2)
        pbuf = region_h[:, 2 * HALF:4 * HALF].rearrange("p (r t) -> p r t", r=2)
        hbuf = region_h[:, :].rearrange("p (r t) -> p r t", r=4)
        mid16 = sq_buf[0:NH, :].bitcast(BF16).rearrange("p (r t) -> p r t", r=2)
        sq = sq_buf[:, :].rearrange("p (n d) -> p n d", d=DH)
        s_wup = xa[:, :, :].rearrange("p m t -> p (m t)")[:, 0:KC * 2 * INNER].rearrange("p (k n) -> p k n", k=KC)
        s_wdn = sz[:, 0, :].rearrange("p (m n) -> p m n", m=MC)
        s_blk = region_b[:, 0:4 * MC * P].rearrange("p (w m c) -> p w m c", w=4, m=MC)
        s_sel = region_f[0:GROW, 0:NH * P].rearrange("p (h t) -> p h t", h=NH)
        s_neg = region_f[:, NH * P:NH * P + 4 * P].rearrange("p (h t) -> p h t", h=4)
        s_wg = region_e[:, 0:3 * MC * 40].rearrange("p (w m c) -> p w m c", w=3, m=MC)

        w_in, blk_in, small_in = sem("m0_w_in"), sem("m0_blk_in"), sem("m0_small_in")
        fold_full, fold_hi, w_hi, w_ready = sem("m0_fold_full"), sem("m0_fold_hi"), sem("m0_w_hi"), sem("m0_w_ready")
        init_done = sem("m0_init_done")
        x_in, x_stats, x_rstd = sem("m0_x_in"), sem("m0_x_stats"), sem("m0_x_rstd")
        xn_ready, xt_full, xt_hi, xt_lo = sem("m0_xn"), sem("m0_xt_full"), sem("m0_xt_hi"), sem("m0_xt_lo")
        up_full, up_act, up_lo = sem("m0_up_full"), sem("m0_up_act"), sem("m0_up_lo")
        conv_init, conv_done = sem("m0_conv_init"), sem("m0_conv_done")
        xa_hi, xa_lo = sem("m0_xa_hi"), sem("m0_xa_lo")
        gates_full, gates_read = sem("m0_gates_full"), sem("m0_gates_read")
        gate_abs, gate_log, gate_scan = sem("m0_gate_abs"), sem("m0_gate_log"), sem("m0_gate_scan")
        gate_args, gate_exp, hi_ready = sem("m0_gate_args"), sem("m0_gate_exp"), sem("m0_hi")
        mid_ready, parts_ready = sem("m0_mid"), sem("m0_parts")
        v_full, v_read = sem("m0_v_full"), sem("m0_v_read")
        kf_full, kf_hi, kf_lo = sem("m0_kf_full"), sem("m0_kf_hi"), sem("m0_kf_lo")
        kt_full, kt_read = sem("m0_kt_full"), sem("m0_kt_read")
        cols_full, cols_ready = sem("m0_cols_full"), sem("m0_cols")
        s_full, d_full, d_ready, p_ready = sem("m0_s_full"), sem("m0_d_full"), sem("m0_d"), sem("m0_p")
        kw_ready, av_full, comb_done = sem("m0_kw"), sem("m0_av_full"), sem("m0_comb")
        st_full, st_done = sem("m0_st_full"), sem("m0_st")
        mean_ready, cen_ready, cen_last, sq_ready = sem("m0_mean"), sem("m0_cen"), sem("m0_cen_last"), sem("m0_sq")
        var_ready, hn_ready, hn_last, skx_ready = sem("m0_var"), sem("m0_hn"), sem("m0_hn_last"), sem("m0_skx")
        ht_full, pre_ready, h32_ready = sem("m0_ht_full"), sem("m0_pre"), sem("m0_h32")
        h_hi, h_lo, dn_full, x_added = sem("m0_h_hi"), sem("m0_h_lo"), sem("m0_dn_full"), sem("m0_x_added")
        u_stats, u_rstd, u_added = sem("m0_u_stats"), sem("m0_u_rstd"), sem("m0_u_added")
        us_full, us_read = sem("m0_us_full"), sem("m0_us_read")

        UP = [(h, m) for part in (0, MC) for h in range(2) for m in range(part, part + MC)]
        NP = NT // 2
        PW = 2 * NH
        NQ = 2 * NT
        NS = NQ - 2

        def unit_cols(q):
            return q // 2, q % 2

        block = stage.enter_context(nc.Block())

        @block.sync
        def _(sp):
            sp.dma_start(s_blk, A["blocks"]).then_inc(blk_in, 16)
            sp.dma_start(s_wg, A["w_gates"]).then_inc(blk_in, 16)
            sp.dma_start(s_wup, A["w_up"].rearrange("(k p) n -> p k n", p=P)).then_inc(w_in, 16)
            sp.dma_start(s_wdn, A["w_down"].rearrange("(m p) n -> p m n", p=P)).then_inc(w_in, 16)
            sp.dma_start(pc[:, :, :], A["chan"]).then_inc(small_in, 16)
            sp.dma_start(gb[:, :], A["gate_bias"]).then_inc(small_in, 16)
            sp.dma_start(s_sel, A["sel"]).then_inc(small_in, 16)
            sp.dma_start(pair_sel[:, :, :], A["pair_sel"]).then_inc(small_in, 16)
            sp.dma_start(s_neg, A["negmask"]).then_inc(small_in, 16)
            for b in range(B):
                sp.dma_start(X[:, b * NT:(b + 1) * NT, :],
                             A["x"][b * S:(b + 1) * S, :].rearrange("(n p) c -> p n c", p=P)).then_inc(x_in, 16)
                sp.wait_ge(x_in, b * 16 + 16)

        @block.tensor
        def _(pe):
            pe.wait_ge(blk_in, 32)
            for m in range(MC):
                pe.matmul(ps[0][:, m * P:(m + 1) * P], s_blk[:, 1, m, :], s_blk[:, 0, m, :], start=True, stop=True)
            for m in range(MC):
                o = ps[1][:, m * 40:(m + 1) * 40]
                pe.matmul(o, s_blk[:, 0, m, :], s_wg[:, 0, m, :], start=True, stop=False)
                pe.matmul(o, s_blk[:, 1, m, :], s_wg[:, 1, m, :], start=False, stop=True)
            for m in range(MC):
                last = pe.matmul(ps[2][:, m * 40:(m + 1) * 40], s_blk[:, 2, m, :], s_wg[:, 2, m, :],
                                 start=True, stop=True)
            last.then_inc(fold_full, 1)
            pe.wait_ge(w_ready, 1)
            pe.wait_ge(small_in, 80)

            def sums(b):
                pe.wait_ge(u_added, b * 3 + 3)
                for k in range(KC):
                    t = pe.matmul(ps[2][:, k:k + 1], xn[:, 0, k * P:(k + 1) * P], K["ones"], start=True, stop=True)
                t.then_inc(us_full, 1)

            def batch(b, first):
                for g in range(4):
                    half, k = g // 2, g % 2
                    pe.wait_ge(xn_ready, b * NT + 4 * half + 4)
                    if not first:
                        pe.wait_ge(x_added, b * NT - NT + g + 1)
                    for j in range(4):
                        t = pe.transpose(ps[g][:, j * P:(j + 1) * P], xn[:, 4 * half + j, k * P:(k + 1) * P],
                                         K["ident"])
                    t.then_inc(xt_full, 1)
                for u, (half, m) in enumerate(UP):
                    if u % 4 == 0:
                        pe.wait_ge(xt_lo, b * 4 + (2 * half + 2 if u == 0 else 4))
                    if u < 4 and not first:
                        pe.wait_ge(x_added, b * NT - NT + 4 + u + 1)
                    if u >= 8:
                        pe.wait_ge(up_act, b * 16 + u - 7)
                        pe.wait_ge(up_lo, b * 8 + u - 7)
                    for k in range(KC):
                        t = product3(pe, ps[(4 + u) % 8][:, :],
                                     [wup[:, a, k, m * P:(m + 1) * P] for a in (0, 1)],
                                     [xn16[:, a, k, half * HALF:(half + 1) * HALF] for a in (0, 1)],
                                     k == 0, k == KC - 1)
                    t.then_inc(up_full, 1)
                pe.wait_ge(up_act, b * 16 + 16)
                for m in range(MC):
                    pe.wait_ge(xa_lo, b * MC + m + 1)
                    for half in range(2):
                        t0 = slice(half * HALF, (half + 1) * HALF)
                        product3(pe, ps[half][0:40, :], [ga[:, a, m, :] for a in (0, 1)],
                                 [xa16[:, a, m, t0] for a in (0, 1)], m == 0, False)
                        t = product3(pe, ps[half][0:40, :], [gv[:, a, m, :] for a in (0, 1)],
                                     [b16[:, a, m, t0] for a in (0, 1)], False, m == MC - 1)
                        if m == MC - 1:
                            t.then_inc(gates_full, 1)
                for n in range(NT):
                    if n >= 6:
                        pe.wait_ge(gates_read, b * 2 + n - 5)
                    for m in range(MC):
                        t = product3(pe, ps[(2 + n) % 8][:, m * P:(m + 1) * P],
                                     [b16[:, a, m, n * P:(n + 1) * P] for a in (0, 1)],
                                     [wv[:, a, m, :] for a in (0, 1)], True, True)
                    t.then_inc(v_full, 1)
                if not first:
                    pe.wait_ge(v_read, b * NT + 1)
                    sums(b - 1)
                for j in range(8):
                    m, half = j // 2, j % 2
                    if j < 7:
                        pe.wait_ge(v_read, b * NT + j + 2)
                    elif not first:
                        pe.wait_ge(us_read, b)
                    t = product3(pe, ps[(11 + j) % 8][:, :], [gk[:, a, m, :] for a in (0, 1)],
                                 [xa16[:, a, m, half * HALF:(half + 1) * HALF] for a in (0, 1)], True, True)
                    t.then_inc(kf_full, 1)
                for n in range(NT):
                    pe.wait_ge(kf_lo, b * 8 + n + 1)
                    for m in range(MC):
                        t = product3(pe, ps[(19 + n) % 8][:, m * P:(m + 1) * P],
                                     [xa16[:, a, m, n * P:(n + 1) * P] for a in (0, 1)],
                                     [gk[:, a, m, :] for a in (0, 1)], True, True)
                    t.then_inc(kt_full, 1)
                pe.wait_ge(kt_read, b * NT + NT)
                pe.wait_ge(gate_exp, b * 4 + 4)
                for g in range(2):
                    for j in range(4):
                        n = 4 * g + j
                        t = pe.transpose(ps[2 + g][:, j * P:j * P + GROW], stack[0:GROW, n * P:(n + 1) * P],
                                         K["ident"][0:GROW, 0:GROW])
                    t.then_inc(cols_full, 1)
                for m in range(MC):
                    t = pe.matmul(ps[4][:, m * NT:(m + 1) * NT], pair_sel[:, m, :], dec_row[:, :],
                                  start=True, stop=True)
                t.then_inc(cols_full, 1)
                pe.wait_ge(hi_ready, b * 2 + 2)
                pe.wait_ge(parts_ready, b * 4 + 4)
                pe.wait_ge(cols_ready, b * 3 + 3)

                def scores(q):
                    c, hf = unit_cols(q)
                    t0 = slice(c * P, (c + 1) * P)
                    if q >= 2:
                        pe.wait_ge(p_ready, b * NQ + q - 1)
                    for pr in range(2):
                        for par in range(2):
                            rows = slice(64 * par, 64 * par + 64)
                            m = 2 * hf + pr
                            t = product3(pe, ps[2 * (q % 2) + par][:, pr * P:(pr + 1) * P],
                                         [kf16[rows, a, m, t0] for a in (0, 1)],
                                         [xa16[rows, a, m, t0] for a in (0, 1)], True, True)
                    t.then_inc(s_full, 1)

                def log_weights(q):
                    c, hf = unit_cols(q)
                    t0 = slice(c * P, (c + 1) * P)
                    if q >= 1:
                        pe.wait_ge(d_ready, b * NQ + q)
                    pe.matmul(ps[4][:, :], ident16[:, :], negmask[:, :, :].rearrange("p h t -> p (h t)"),
                              start=True, stop=False)
                    pe.matmul(ps[4][:, :], part_a[:, t0],
                              sel[:, 4 * hf:4 * hf + 4, :].rearrange("p h t -> p (h t)"), start=False, stop=False)
                    for s in range(4):
                        t = pe.matmul(ps[4][:, s * P:(s + 1) * P], sel[:, 4 * hf + s, :], part_n[:, t0],
                                      start=False, stop=(s == 3))
                    t.then_inc(d_full, 1)

                scores(0)
                log_weights(0)
                for q in range(NQ):
                    c, hf = unit_cols(q)
                    t0 = slice(c * P, (c + 1) * P)
                    if q + 1 < NQ:
                        scores(q + 1)
                        log_weights(q + 1)
                    pe.wait_ge(p_ready, b * NQ + q + 1)
                    if q >= 1:
                        pe.wait_ge(comb_done, b * NQ + q)
                    for s in range(4):
                        h = slot_head(4 * hf + s)
                        t = pe.matmul(ps[5][:, (h % 4) * VW:(h % 4 + 1) * VW], pbuf[:, q % 2, s * P:(s + 1) * P],
                                      vext[:, c, h * VW:(h + 1) * VW], start=True, stop=True)
                    if c > 0:
                        pe.wait_ge(st_done, b * NS + q - 1)
                        for pr in range(2):
                            t = pe.matmul(ps[6][:, pr * 2 * VW:(pr + 1) * 2 * VW], xa[:, 2 * hf + pr, t0],
                                          state[:, 2 * hf + pr, :], start=True, stop=True)
                    t.then_inc(av_full, 1)
                    if c < NT - 1:
                        pe.wait_ge(kw_ready, b * NS + q + 1)
                        if q >= 1:
                            pe.wait_ge(st_done, b * NS + q)
                        for pr in range(2):
                            m = 2 * hf + pr
                            t = pe.matmul(ps[7][:, pr * 2 * VW:(pr + 1) * 2 * VW], kt[:, q % 2, pr * P:(pr + 1) * P],
                                          vext[:, c, m * 2 * VW:(m + 1) * 2 * VW], start=True, stop=True)
                        t.then_inc(st_full, 1)
                for half in range(2):
                    for pair in range(2):
                        if half == 1 and pair == 1:
                            pe.wait_ge(hn_last, b + 1)
                        else:
                            pe.wait_ge(hn_ready, b * 3 + 2 * half + pair + 1)
                        if half == 1 and pair == 0:
                            pe.wait_ge(comb_done, b * NQ + NQ)
                        for m in range(MC):
                            for j in (2 * pair, 2 * pair + 1):
                                t = pe.transpose(ps[4 * half + m][:, j * P:(j + 1) * P],
                                                 ktok[:, 4 * half + j, m * P:(m + 1) * P], K["ident"])
                            if pair == 1:
                                t.then_inc(ht_full, 1)
                    pe.wait_ge(h_lo, b * 8 + 4 * half + 4)
                    for n in range(4 * half, 4 * half + 4):
                        for m in range(MC):
                            t = product3(pe, ps[n][:, 0:C], [xa16[:, a, m, n * P:(n + 1) * P] for a in (0, 1)],
                                         [wdn[:, a, m, :] for a in (0, 1)], m == 0, m == MC - 1)
                        t.then_inc(dn_full, 1)

            batch(0, True)
            with pe.Fori(1, B) as b:
                batch(b, False)
            pe.wait_ge(x_added, B * NT)
            sums(B - 1)

        @block.scalar
        def _(act):
            act.wait_ge(w_in, 32)
            act.activation(wup[:, 0, :, :], s_wup, ACT.Identity)
            act.activation(wdn[:, 0, :, :], s_wdn, ACT.Identity)
            act.wait_ge(blk_in, 32)
            act.activation(wv[:, 0, :, :], s_blk[:, 3, :, :], ACT.Identity).then_inc(w_hi, 1)
            act.wait_ge(fold_full, 1)
            act.activation(gk[:, 0, :, :].rearrange("p m c -> p (m c)"), ps[0][:, :], ACT.Identity, scale=DH ** -0.5)
            act.activation(ga[:, 0, :, :].rearrange("p m c -> p (m c)"), ps[1][:, 0:MC * 40], ACT.Identity)
            act.activation(gv[:, 0, :, :].rearrange("p m c -> p (m c)"), ps[2][:, 0:MC * 40],
                           ACT.Identity).then_inc(fold_hi, 1)
            act.wait_ge(small_in, 80)
            act.activation(sel[:, :, :], s_sel, ACT.Identity)
            act.activation(negmask[:, :, :], s_neg, ACT.Identity)
            act.activation(ident16[:, :], K["ident"], ACT.Identity)
            act.wait_ge(init_done, 1)

            def normalise(b, n):
                act.activation(xn[:, n, :], row(X, b * NT + n), ACT.Identity, scale=rstd[:, n:n + 1],
                               bias=xbias[:, n:n + 1]).then_inc(xn_ready, 1)

            def batch(b, last):
                for g in range(4):
                    half, k = g // 2, g % 2
                    act.wait_ge(xt_full, b * 4 + g + 1)
                    act.activation(xn16[:, 0, k, half * HALF:(half + 1) * HALF], ps[g][:, :],
                                   ACT.Identity).then_inc(xt_hi, 1)

                def silu_pair(i):
                    for m in (2 * i, 2 * i + 1):
                        act.wait_ge(conv_done, b * MC + m + 1)
                        act.activation(xa16[:, 0, m, :], xa[:, m, :], ACT.Silu)
                    act.drain()
                    for m in (2 * i, 2 * i + 1):
                        act.activation(xa[:, m, :], xa[:, m, :], ACT.Silu).then_inc(xa_hi, 1)

                for u, (half, m) in enumerate(UP):
                    src = ps[(4 + u) % 8][:, :]
                    t0 = slice(half * HALF, (half + 1) * HALF)
                    act.wait_ge(up_full, b * 16 + u + 1)
                    if m < MC:
                        act.activation(xm32[:, m, TAPS - 1 + half * HALF:TAPS - 1 + (half + 1) * HALF], src,
                                       ACT.Identity)
                        if m < 2:
                            t = act.activation(xa[:, m, t0], src, ACT.Identity, bias=pc[:, m, PC_CB:PC_CB + 1],
                                               scale=pc[:, m, TAPS - 1:TAPS])
                            if half == 1:
                                t.then_inc(conv_init, 1)
                        act.activation(b16[:, 0, m, t0], src, ACT.Identity).then_inc(up_act, 1)
                    else:
                        act.activation(sz[:, m - MC, t0], src, ACT.Silu).then_inc(up_act, 1)
                    if u == 8:
                        act.drain()
                        for i in (2, 3):
                            act.activation(xa[:, i, :], xm32[:, i, TAPS - 1:TAPS - 1 + S], ACT.Identity,
                                           bias=pc[:, i, PC_CB:PC_CB + 1],
                                           scale=pc[:, i, TAPS - 1:TAPS]).then_inc(conv_init, 1)
                    if u == 13:
                        silu_pair(0)
                silu_pair(1)
                act.wait_ge(gate_abs, b + 1)
                act.activation(rows_a[:, 1, :], rows_a[:, 1, :], ACT.Exp)
                act.drain()
                act.activation(rows_a[:, 1, :], rows_a[:, 1, :], ACT.Ln,
                               bias=K["ones"][0:NH, :]).then_inc(gate_log, 1)
                for n in range(NT):
                    act.wait_ge(v_full, b * NT + n + 1)
                    act.activation(vext[:, n, :].rearrange("p (h v) -> p h v", v=VW)[:, :, 0:DH],
                                   ps[(2 + n) % 8][:, :].rearrange("p (h v) -> p h v", v=DH),
                                   ACT.Identity).then_inc(v_read, 1)
                for j in range(8):
                    m, half = j // 2, j % 2
                    act.wait_ge(kf_full, b * 8 + j + 1)
                    act.activation(kf16[:, 0, m, half * HALF:(half + 1) * HALF], ps[(11 + j) % 8][:, :],
                                   ACT.Identity).then_inc(kf_hi, 1)
                act.wait_ge(gate_scan, b + 1)
                act.activation(part_n[0:NH, :], rows_a[:, 0, :], ACT.Identity, scale=-1.0).then_inc(hi_ready, 1)
                act.activation(part_a[0:NH, :], rows_a[:, 3, :], ACT.Identity).then_inc(hi_ready, 1)
                act.wait_ge(gate_args, b + 1)
                act.activation(stack[0:NH, :], rows_h[:, 0, :], ACT.Exp).then_inc(gate_exp, 1)
                act.activation(stack[32:32 + NH, :], rows_h[:, 1, :], ACT.Exp).then_inc(gate_exp, 1)
                act.activation(stack[64:64 + NH, :], rows_a[:, 1, :], ACT.Exp).then_inc(gate_exp, 1)
                act.activation(dec_row[:, :], dec_row[:, :], ACT.Exp).then_inc(gate_exp, 1)
                for n in range(NT):
                    act.wait_ge(kt_full, b * NT + n + 1)
                    act.activation(ktok[:, n, :], ps[(19 + n) % 8][:, :], ACT.Identity).then_inc(kt_read, 1)
                for i, part in enumerate((part_n, part_a)):
                    act.wait_ge(mid_ready, b * 2 + i + 1)
                    act.activation(part[32:32 + NH, :], mid16[:, i, :], ACT.Identity).then_inc(parts_ready, 1)

                def skip_half(half):
                    act.wait_ge(av_full, b * NQ + (half + 1) * NT)
                    for m in range(MC):
                        x = xa[:, m, half * HALF:(half + 1) * HALF]
                        t = act.activation(x, x, ACT.Identity, scale=pc[:, m, PC_SKIP:PC_SKIP + 1])
                    t.then_inc(skx_ready, 1)

                for q in range(NQ):
                    act.wait_ge(d_full, b * NQ + q + 1)
                    if q >= 2:
                        act.wait_ge(p_ready, b * NQ + q - 1)
                    else:
                        act.wait_ge(cols_ready, b * 3 + 3)
                    act.activation(dbuf[:, q % 2, :], ps[4][:, :], ACT.Exp).then_inc(d_ready, 1)
                    if q % 4 == 2 and q > 4:
                        act.wait_ge(cen_ready, b * 3 + q // 4)
                        act.activation(sq, cen[:, (q // 4 - 1) * PW:q // 4 * PW, :], ACT.Square).then_inc(sq_ready, 1)
                    if q == 11:
                        skip_half(0)
                skip_half(1)
                act.wait_ge(cen_last, b + 1)
                act.activation(sq, cen[:, (NP - 1) * PW:NP * PW, :], ACT.Square).then_inc(sq_ready, 1)
                for g in range(8):
                    half, m = g // 4, g % 4
                    act.wait_ge(h32_ready, b * 8 + g + 1)
                    act.activation(xa16[:, 0, m, half * HALF:(half + 1) * HALF], hbuf[:, g % 4, :],
                                   ACT.Identity).then_inc(h_hi, 1)
                if not last:
                    act.wait_ge(x_rstd, b + 2)
                    for n in range(NT):
                        if n % 2 == 0:
                            act.wait_ge(h_lo, b * 8 + 5 + n // 2)
                        normalise(b + 1, n)

            act.wait_ge(x_rstd, 1)
            for n in range(NT):
                normalise(0, n)
            with act.Fori(0, B - 1) as b:
                batch(b, False)
            batch(B - 1, True)

        @block.gpsimd
        def _(pool):
            pool.memset(stack[:, :], 0.0)
            pool.memset(part_a[:, :], 0.0)
            pool.memset(part_n[:, :], 0.0)
            pool.memset(state[:, :, :], 0.0)
            pool.memset(vext[:, :, :], 1.0)
            pool.drain().then_inc(init_done, 1)

            def x_root(b):
                pool.wait_ge(x_stats, b + 1)
                pool.tensor_tensor(rstd[:, :], lnv[:, :], K["neg_half"], ALU.pow)
                pool.drain()
                pool.tensor_tensor(xbias[:, :], xneg[:, :], rstd[:, :], ALU.mult).then_inc(x_rstd, 1)

            def sums_add(b, last):
                pool.wait_ge(u_stats, b + 1)
                if not last:
                    pool.wait_ge(xt_full, b * 4 + 8)
                pool.tensor_tensor(urstd[:, :], uvar[:, :], K["neg_half"], ALU.pow).then_inc(u_rstd, 1)
                pool.drain()
                for h in (0, 4):
                    pool.tensor_tensor(xn[:, h:h + 4, :], X[:, bass.ds(b * NT + h, 4), :],
                                       umv[:, h:h + 4, 0].unsqueeze(2).broadcast_to([P, 4, C]), ALU.subtract)
                pool.drain()
                for h in (0, 4):
                    pool.tensor_tensor(xn[:, h:h + 4, :], xn[:, h:h + 4, :],
                                       urstd[:, h:h + 4].unsqueeze(2).broadcast_to([P, 4, C]), ALU.mult)
                pool.drain()
                for h in (4, 2, 1):
                    pool.tensor_tensor(xn[:, 0:h, :], xn[:, 0:h, :], xn[:, h:2 * h, :], ALU.add).then_inc(u_added, 1)
                    pool.drain()

            def batch(b, first, last):
                if not first:
                    sums_add(b - 1, False)

                def keys(q):
                    c, hf = unit_cols(q)
                    if q >= 2:
                        pool.wait_ge(st_full, b * NS + q - 1)
                    pool.tensor_tensor(kt[:, q % 2, :].rearrange("p (h d) -> p h d", h=4),
                                       ktok[:, c, hf * 4 * DH:(hf + 1) * 4 * DH].rearrange("p (h d) -> p h d", h=4),
                                       cols[:, c, 64 + 4 * hf:68 + 4 * hf].unsqueeze(2).broadcast_to([P, 4, DH]),
                                       ALU.mult).then_inc(kw_ready, 1)

                def centre(p):
                    pool.drain()
                    pool.wait_ge(mean_ready, b * 3 + p + 1)
                    pool.tensor_tensor(cen[:, p * PW:(p + 1) * PW, :], num4[:, p * PW:(p + 1) * PW, 0:DH],
                                       sm[:, 1, p * PW:(p + 1) * PW].unsqueeze(2).broadcast_to([P, PW, DH]),
                                       ALU.subtract).then_inc(cen_ready, 1)

                def scale(p):
                    pool.wait_ge(var_ready, b * 3 + p + 1)
                    pool.tensor_tensor(sm[:, 3, p * PW:(p + 1) * PW], sm[:, 2, p * PW:(p + 1) * PW],
                                       K["neg_half"][:, 0:1].broadcast_to([P, PW]), ALU.pow)
                    pool.drain()
                    pool.tensor_tensor(cen[:, p * PW:(p + 1) * PW, :], cen[:, p * PW:(p + 1) * PW, :],
                                       sm[:, 3, p * PW:(p + 1) * PW].unsqueeze(2).broadcast_to([P, PW, DH]),
                                       ALU.mult).then_inc(hn_ready, 1)

                pool.wait_ge(kt_read, b * NT + NT)
                pool.wait_ge(cols_ready, b * 3 + 3)
                for q in range(NS):
                    keys(q)
                    if q in (5, 9, 13):
                        centre(q // 4 - 1)
                    if q in (8, 12):
                        scale(q // 4 - 2)
                    if q == 10 and not last:
                        x_root(b + 1)
                scale(NP - 2)
                for g in range(8):
                    half, m = g // 4, g % 4
                    pool.wait_ge(pre_ready, b * 8 + g + 1)
                    pool.tensor_tensor(hbuf[:, g % 4, :], hbuf[:, g % 4, :],
                                       sz[:, m, half * HALF:(half + 1) * HALF], ALU.mult).then_inc(h32_ready, 1)

            x_root(0)
            batch(0, True, False)
            with pool.Fori(1, B - 1) as b:
                batch(b, False, False)
            batch(B - 1, False, True)
            sums_add(B - 1, True)

        @block.vector
        def _(dve):
            dve.wait_ge(w_hi, 1)
            dve.tensor_tensor(wup[:, 1, :, :], s_wup, wup[:, 0, :, :], ALU.subtract)
            dve.tensor_tensor(wdn[:, 1, :, :], s_wdn, wdn[:, 0, :, :], ALU.subtract)
            dve.tensor_tensor(wv[:, 1, :, :], s_blk[:, 3, :, :], wv[:, 0, :, :], ALU.subtract)
            dve.wait_ge(fold_hi, 1)
            dve.scalar_tensor_tensor(out=gk[:, 1, :, :].rearrange("p m c -> p (m c)"), in0=ps[0][:, :],
                                     scalar=DH ** -0.5, in1=gk[:, 0, :, :].rearrange("p m c -> p (m c)"),
                                     op0=ALU.mult, op1=ALU.subtract)
            dve.tensor_tensor(ga[:, 1, :, :].rearrange("p m c -> p (m c)"), ps[1][:, 0:MC * 40],
                              ga[:, 0, :, :].rearrange("p m c -> p (m c)"), ALU.subtract)
            dve.tensor_tensor(gv[:, 1, :, :].rearrange("p m c -> p (m c)"), ps[2][:, 0:MC * 40],
                              gv[:, 0, :, :].rearrange("p m c -> p (m c)"), ALU.subtract).then_inc(w_ready, 1)
            dve.wait_ge(small_in, 80)

            def x_moments(b, n):
                dve.bn_stats(st6[:, n, :], row(X, b * NT + n))

            def x_variance():
                dve.drain()
                for n in range(NT):
                    dve.bn_aggr(mv[:, n, :], st6[:, n, :])
                dve.drain()
                dve.tensor_scalar(lnv[:, :], mv[:, :, 1], 1e-6, None, ALU.add)
                dve.tensor_scalar(xneg[:, :], mv[:, :, 0], -1.0, None, ALU.mult).then_inc(x_stats, 1)

            def sums_moments(b, n):
                dve.bn_stats(ust[:, n, :], row(X, b * NT + n))

            def sums_variance():
                dve.drain()
                for n in range(NT):
                    dve.bn_aggr(umv[:, n, :], ust[:, n, :])
                dve.drain()
                dve.tensor_scalar(uvar[:, :], umv[:, :, 1], 1e-5, None, ALU.add).then_inc(u_stats, 1)

            def sums_kept(b):
                dve.wait_ge(u_rstd, b + 1)
                dve.tensor_copy(K["ln_mean"][:, bass.ds(b * NT, NT)], umv[:, :, 0])
                dve.tensor_copy(K["ln_rstd"][:, bass.ds(b * NT, NT)], urstd[:, :])

            def sums_read(b):
                dve.wait_ge(us_full, b + 1)
                dve.tensor_copy(usum[:, :, bass.ds(b, 1)].rearrange("p k o -> p (k o)"),
                                ps[2][:, 0:KC]).then_inc(us_read, 1)

            def batch(b, first, last):
                for g in range(4):
                    half, k = g // 2, g % 2
                    t0 = slice(half * HALF, (half + 1) * HALF)
                    dve.wait_ge(xt_hi, b * 4 + g + 1)
                    dve.tensor_tensor(xn16[:, 1, k, t0], ps[g][:, :], xn16[:, 0, k, t0],
                                      ALU.subtract).then_inc(xt_lo, 1)
                for m in range(MC):
                    dve.memset(xm32[:, m, 0:TAPS - 1], 0.0)
                for u in range(8):
                    half, m = UP[u]
                    t0 = slice(half * HALF, (half + 1) * HALF)
                    dve.wait_ge(up_act, b * 16 + u + 1)
                    dve.tensor_tensor(b16[:, 1, m, t0], ps[(4 + u) % 8][:, :], b16[:, 0, m, t0],
                                      ALU.subtract).then_inc(up_lo, 1)
                    if not first:
                        sums_moments(b - 1, u)
                if not first:
                    sums_variance()

                def low_act(m):
                    dve.wait_ge(xa_hi, b * MC + m + 1)
                    dve.tensor_tensor(xa16[:, 1, m, :], xa[:, m, :], xa16[:, 0, m, :],
                                      ALU.subtract).then_inc(xa_lo, 1)

                for i in range(2):
                    for j in range(TAPS - 1):
                        dve.drain()
                        for m in (2 * i, 2 * i + 1):
                            if j == 0:
                                dve.wait_ge(conv_init, b * MC + m + 1)
                            t = dve.scalar_tensor_tensor(out=xa[:, m, :], in0=xm32[:, m, j:j + S],
                                                         scalar=pc[:, m, j:j + 1], in1=xa[:, m, :],
                                                         op0=ALU.mult, op1=ALU.add)
                            if j == TAPS - 2:
                                t.then_inc(conv_done, 1)
                        if i == 1 and j >= 1:
                            low_act(j - 1)
                low_act(2)
                low_act(3)
                if not first:
                    sums_kept(b - 1)
                F, L, CUM, I = (rows_a[:, r, :] for r in range(4))
                for half in range(2):
                    t0 = slice(half * HALF, (half + 1) * HALF)
                    dve.wait_ge(gates_full, b * 2 + half + 1)
                    dve.tensor_scalar(F[:, t0], ps[half][32:32 + NH, :], gb[32:32 + NH, :], None, ALU.add)
                    dve.tensor_scalar(I[:, t0], ps[half][0:NH, :], gb[0:NH, :], None,
                                      ALU.add).then_inc(gates_read, 1)
                dve.drain()
                dve.scalar_tensor_tensor(out=L, in0=F, scalar=-1.0, in1=F, op0=ALU.mult,
                                         op1=ALU.min).then_inc(gate_abs, 1)
                dve.wait_ge(gate_log, b + 1)
                dve.scalar_tensor_tensor(out=F, in0=F, scalar=0.0, in1=L, op0=ALU.min, op1=ALU.subtract)
                dve.drain()
                dve.tensor_tensor_scan(CUM, F, F, 0.0, ALU.add, ALU.bypass)
                dve.drain()
                dve.tensor_tensor(I, I, CUM, ALU.subtract)
                dve.drain()
                dve.tensor_tensor_scan(F, I, I, -3.0e38, ALU.max, ALU.bypass)
                dve.drain().then_inc(gate_scan, 1)
                if not first:
                    sums_read(b - 1)
                Fc = F.rearrange("p (n t) -> p n t", n=NT)
                Ic = I.rearrange("p (n t) -> p n t", n=NT)
                Lc = L.rearrange("p (n t) -> p n t", n=NT)
                ends = Fc[:, :, P - 1:P]
                dve.scalar_tensor_tensor(out=rows_h[:, 0, :], in0=CUM, scalar=-1.0, in1=F, op0=ALU.mult,
                                         op1=ALU.subtract)
                Dc = rows_h[:, 1, :].rearrange("p (n t) -> p n t", n=NT)
                dve.memset(Dc[:, 0, :], 0.0)
                dve.tensor_tensor(Dc[:, 1:NT, :], ends[:, 0:NT - 1, :].broadcast_to([NH, NT - 1, P]), Fc[:, 1:NT, :],
                                  ALU.subtract)
                dve.tensor_tensor(Lc, Ic, ends.broadcast_to([NH, NT, P]), ALU.subtract)
                dve.memset(dec_row[:, 0:1], 0.0)
                dve.tensor_tensor(dec_row[:, 1:NT], Fc[:, 0:NT - 1, P - 1], Fc[:, 1:NT, P - 1],
                                  ALU.subtract)
                dve.drain().then_inc(gate_args, 1)

                def low_keys(j):
                    m, half = j // 2, j % 2
                    t0 = slice(half * HALF, (half + 1) * HALF)
                    dve.wait_ge(kf_hi, b * 8 + j + 1)
                    dve.tensor_tensor(kf16[:, 1, m, t0], ps[(11 + j) % 8][:, :], kf16[:, 0, m, t0],
                                      ALU.subtract).then_inc(kf_lo, 1)

                for j in range(4):
                    low_keys(j)
                rest = (CUM, rows_h[:, 0, :])
                for i, (src, sign, part) in enumerate(((F, -1.0, part_n), (I, 1.0, part_a))):
                    dve.wait_ge(hi_ready, b * 2 + i + 1)
                    if i == 1:
                        dve.wait_ge(gate_exp, b * 4 + 1)
                    dve.scalar_tensor_tensor(out=rest[i], in0=src, scalar=sign, in1=part[0:NH, :], op0=ALU.mult,
                                             op1=ALU.subtract)
                    dve.drain()
                    dve.tensor_copy(mid16[:, i, :], rest[i]).then_inc(mid_ready, 1)
                    low_keys(4 + 2 * i)
                    dve.drain()
                    dve.tensor_tensor(part[64:64 + NH, :], rest[i], mid16[:, i, :],
                                      ALU.subtract).then_inc(parts_ready, 1)
                    low_keys(5 + 2 * i)
                for g in range(2):
                    dve.wait_ge(cols_full, b * 3 + g + 1)
                    dve.tensor_copy(cols[:, 4 * g:4 * g + 4, :],
                                    ps[2 + g][:, :].rearrange("p (n r) -> p n r", n=4)[:, :, 0:GROW]
                                    ).then_inc(cols_ready, 1)
                dve.wait_ge(cols_full, b * 3 + 3)
                dve.tensor_copy(dec[:, :, :].rearrange("p m n -> p (m n)"), ps[4][:, 0:MC * NT]
                                ).then_inc(cols_ready, 1)
                dve.drain()
                dve.tensor_scalar(cols[:, :, 0:NH], cols[:, :, 0:NH], 1e-6, None, ALU.add)

                def weigh(q):
                    dve.wait_ge(s_full, b * NQ + q + 1)
                    dve.wait_ge(d_ready, b * NQ + q + 1)
                    if q >= 2:
                        dve.wait_ge(av_full, b * NQ + q - 1)
                    for par in range(2):
                        t1 = slice(par * 2 * P, (par + 1) * 2 * P)
                        t = dve.tensor_tensor(pbuf[:, q % 2, t1], ps[2 * (q % 2) + par][:, 0:2 * P],
                                              dbuf[:, q % 2, t1], ALU.mult)
                    t.then_inc(p_ready, 1)

                def combine(q):
                    c, hf = unit_cols(q)
                    dst = num[:, c, hf * 4 * VW:(hf + 1) * 4 * VW]
                    dve.wait_ge(av_full, b * NQ + q + 1)
                    if c == 0:
                        dve.tensor_copy(dst, ps[5][:, 0:4 * VW]).then_inc(comb_done, 1)
                    else:
                        dve.tensor_tensor(tmp[:, :].rearrange("p (h v) -> p h v", h=4),
                                          ps[6][:, 0:4 * VW].rearrange("p (h v) -> p h v", h=4),
                                          cols[:, c, 32 + 4 * hf:36 + 4 * hf].unsqueeze(2).broadcast_to([P, 4, VW]),
                                          ALU.mult)
                        dve.drain()
                        dve.tensor_tensor(dst, tmp[:, :], ps[5][:, 0:4 * VW], ALU.add).then_inc(comb_done, 1)

                def update(q):
                    c, hf = unit_cols(q)
                    dve.wait_ge(st_full, b * NS + q + 1)
                    for pr in range(2):
                        m = 2 * hf + pr
                        for par in range(2):
                            rows = slice(64 * par, 64 * par + 64)
                            own = state[rows, m, par * VW:(par + 1) * VW]
                            new = ps[7][rows, (2 * pr + par) * VW:(2 * pr + par + 1) * VW]
                            if c == 0:
                                t = dve.tensor_copy(own, new)
                            else:
                                t = dve.scalar_tensor_tensor(out=own, in0=own, scalar=dec[rows, m, c:c + 1],
                                                             in1=new, op0=ALU.mult, op1=ALU.add)
                    t.then_inc(st_done, 1)

                def pair_cols(i, p):
                    return sm[:, i, p * PW:(p + 1) * PW]

                def mean(p):
                    dve.drain()
                    den = num4[:, p * PW:(p + 1) * PW, DH]
                    dve.tensor_reduce(pair_cols(4, p), num4[:, p * PW:(p + 1) * PW, 0:DH], AX_X, ALU.add)
                    dve.scalar_tensor_tensor(out=pair_cols(0, p), in0=den, scalar=-1.0, in1=den, op0=ALU.mult,
                                             op1=ALU.max)
                    dve.drain()
                    t = dve.tensor_scalar(pair_cols(1, p), pair_cols(4, p), 1.0 / DH, None, ALU.mult)
                    if p < NP - 1:
                        t.then_inc(mean_ready, 1)
                    dve.scalar_tensor_tensor(out=pair_cols(0, p).rearrange("p (n h) -> p n h", n=2),
                                             in0=pair_cols(0, p).rearrange("p (n h) -> p n h", n=2), scalar=1e-6,
                                             in1=cols[:, 2 * p:2 * p + 2, 0:NH], op0=ALU.add, op1=ALU.max)
                    dve.drain()
                    dve.scalar_tensor_tensor(out=pair_cols(0, p), in0=pair_cols(0, p), scalar=1e-5,
                                             in1=pair_cols(0, p), op0=ALU.mult, op1=ALU.mult)

                def variance(p):
                    dve.wait_ge(sq_ready, b * NP + p + 1)
                    dve.tensor_reduce(pair_cols(4, p), sq, AX_X, ALU.add)
                    dve.drain()
                    t = dve.scalar_tensor_tensor(out=pair_cols(2, p), in0=pair_cols(4, p), scalar=1.0 / DH,
                                                 in1=pair_cols(0, p), op0=ALU.mult, op1=ALU.add)
                    if p < NP - 1:
                        t.then_inc(var_ready, 1)

                weigh(0)
                for q in range(NQ):
                    if q + 1 < NQ:
                        weigh(q + 1)
                    combine(q)
                    if q < NS:
                        update(q)
                    if q in (4, 8, 12):
                        mean(q // 4 - 1)
                    if q in (6, 10, 14):
                        variance(q // 4 - 1)
                    if not last:
                        if q == 0:
                            dve.wait_ge(x_in, b * 16 + 32)
                        if q < 8:
                            x_moments(b + 1, q)
                        if q == 9:
                            x_variance()

                def gate(g):
                    half, m = g // 4, g % 4
                    if g % 4 == 0:
                        dve.wait_ge(skx_ready, b * 2 + half + 1)
                    dve.wait_ge(ht_full, b * 8 + g + 1)
                    dve.scalar_tensor_tensor(out=hbuf[:, g % 4, :], in0=ps[g][:, :],
                                             scalar=pc[:, m, PC_NW:PC_NW + 1],
                                             in1=xa[:, m, half * HALF:(half + 1) * HALF],
                                             op0=ALU.mult, op1=ALU.add).then_inc(pre_ready, 1)

                def low_part(g):
                    half, m = g // 4, g % 4
                    dve.wait_ge(h_hi, b * 8 + g + 1)
                    dve.tensor_tensor(xa16[:, 1, m, half * HALF:(half + 1) * HALF], hbuf[:, g % 4, :],
                                      xa16[:, 0, m, half * HALF:(half + 1) * HALF],
                                      ALU.subtract).then_inc(h_lo, 1)

                def add(n):
                    dve.wait_ge(dn_full, b * NT + n + 1)
                    dve.tensor_tensor(row(X, b * NT + n), row(X, b * NT + n), ps[n][:, 0:C],
                                      ALU.add).then_inc(x_added, 1)

                p = NP - 1
                mean(p)
                last_pair = cen[:, p * PW:(p + 1) * PW, :]
                dve.tensor_tensor(last_pair, num4[:, p * PW:(p + 1) * PW, 0:DH],
                                  pair_cols(1, p).unsqueeze(2).broadcast_to([P, PW, DH]),
                                  ALU.subtract).then_inc(cen_last, 1)
                gate(0)
                gate(1)
                variance(p)
                dve.drain()
                inverse_root(dve, pair_cols(3, p), pair_cols(2, p), pair_cols(4, p))
                dve.tensor_tensor(last_pair, last_pair,
                                  pair_cols(3, p).unsqueeze(2).broadcast_to([P, PW, DH]),
                                  ALU.mult).then_inc(hn_last, 1)
                gate(2)
                gate(3)
                for g in range(4):
                    low_part(g)
                dve.drain()
                for g in range(4, 8):
                    gate(g)
                    add(g - 4)
                for g in range(4, 8):
                    low_part(g)
                for n in range(4, NT):
                    add(n)
                dve.drain()

            dve.wait_ge(x_in, 16)
            for n in range(NT):
                x_moments(0, n)
            x_variance()
            batch(0, True, False)
            with dve.Fori(1, B - 1) as b:
                batch(b, False, False)
            batch(B - 1, False, True)
            for n in range(NT):
                sums_moments(B - 1, n)
            sums_variance()
            sums_kept(B - 1)
            sums_read(B - 1)


def build(nc, A, out):
    with ExitStack() as ctx:
        def sb(name, shape, dt=F32):
            return ctx.enter_context(nc.sbuf_tensor(name, shape, dt))

        def sem(name):
            return ctx.enter_context(nc.semaphore(name))

        X = sb("X", [P, B * NT, C])
        ident = sb("ident", [P, P])
        consts = sb("consts", [P, 17])
        usum = sb("usum", [P, KC, B])
        ln_mean = sb("ln_mean", [P, B * NT])
        ln_rstd = sb("ln_rstd", [P, B * NT])
        K = {"ln_mean": ln_mean, "ln_rstd": ln_rstd, "ident": ident[:, :], "ones": consts[:, 0:1], "neg_half": consts[:, 1:1 + NT],
             "half": consts[:, 1 + NT:1 + 2 * NT]}
        c_in = sem("c_in")
        c_set = sem("c_set")
        with nc.Block() as block:
            @block.sync
            def _(sp):
                sp.dma_start(ident[:, :], A["ident"]).then_inc(c_in, 16)
                sp.wait_ge(c_in, 16)

            @block.vector
            def _(dve):
                dve.memset(consts[:, 0:1], 1.0)
                dve.memset(consts[:, 1:1 + NT], -0.5)
                dve.memset(consts[:, 1 + NT:1 + 2 * NT], 0.5).then_inc(c_set, 1)
                dve.wait_ge(c_set, 1)
        mixer0(nc, X, K, A, usum)
        experts(nc, X, K, A, usum, 0)
        mixer1(nc, X, K, A, usum)
        experts(nc, X, K, A, usum, 1, out)


def experts(nc, X, K, A, usum, layer, out=None):
    L = f"e{layer}_"
    sems = []
    with ExitStack() as ctx, cleared(nc, sems), ExitStack() as stage:
        def sb(name, shape, dt=F32):
            return ctx.enter_context(nc.sbuf_tensor(L + name, shape, dt))

        def sem(name):
            sems.append(ctx.enter_context(nc.semaphore(name)))
            return sems[-1]

        ps = [ctx.enter_context(nc.psum_tensor(f"{L}ps{i}", [P, HALF], F32)) for i in range(8)]
        wr = sb("wr", [P, KC, NE])
        br = sb("br", [B, NE])
        ones4 = sb("ones4", [B, P])
        own = sb("own", [B, B, TOPK])
        gam, bet = sb("gam", [P, C]), sb("bet", [P, C])
        lg, rw, ex = sb("lg", [B, NE]), sb("rw", [B, NE]), sb("ex", [B, NE])
        sc = sb("sc", [B, 12])
        top, idx = sb("top", [B, NE]), sb("idx", [B, NE], U32)
        wexp = sb("wexp", [B, B, TOPK])
        idx_row = sb("idx_row", [1, B * TOPK], U32)
        wcol = sb("wcol", [P, B, TOPK])
        s1, s2 = sb("s1", [P, TOPK, KC, FF]), sb("s2", [P, TOPK, FC, C])
        sb1, sb2 = sb("sb1", [P, TOPK, FC]), sb("sb2", [P, TOPK, C])
        w1, w2 = sb("w1", [P, TOPK, 2, KC, FF], F16), sb("w2", [P, TOPK, 2, FC, C], F16)
        b1, b2 = sb("b1", [P, TOPK, FC]), sb("b2", [P, C])
        u = sb("u", [P, NT, C])
        y = sb("y", [P, NT, C])
        uf = sb("uf", [P, 2, KC, S], F16)
        g32 = sb("g32", [P, 4, HALF])
        hp = sb("hp", [P, 2, 2, TOPK * FC, HALF], F16)
        yst, ymv = sb("yst", [P, NT, 6]), sb("ymv", [P, NT, 2])
        yvar, yrstd = sb("yvar", [P, NT]), sb("yrstd", [P, NT])

        names = ("small_in lg_full sm_max sm_exp r_rw ld_full sm_max2 sm_exp2 r_top r_exp r_wexp wc_full idx_ok "
                 "idx_in w1_in w2_in w2_scaled w1_hi w2_hi w1_split w2_split wc_read u_ready ut_full uf_hi "
                 "uf_lo h_full g_ready h_lo ub_ready y_full y_read y_stats y_rstd z_ready z_done x_out").split()
        (small_in, lg_full, sm_max, sm_exp, r_rw, ld_full, sm_max2, sm_exp2, r_top, r_exp, r_wexp, wc_full, idx_ok,
         idx_in, w1_in, w2_in, w2_scaled, w1_hi, w2_hi, w1_split, w2_split, wc_read, u_ready, ut_full, uf_hi,
         uf_lo, h_full, g_ready, h_lo, ub_ready, y_full, y_read, y_stats, y_rstd, z_ready, z_done,
         x_out) = (sem(L + n) for n in names)
        NU = TOPK * FC
        N2 = 2 * NU

        block = stage.enter_context(nc.Block())

        @block.sync
        def _(sp):
            sp.dma_start(wr[:, :, :], A[L + "wr"]).then_inc(small_in, 16)
            sp.dma_start(br[:, :], A[L + "br"].broadcast_to([B, NE])).then_inc(small_in, 16)
            sp.dma_start(ones4[:, :], A["ones4"]).then_inc(small_in, 16)
            sp.dma_start(own[:, :, :], A["own"]).then_inc(small_in, 16)
            sp.dma_start(gam[:, :], A[L + "gamma"].broadcast_to([P, C])).then_inc(small_in, 16)
            sp.dma_start(bet[:, :], A[L + "beta"].broadcast_to([P, C])).then_inc(small_in, 16)
            sp.wait_ge(idx_ok, 1)
            sp.dma_start(idx_row[:, :], idx[:, 0:TOPK]).then_inc(idx_in, 16)
            sp.wait_ge(idx_in, 16)

            def experts_of(b):
                return [sp.value_load(idx_row[0:1, bass.ds(b * TOPK + s, 1)], min_val=0, max_val=NE - 1)
                        for s in range(TOPK)]

            def load_first(chosen):
                for s, e in enumerate(chosen):
                    sp.dma_start(s1[:, s, :, :], A[L + "w1"][bass.ds(e, 1), :, :].rearrange(
                        "o (k p) f -> p (o k) f", p=P)).then_inc(w1_in, 16)
                    sp.dma_start(sb1[:, s, :], A[L + "b1"][bass.ds(e, 1), :, :].rearrange(
                        "o p f -> p (o f)")).then_inc(w1_in, 16)

            def load_second(chosen):
                for s, e in enumerate(chosen):
                    sp.dma_start(s2[:, s, :, :], A[L + "w2"][bass.ds(e, 1), :, :].rearrange(
                        "o (k p) f -> p (o k) f", p=P)).then_inc(w2_in, 16)
                    sp.dma_start(sb2[:, s, :], A[L + "b2"][bass.ds(e, 1), :].broadcast_to([P, C])).then_inc(w2_in, 16)

            def store(b):
                if out is not None:
                    sp.wait_ge(z_done, b * NT + NT)
                    sp.dma_start(out[bass.ds(b * S, S), :].rearrange("(n p) c -> p n c", p=P),
                                 X[:, bass.ds(b * NT, NT), :]).then_inc(x_out, 16)

            def reload(b):
                chosen = experts_of(b + 1)
                sp.wait_ge(w1_split, b + 1)
                load_first(chosen)
                sp.wait_ge(w2_split, b + 1)
                load_second(chosen)

            chosen = experts_of(0)
            load_first(chosen)
            load_second(chosen)
            reload(0)
            with sp.Fori(1, B - 1) as b:
                reload(b)
                store(b - 1)
            store(B - 2)
            store(B - 1)
            if out is not None:
                sp.wait_ge(x_out, 16 * B)

        @block.tensor
        def _(pe):
            pe.wait_ge(small_in, 96)
            for k in range(KC):
                t = pe.matmul(ps[0][0:B, 0:NE], usum[:, k, :], wr[:, k, :], start=(k == 0), stop=(k == KC - 1))
            t.then_inc(lg_full, 1)
            pe.wait_ge(r_rw, 1)
            pe.matmul(ps[1][0:B, 0:NE], ones4[:, 0:B], rw[:, :], start=True, stop=True).then_inc(ld_full, 1)
            pe.wait_ge(r_wexp, 1)
            pe.matmul(ps[4][:, 0:B * TOPK], ones4[:, :], wexp[:, :, :].rearrange("b c s -> b (c s)"),
                      start=True, stop=True).then_inc(wc_full, 1)

            def turn(b, half):
                pe.wait_ge(u_ready, b * NT + 4 * half + 4)
                for k in range(KC):
                    g = 2 * half + k
                    for j in range(4):
                        t = pe.transpose(ps[g][:, j * P:(j + 1) * P], u[:, 4 * half + j, k * P:(k + 1) * P],
                                         K["ident"])
                    t.then_inc(ut_full, 1)

            def compute(b, first, last):
                pe.wait_ge(w1_split, b + 1)
                for half in range(2):
                    pe.wait_ge(uf_lo, b * 4 + (4 if half else 2))
                    for j in range(NU):
                        i = half * NU + j
                        s, f = j // FC, j % FC
                        if i == 2:
                            pe.wait_ge(uf_lo, b * 4 + 4)
                        if i >= 4:
                            pe.wait_ge(g_ready, b * N2 + i - 3)
                        for k in range(KC):
                            t = product3(pe, ps[i % 4][:, :], [w1[:, s, a, k, f * P:(f + 1) * P] for a in (0, 1)],
                                         [uf[:, a, k, half * HALF:(half + 1) * HALF] for a in (0, 1)],
                                         k == 0, k == KC - 1)
                        t.then_inc(h_full, 1)
                pe.wait_ge(w2_split, b + 1)
                for n in range(NT):
                    half = n // 4
                    if n % 4 == 0:
                        pe.wait_ge(h_lo, b * N2 + (half + 1) * NU)
                    if n >= 4 or not first:
                        pe.wait_ge(y_read, b * NT + n - 3)
                    for j in range(NU):
                        s, f = j // FC, j % FC
                        t = product3(pe, ps[4 + n % 4][:, 0:C],
                                     [hp[:, half, a, j, (n % 4) * P:(n % 4 + 1) * P] for a in (0, 1)],
                                     [w2[:, s, a, f, :] for a in (0, 1)], j == 0, j == NU - 1)
                    t.then_inc(y_full, 1)
                    if n == 3 and not last:
                        pe.wait_ge(g_ready, b * N2 + N2)
                        turn(b + 1, 0)
                    if n == 5 and not last:
                        turn(b + 1, 1)

            turn(0, 0)
            turn(0, 1)
            pe.wait_ge(wc_read, 1)
            compute(0, True, False)
            with pe.Fori(1, B - 1) as b:
                compute(b, False, False)
            compute(B - 1, False, True)

        @block.scalar
        def _(act):
            act.wait_ge(sm_max, 1)
            act.activation(ex[:, :], lg[:, :], ACT.Exp, bias=sc[:, 0:1], accum_out=sc[:, 1:2]).then_inc(sm_exp, 1)
            act.wait_ge(sm_max2, 1)
            act.activation(ex[:, :], lg[:, :], ACT.Exp, bias=sc[:, 3:4], accum_out=sc[:, 4:5]).then_inc(sm_exp2, 1)
            act.wait_ge(r_top, 1)
            act.activation(sc[:, 7:8], sc[:, 6:7], ACT.Exp).then_inc(r_exp, 1)

            def turn_parts(b, half):
                for k in range(KC):
                    act.wait_ge(ut_full, b * 4 + 2 * half + k + 1)
                    act.activation(uf[:, 0, k, half * HALF:(half + 1) * HALF], ps[2 * half + k][:, :],
                                   ACT.Identity).then_inc(uf_hi, 1)

            def first_weights(b):
                act.drain()
                act.wait_ge(w1_in, b * 64 + 64)
                act.activation(b1[:, :, :], sb1[:, :, :], ACT.Identity)
                for s in range(TOPK):
                    act.activation(w1[:, s, 0, :, :], s1[:, s, :, :], ACT.Identity).then_inc(w1_hi, 1)
                act.drain()

            def hidden(b, i):
                s, f = (i % NU) // FC, i % FC
                act.wait_ge(h_full, b * N2 + i + 1)
                if i >= 4:
                    act.wait_ge(h_lo, b * N2 + i - 3)
                act.activation(hp[:, i // NU, 0, i % NU, :], ps[i % 4][:, :], ACT.Gelu, bias=b1[:, s, f:f + 1])
                act.activation(g32[:, i % 4, :], ps[i % 4][:, :], ACT.Gelu,
                               bias=b1[:, s, f:f + 1]).then_inc(g_ready, 1)

            def compute(b, last):
                for i in range(N2):
                    hidden(b, i)
                    if i in (1, 3):
                        s = i // 2
                        act.wait_ge(w2_scaled, b * TOPK + s + 1)
                        act.activation(w2[:, s, 0, :, :], s2[:, s, :, :], ACT.Identity).then_inc(w2_hi, 1)
                if not last:
                    first_weights(b + 1)
                    for half in range(2):
                        turn_parts(b + 1, half)

            first_weights(0)
            for half in range(2):
                turn_parts(0, half)
            with act.Fori(0, B - 1) as b:
                compute(b, False)
            compute(B - 1, True)

        @block.gpsimd
        def _(pool):
            pool.wait_ge(small_in, 96)

            def tail(b):
                pool.wait_ge(y_stats, b + 1)
                pool.tensor_tensor(yrstd[:, :], yvar[:, :], K["neg_half"], ALU.pow).then_inc(y_rstd, 1)
                for n in range(NT):
                    pool.wait_ge(z_ready, b * NT + n + 1)
                    pool.tensor_tensor(y[:, n, :], y[:, n, :], gam[:, :], ALU.mult)
                for n in range(NT):
                    if n == 0:
                        pool.drain()
                    pool.tensor_tensor(y[:, n, :], y[:, n, :], bet[:, :], ALU.add)
                pool.drain()
                for n in range(NT):
                    pool.tensor_tensor(row(X, b * NT + n), row(X, b * NT + n), y[:, n, :], ALU.add).then_inc(z_done, 1)
                pool.drain()

            def with_bias(b):
                pool.wait_ge(w2_split, b + 1)
                for n in range(NT):
                    pool.tensor_tensor(y[:, n, :], u[:, n, :], b2[:, :], ALU.add).then_inc(ub_ready, 1)

            with_bias(0)
            with pool.Fori(1, B - 1) as b:
                tail(b - 1)
                with_bias(b)
            tail(B - 2)
            with_bias(B - 1)
            tail(B - 1)

        @block.vector
        def _(dve):
            dve.wait_ge(small_in, 96)
            dve.wait_ge(lg_full, 1)
            dve.scalar_tensor_tensor(out=lg[:, :], in0=ps[0][0:B, 0:NE], scalar=1.0 / S, in1=br[:, :],
                                     op0=ALU.mult, op1=ALU.add)
            dve.drain()
            dve.tensor_reduce(sc[:, 8:9], lg[:, :], AX_X, ALU.max)
            dve.drain()
            dve.tensor_scalar(sc[:, 0:1], sc[:, 8:9], -1.0, None, ALU.mult).then_inc(sm_max, 1)
            dve.wait_ge(sm_exp, 1)
            dve.reciprocal(sc[:, 2:3], sc[:, 1:2])
            dve.drain()
            dve.tensor_scalar(rw[:, :], ex[:, :], sc[:, 2:3], None, ALU.mult).then_inc(r_rw, 1)
            dve.wait_ge(ld_full, 1)
            dve.tensor_scalar(lg[:, :], ps[1][0:B, 0:NE], float(S), None, ALU.mult)
            dve.drain()
            dve.reciprocal(lg[:, :], lg[:, :])
            dve.drain()
            dve.tensor_scalar(lg[:, :], lg[:, :], CAPACITY, 1.0, ALU.mult, ALU.min)
            dve.drain()
            dve.tensor_tensor(lg[:, :], lg[:, :], rw[:, :], ALU.mult)
            dve.drain()
            dve.tensor_reduce(sc[:, 9:10], lg[:, :], AX_X, ALU.max)
            dve.drain()
            dve.tensor_scalar(sc[:, 3:4], sc[:, 9:10], -1.0, None, ALU.mult).then_inc(sm_max2, 1)
            dve.wait_ge(sm_exp2, 1)
            dve.reciprocal(sc[:, 5:6], sc[:, 4:5])
            dve.drain()
            dve.tensor_scalar(rw[:, :], ex[:, :], sc[:, 5:6], None, ALU.mult)
            dve.drain()
            dve.max(top[:, :], rw[:, :])
            dve.drain()
            dve.max_index(idx[:, :], top[:, :], rw[:, :]).then_inc(idx_ok, 1)
            dve.tensor_tensor(sc[:, 6:7], top[:, 1:2], top[:, 0:1], ALU.subtract).then_inc(r_top, 1)
            dve.wait_ge(r_exp, 1)
            dve.tensor_scalar(sc[:, 8:9], sc[:, 7:8], 1.0, None, ALU.add)
            dve.drain()
            dve.reciprocal(sc[:, 10:11], sc[:, 8:9])
            dve.drain()
            dve.tensor_tensor(sc[:, 11:12], sc[:, 10:11], sc[:, 7:8], ALU.mult)
            dve.drain()
            dve.tensor_tensor(wexp[:, :, :], own[:, :, :],
                              sc[:, 10:12].unsqueeze(1).broadcast_to([B, B, TOPK]), ALU.mult).then_inc(r_wexp, 1)
            dve.wait_ge(wc_full, 1)
            dve.tensor_copy(wcol[:, :, :].rearrange("p b s -> p (b s)"), ps[4][:, 0:B * TOPK]).then_inc(wc_read, 1)
            dve.drain()

            def weight(b, s):
                return wcol[:, bass.ds(b, 1), s:s + 1].rearrange("p o s -> p (o s)")

            def front_norm(b):
                for n in range(NT):
                    dve.tensor_scalar(u[:, n, :], row(X, b * NT + n), K["ln_mean"][:, bass.ds(b * NT + n, 1)],
                                      K["ln_rstd"][:, bass.ds(b * NT + n, 1)],
                                      ALU.subtract, ALU.mult).then_inc(u_ready, 1)

            def first_weights(b, s):
                dve.wait_ge(w1_hi, b * TOPK + s + 1)
                t = dve.tensor_tensor(w1[:, s, 1, :, :], s1[:, s, :, :], w1[:, s, 0, :, :], ALU.subtract)
                if s == TOPK - 1:
                    t.then_inc(w1_split, 1)

            def turn_parts(b, half):
                t0 = slice(half * HALF, (half + 1) * HALF)
                for k in range(KC):
                    dve.wait_ge(uf_hi, b * 4 + 2 * half + k + 1)
                    dve.tensor_tensor(uf[:, 1, k, t0], ps[2 * half + k][:, :], uf[:, 0, k, t0],
                                      ALU.subtract).then_inc(uf_lo, 1)

            def scale_second(b):
                dve.wait_ge(w2_in, b * 64 + 64)
                for s in range(TOPK):
                    dve.tensor_scalar(s2[:, s, :, :], s2[:, s, :, :], weight(b, s), None,
                                      ALU.mult).then_inc(w2_scaled, 1)
                dve.tensor_scalar(b2[:, :], sb2[:, 0, :], weight(b, 0), None, ALU.mult)
                dve.drain()
                dve.scalar_tensor_tensor(out=b2[:, :], in0=sb2[:, 1, :], scalar=weight(b, 1), in1=b2[:, :],
                                         op0=ALU.mult, op1=ALU.add)

            def second_weights(b, s):
                dve.wait_ge(w2_hi, b * TOPK + s + 1)
                t = dve.tensor_tensor(w2[:, s, 1, :, :], s2[:, s, :, :], w2[:, s, 0, :, :], ALU.subtract)
                if s == TOPK - 1:
                    t.then_inc(w2_split, 1)

            def low_hidden(b, i):
                half, j = i // NU, i % NU
                dve.wait_ge(g_ready, b * N2 + i + 1)
                dve.tensor_tensor(hp[:, half, 1, j, :], g32[:, i % 4, :], hp[:, half, 0, j, :],
                                  ALU.subtract).then_inc(h_lo, 1)

            def sum_rows(b, n):
                dve.wait_ge(ub_ready, b * NT + n + 1)
                dve.wait_ge(y_full, b * NT + n + 1)
                dve.tensor_tensor(y[:, n, :], y[:, n, :], ps[4 + n % 4][:, 0:C], ALU.add).then_inc(y_read, 1)
                dve.drain()
                dve.bn_stats(yst[:, n, :], y[:, n, :])

            def sum_stats(b):
                dve.drain()
                for n in range(NT):
                    dve.bn_aggr(ymv[:, n, :], yst[:, n, :])
                dve.drain()
                dve.tensor_scalar(yvar[:, :], ymv[:, :, 1], 1e-5, None, ALU.add).then_inc(y_stats, 1)

            def sum_norm(b, n):
                dve.tensor_scalar(y[:, n, :], y[:, n, :], ymv[:, n, 0:1], yrstd[:, n:n + 1],
                                  ALU.subtract, ALU.mult).then_inc(z_ready, 1)

            def compute(b, first, last):
                scale_second(b)
                for i in range(N2):
                    low_hidden(b, i)
                    if i == 0 and not first:
                        dve.wait_ge(y_rstd, b)
                        for n in range(NT):
                            sum_norm(b - 1, n)
                    if i in (3, 5):
                        second_weights(b, (i - 3) // 2)
                if not last:
                    dve.wait_ge(ub_ready, b * NT + NT)
                    front_norm(b + 1)
                for n in range(NT):
                    sum_rows(b, n)
                    if not last:
                        if n in (1, 2):
                            first_weights(b + 1, n - 1)
                        if n in (4, 6):
                            turn_parts(b + 1, n // 2 - 2)
                sum_stats(b)

            front_norm(0)
            for s in range(TOPK):
                first_weights(0, s)
            for half in range(2):
                turn_parts(0, half)
            compute(0, True, False)
            with dve.Fori(1, B - 1) as b:
                compute(b, False, False)
            compute(B - 1, False, True)
            dve.wait_ge(y_rstd, B)
            for n in range(NT):
                sum_norm(B - 1, n)


def mixer1(nc, X, K, A, usum):
    sems = []
    with ExitStack() as ctx, cleared(nc, sems), ExitStack() as stage:
        def sb(name, shape, dt=F32):
            return ctx.enter_context(nc.sbuf_tensor("m1_" + name, shape, dt))

        def sem(name):
            sems.append(ctx.enter_context(nc.semaphore(name)))
            return sems[-1]

        ps = [ctx.enter_context(nc.psum_tensor(f"m1_ps{i}", [P, HALF], F32)) for i in range(4)]
        pa = [ctx.enter_context(nc.psum_tensor(f"m1_pa{i}", [P, 2 * HALF], F32)) for i in range(2)]
        wst = sb("wst", [P, 2, KC, C])
        wadj, waff = sb("wadj", [P, 2, KC, C], F16), sb("waff", [P, 2, KC, C], F16)
        aff_b, ln_g, ln_b = sb("aff_b", [P, C]), sb("ln_g", [P, C]), sb("ln_b", [P, C])
        nf = sb("nf", [P, NT, C])
        nf16 = sb("nf16", [P, 2, KC, S], F16)
        g16 = sb("g16", [P, 2, KC, S], F16)
        h32 = sb("h32", [P, 3, C])
        h16 = sb("h16", [P, 2, NT, C], F16)
        pr = sb("pr", [P, 2, S])
        pt16 = sb("pt16", [P, 2, 2, NT, P], F16)
        y = sb("y", [P, 2, C])
        un = sb("un", [P, NT, C])
        st6, mv = sb("st6", [P, NT, 6]), sb("mv", [P, NT, 2])
        ust, umv, uvar, urstd = sb("ust", [P, NT, 6]), sb("umv", [P, NT, 2]), sb("uvar", [P, NT]), sb("urstd", [P, NT])
        uneg, ubias, xneg = sb("uneg", [P, NT]), sb("ubias", [P, NT]), sb("xneg", [P, NT])
        sm = sb("sm", [P, 8, NT])
        mx, nmx = sb("mx", [P, 2]), sb("nmx", [P, 2])
        ssum = sb("ssum", [P, 2])
        yst, ymv, ys = sb("yst", [P, 2, 6]), sb("ymv", [P, 2, 2]), sb("ys", [P, 2, 4])
        names = ("w_in w_hi w_ready x_stats x_rstd n2_ready n_scale nf_scale nf_ready nt_full nf_hi nf_lo "
                 "gf_full gf_hi gf_lo hf_full h_ready h_hi h_lo a_full mx_ready p_ready pt_full pt_hi pt_lo o_full "
                 "y_stats y_rstd y_norm y_aff x_done u_stats u_rstd u_ready u_added us_full us_read").split()
        (w_in, w_hi, w_ready, x_stats, x_rstd, n2_ready, n_scale, nf_scale, nf_ready, nt_full, nf_hi, nf_lo,
         gf_full, gf_hi, gf_lo, hf_full, h_ready, h_hi, h_lo, a_full, mx_ready, p_ready, pt_full, pt_hi, pt_lo,
         o_full, y_stats, y_rstd, y_norm, y_aff, x_done, u_stats, u_rstd, u_ready, u_added,
         us_full, us_read) = (sem("m1_" + n) for n in names)
        block = stage.enter_context(nc.Block())

        @block.sync
        def _(sp):
            sp.dma_start(wst[:, 0, :, :], A["adj"].rearrange("(k p) n -> p k n", p=P)).then_inc(w_in, 16)
            sp.dma_start(wst[:, 1, :, :], A["affine"].rearrange("(k p) n -> p k n", p=P)).then_inc(w_in, 16)
            sp.dma_start(aff_b[:, :], A["affine_b"].broadcast_to([P, C])).then_inc(w_in, 16)
            sp.dma_start(ln_g[:, :], A["ln_g"].broadcast_to([P, C])).then_inc(w_in, 16)
            sp.dma_start(ln_b[:, :], A["ln_b"].broadcast_to([P, C])).then_inc(w_in, 16)
            sp.wait_ge(w_in, 80)

        @block.tensor
        def _(pe):
            pe.wait_ge(w_ready, 1)

            def front(b, first):
                for g in range(4):
                    half, k = g // 2, g % 2
                    pe.wait_ge(nf_ready, b * NT + 4 * half + 4)
                    for j in range(4):
                        t = pe.transpose(pa[half][:, k * HALF + j * P:k * HALF + (j + 1) * P],
                                         nf[:, 4 * half + j, k * P:(k + 1) * P], K["ident"])
                    t.then_inc(nt_full, 1)
                for i in range(4):
                    half, d = i // 2, i % 2
                    pe.wait_ge(nf_lo, b * 4 + (2 * half + 2 if i < 2 else 4))
                    if i >= 2 and not first:
                        pe.wait_ge(y_norm, b * NT + i - 3)
                    for k in range(KC):
                        t = product3(pe, ps[i][:, :], [wadj[:, a, k, d * P:(d + 1) * P] for a in (0, 1)],
                                     [nf16[:, a, k, half * HALF:(half + 1) * HALF] for a in (0, 1)],
                                     k == 0, k == KC - 1)
                    t.then_inc(gf_full, 1)
                for n in range(NT):
                    if n < 4:
                        pe.wait_ge(gf_lo, b * 4 + n + 1)
                    else:
                        pe.wait_ge(h_ready, b * NT + n - 3)
                    for k in range(KC):
                        t = product3(pe, ps[n % 4][:, 0:C], [nf16[:, a, k, n * P:(n + 1) * P] for a in (0, 1)],
                                     [waff[:, a, k, :] for a in (0, 1)], k == 0, k == KC - 1)
                    t.then_inc(hf_full, 1)

            def sums(b):
                pe.wait_ge(u_added, b * 3 + 3)
                for k in range(KC):
                    t = pe.matmul(ps[3][:, k:k + 1], un[:, 0, k * P:(k + 1) * P], K["ones"], start=True, stop=True)
                t.then_inc(us_full, 1)

            def attention(b, first):
                def logits(n):
                    if n >= 2:
                        pe.wait_ge(p_ready, b * NT + n - 1)
                    for half in range(2):
                        for k in range(KC):
                            t = product3(pe, pa[n % 2][:, half * HALF:(half + 1) * HALF],
                                         [g16[:, a, k, n * P:(n + 1) * P] for a in (0, 1)],
                                         [nf16[:, a, k, half * HALF:(half + 1) * HALF] for a in (0, 1)],
                                         k == 0, k == KC - 1)
                    t.then_inc(a_full, 1)

                def turn(n):
                    pe.wait_ge(p_ready, b * NT + n + 1)
                    for g in range(2):
                        if n >= 1:
                            pe.wait_ge(pt_lo, b * 2 * NT + 2 * n + g - 1)
                        for j in range(4):
                            t = pe.transpose(ps[g][:, j * P:(j + 1) * P], pr[:, n % 2, (4 * g + j) * P:(4 * g + j + 1) * P],
                                             K["ident"])
                        t.then_inc(pt_full, 1)

                def mix(n):
                    pe.wait_ge(pt_lo, b * 2 * NT + 2 * n + 2)
                    if n == 0:
                        pe.wait_ge(h_lo, b * NT + NT)
                    if n == 1 and not first:
                        pe.wait_ge(us_read, b)
                    if n >= 2:
                        pe.wait_ge(y_norm, b * NT + n - 1)
                    for m in range(NT):
                        t = product3(pe, ps[2 + n % 2][:, 0:C], [pt16[:, n % 2, a, m, :] for a in (0, 1)],
                                     [h16[:, a, m, :] for a in (0, 1)], m == 0, m == NT - 1)
                    t.then_inc(o_full, 1)

                logits(0)
                pe.wait_ge(h_ready, b * NT + NT)
                for n in range(NT):
                    if n + 1 < NT:
                        logits(n + 1)
                    if n == 1 and not first:
                        sums(b - 1)
                    turn(n)
                    if n >= 1:
                        mix(n - 1)
                mix(NT - 1)

            front(0, True)
            attention(0, True)
            with pe.Fori(1, B) as b:
                front(b, False)
                attention(b, False)
            sums(B - 1)

        @block.scalar
        def _(act):
            act.wait_ge(w_in, 80)
            act.activation(wadj[:, 0, :, :], wst[:, 0, :, :], ACT.Identity)
            act.activation(waff[:, 0, :, :], wst[:, 1, :, :], ACT.Identity).then_inc(w_hi, 1)

            def normalise(b, n):
                if n == 0:
                    act.wait_ge(nf_scale, b + 1)
                act.activation(nf[:, n, :], row(X, b * NT + n), ACT.Identity, scale=sm[:, 4, n:n + 1],
                               bias=sm[:, 6, n:n + 1]).then_inc(nf_ready, 1)

            def sums_norm(b, rows):
                if rows[0] == 0:
                    act.wait_ge(u_rstd, b + 1)
                for n in rows:
                    t = act.activation(un[:, n, :], row(X, b * NT + n), ACT.Identity, scale=urstd[:, n:n + 1],
                                       bias=ubias[:, n:n + 1])
                if rows[-1] == NT - 1:
                    t.then_inc(u_ready, 1)

            def compute(b, first, last):
                for g in range(4):
                    half, k = g // 2, g % 2
                    act.wait_ge(nt_full, b * 4 + g + 1)
                    act.activation(nf16[:, 0, k, half * HALF:(half + 1) * HALF],
                                   pa[half][:, k * HALF:(k + 1) * HALF], ACT.Identity).then_inc(nf_hi, 1)
                for i in range(4):
                    half, d = i // 2, i % 2
                    act.wait_ge(gf_full, b * 4 + i + 1)
                    act.activation(g16[:, 0, d, half * HALF:(half + 1) * HALF], ps[i][:, :],
                                   ACT.Identity).then_inc(gf_hi, 1)
                for n in range(NT):
                    act.wait_ge(h_ready, b * NT + n + 1)
                    act.activation(h16[:, 0, n, :], h32[:, n % 3, :], ACT.Identity).then_inc(h_hi, 1)
                    if n >= 4 and not first:
                        sums_norm(b - 1, [n - 4])
                if not first:
                    sums_norm(b - 1, range(4, NT))
                for n in range(NT):
                    act.wait_ge(mx_ready, b * NT + n + 1)
                    if n >= 2:
                        act.wait_ge(pt_full, b * 2 * NT + 2 * n - 2)
                        act.wait_ge(y_stats, b * NT + n - 1)
                    act.activation(pr[:, n % 2, :], pa[n % 2][:, :], ACT.Exp, bias=nmx[:, n % 2:n % 2 + 1],
                                   scale=5.0, accum_out=ssum[:, n % 2:n % 2 + 1]).then_inc(p_ready, 1)
                    if n >= 2:
                        act.wait_ge(o_full, b * NT + n - 1)
                    for g in range(2):
                        act.wait_ge(pt_full, b * 2 * NT + 2 * n + g + 1)
                        act.activation(pt16[:, n % 2, 0, 4 * g:4 * g + 4, :].rearrange("p m t -> p (m t)"),
                                       ps[g][:, :], ACT.Identity).then_inc(pt_hi, 1)
                    if n in (5, 6) and not last:
                        for r in range(4 * (n - 5), 4 * (n - 5) + 4):
                            normalise(b + 1, r)

            for n in range(NT):
                normalise(0, n)
            compute(0, True, False)
            with act.Fori(1, B - 1) as b:
                compute(b, False, False)
            compute(B - 1, False, True)
            sums_norm(B - 1, range(NT))

        @block.gpsimd
        def _(pool):
            pool.wait_ge(w_in, 80)

            def x_root(b):
                pool.wait_ge(x_stats, b + 1)
                pool.tensor_tensor(sm[:, 1, :], sm[:, 0, :], K["neg_half"], ALU.pow).then_inc(x_rstd, 1)

            def norm_root(b, i):
                if i == 0:
                    pool.wait_ge(n2_ready, b + 1)
                power = K["half"] if i else K["neg_half"]
                pool.tensor_tensor(sm[:, 4 + i, :], sm[:, 2, :], power, ALU.pow).then_inc(n_scale, 1)

            def sums_root(b):
                pool.wait_ge(u_stats, b + 1)
                pool.tensor_tensor(urstd[:, :], uvar[:, :], K["neg_half"], ALU.pow)
                pool.drain()
                pool.tensor_tensor(ubias[:, :], uneg[:, :], urstd[:, :], ALU.mult).then_inc(u_rstd, 1)

            def sums_add(b):
                pool.wait_ge(u_ready, b + 1)
                for h in (4, 2, 1):
                    pool.tensor_tensor(un[:, 0:h, :], un[:, 0:h, :], un[:, h:2 * h, :], ALU.add).then_inc(u_added, 1)
                    pool.drain()

            def attention(b, first, last):
                if not first:
                    sums_add(b - 1)
                for n in range(NT):
                    pool.wait_ge(y_stats, b * NT + n + 1)
                    pool.tensor_tensor(ys[:, n % 2, 3:4], ys[:, n % 2, 1:2], K["neg_half"][:, 0:1],
                                       ALU.pow).then_inc(y_rstd, 1)
                    pool.wait_ge(y_norm, b * NT + n + 1)
                    pool.tensor_tensor(y[:, n % 2, :], y[:, n % 2, :], ln_g[:, :], ALU.mult)
                    pool.drain()
                    pool.tensor_tensor(y[:, n % 2, :], y[:, n % 2, :], ln_b[:, :], ALU.add).then_inc(y_aff, 1)
                    if n == 1 and not last:
                        x_root(b + 1)
                    if n in (2, 3) and not last:
                        norm_root(b + 1, n - 2)
                sums_root(b)

            x_root(0)
            norm_root(0, 0)
            norm_root(0, 1)
            attention(0, True, False)
            with pool.Fori(1, B - 1) as b:
                attention(b, False, False)
            attention(B - 1, False, True)
            sums_add(B - 1)

        @block.vector
        def _(dve):
            dve.wait_ge(w_hi, 1)
            dve.tensor_tensor(wadj[:, 1, :, :], wst[:, 0, :, :], wadj[:, 0, :, :], ALU.subtract)
            dve.tensor_tensor(waff[:, 1, :, :], wst[:, 1, :, :], waff[:, 0, :, :], ALU.subtract).then_inc(w_ready, 1)

            def x_moments(b, rows):
                for n in rows:
                    dve.bn_stats(st6[:, n, :], row(X, b * NT + n))

            def x_variance():
                dve.drain()
                for n in range(NT):
                    dve.bn_aggr(mv[:, n, :], st6[:, n, :])
                dve.drain()
                dve.tensor_scalar(sm[:, 0, :], mv[:, :, 1], 1e-6, None, ALU.add).then_inc(x_stats, 1)

            def norm_square(b):
                dve.wait_ge(x_rstd, b + 1)
                dve.tensor_tensor(sm[:, 2, :], mv[:, :, 1], sm[:, 1, :], ALU.mult)
                dve.drain()
                dve.tensor_tensor(sm[:, 2, :], sm[:, 2, :], sm[:, 1, :], ALU.mult)
                dve.drain()
                dve.tensor_scalar(sm[:, 2, :], sm[:, 2, :], float(C), 1e-24, ALU.mult, ALU.max).then_inc(n2_ready, 1)

            def norm_scale(b):
                dve.wait_ge(n_scale, b * 2 + 2)
                dve.tensor_tensor(sm[:, 4, :], sm[:, 4, :], sm[:, 1, :], ALU.mult)
                dve.tensor_scalar(xneg[:, :], mv[:, :, 0], -1.0, None, ALU.mult)
                dve.drain()
                dve.tensor_tensor(sm[:, 6, :], sm[:, 4, :], xneg[:, :], ALU.mult).then_inc(nf_scale, 1)

            def sums_variance(b):
                dve.drain()
                for n in range(NT):
                    dve.bn_aggr(umv[:, n, :], ust[:, n, :])
                dve.drain()
                dve.tensor_scalar(uvar[:, :], umv[:, :, 1], 1e-5, None, ALU.add)
                dve.tensor_scalar(uneg[:, :], umv[:, :, 0], -1.0, None, ALU.mult).then_inc(u_stats, 1)

            def sums_kept(b):
                dve.wait_ge(u_rstd, b + 1)
                dve.tensor_copy(K["ln_mean"][:, bass.ds(b * NT, NT)], umv[:, :, 0])
                dve.tensor_copy(K["ln_rstd"][:, bass.ds(b * NT, NT)], urstd[:, :])

            def sums_read(b):
                dve.wait_ge(us_full, b + 1)
                dve.tensor_copy(usum[:, :, bass.ds(b, 1)].rearrange("p k o -> p (k o)"),
                                ps[3][:, 0:KC]).then_inc(us_read, 1)

            def out_add(b, n):
                i = n % 2
                dve.wait_ge(y_aff, b * NT + n + 1)
                dve.scalar_tensor_tensor(out=y[:, i, :], in0=y[:, i, :], scalar=0.01, in1=y[:, i, :],
                                         op0=ALU.mult, op1=ALU.max)
                dve.drain()
                dve.tensor_tensor(row(X, b * NT + n), row(X, b * NT + n), y[:, i, :], ALU.add)

            def sums_moments(b, n):
                dve.bn_stats(ust[:, n, :], row(X, b * NT + n))

            def front(b, first):
                for g in range(4):
                    half, k = g // 2, g % 2
                    t0 = slice(half * HALF, (half + 1) * HALF)
                    dve.wait_ge(nf_hi, b * 4 + g + 1)
                    dve.tensor_tensor(nf16[:, 1, k, t0], pa[half][:, k * HALF:(k + 1) * HALF], nf16[:, 0, k, t0],
                                      ALU.subtract).then_inc(nf_lo, 1)
                    if g == 1 and not first:
                        out_add(b - 1, NT - 2)
                        sums_moments(b - 1, NT - 3)
                for i in range(4):
                    half, d = i // 2, i % 2
                    t0 = slice(half * HALF, (half + 1) * HALF)
                    if i == 1 and not first:
                        out_add(b - 1, NT - 1)
                        sums_moments(b - 1, NT - 2)
                    if i == 2 and not first:
                        dve.drain()
                        sums_moments(b - 1, NT - 1)
                    if i == 3 and not first:
                        sums_variance(b - 1)
                    dve.wait_ge(gf_hi, b * 4 + i + 1)
                    dve.tensor_tensor(g16[:, 1, d, t0], ps[i][:, :], g16[:, 0, d, t0],
                                      ALU.subtract).then_inc(gf_lo, 1)
                for n in range(NT + 1):
                    if n < NT:
                        dve.wait_ge(hf_full, b * NT + n + 1)
                        if n >= 3:
                            dve.wait_ge(h_lo, b * NT + n - 2)
                        dve.scalar_tensor_tensor(out=h32[:, n % 3, :], in0=ps[n % 4][:, 0:C], scalar=sm[:, 5, n:n + 1],
                                                 in1=aff_b[:, :], op0=ALU.mult, op1=ALU.add).then_inc(h_ready, 1)
                    if n >= 1:
                        dve.wait_ge(h_hi, b * NT + n)
                        dve.tensor_tensor(h16[:, 1, n - 1, :], h32[:, (n - 1) % 3, :], h16[:, 0, n - 1, :],
                                          ALU.subtract).then_inc(h_lo, 1)
                if not first:
                    sums_kept(b - 1)

            def attention(b, first, last):
                def row_max(n):
                    dve.wait_ge(a_full, b * NT + n + 1)
                    if n >= 2:
                        dve.wait_ge(p_ready, b * NT + n - 1)
                    dve.tensor_reduce(mx[:, n % 2:n % 2 + 1], pa[n % 2][:, :], AX_X, ALU.max)
                    dve.drain()
                    dve.tensor_scalar(nmx[:, n % 2:n % 2 + 1], mx[:, n % 2:n % 2 + 1], -5.0, None,
                                      ALU.mult).then_inc(mx_ready, 1)

                def low_weights(n):
                    for g in range(2):
                        dve.wait_ge(pt_hi, b * 2 * NT + 2 * n + g + 1)
                        dve.tensor_tensor(pt16[:, n % 2, 1, 4 * g:4 * g + 4, :].rearrange("p m t -> p (m t)"),
                                          ps[g][:, :],
                                          pt16[:, n % 2, 0, 4 * g:4 * g + 4, :].rearrange("p m t -> p (m t)"),
                                          ALU.subtract).then_inc(pt_lo, 1)

                def out_stats(n):
                    i = n % 2
                    dve.wait_ge(o_full, b * NT + n + 1)
                    dve.bn_stats(yst[:, i, :], ps[2 + i][:, 0:C])
                    dve.tensor_scalar(ys[:, i, 0:1], ssum[:, i:i + 1], ssum[:, i:i + 1], 1e-5, ALU.mult, ALU.mult)
                    dve.drain()
                    dve.bn_aggr(ymv[:, i, :], yst[:, i, :])
                    dve.drain()
                    dve.tensor_tensor(ys[:, i, 1:2], ymv[:, i, 1:2], ys[:, i, 0:1], ALU.add).then_inc(y_stats, 1)

                def out_norm(n):
                    i = n % 2
                    dve.wait_ge(y_rstd, b * NT + n + 1)
                    dve.tensor_scalar(y[:, i, :], ps[2 + i][:, 0:C], ymv[:, i, 0:1], ys[:, i, 3:4],
                                      ALU.subtract, ALU.mult).then_inc(y_norm, 1)

                row_max(0)
                for n in range(NT):
                    if n + 1 < NT:
                        row_max(n + 1)
                    low_weights(n)
                    if n == 1 and not first:
                        sums_read(b - 1)
                    if not last:
                        if n in (0, 1):
                            x_moments(b + 1, range(4 * n, 4 * n + 4))
                        if n == 2:
                            x_variance()
                        if n == 3:
                            norm_square(b + 1)
                        if n == 5:
                            norm_scale(b + 1)
                    if n >= 1:
                        out_stats(n - 1)
                        if n >= 3:
                            sums_moments(b, n - 3)
                        out_norm(n - 1)
                    if n >= 2:
                        out_add(b, n - 2)
                out_stats(NT - 1)
                out_norm(NT - 1)

            x_moments(0, range(NT))
            x_variance()
            norm_square(0)
            norm_scale(0)
            front(0, True)
            attention(0, True, False)
            with dve.Fori(1, B - 1) as b:
                front(b, False)
                attention(b, False, False)
            front(B - 1, False)
            attention(B - 1, False, True)
            for n in (NT - 2, NT - 1):
                out_add(B - 1, n)
            dve.drain()
            for n in (NT - 3, NT - 2, NT - 1):
                sums_moments(B - 1, n)
            sums_variance(B - 1)
            sums_kept(B - 1)
            sums_read(B - 1)


def block_diagonal(w):
    w = np.asarray(w)
    full = np.zeros((MC, P // 4, 4, P // 4, 4), w.dtype)
    blocks = w.reshape(MC, P // 4, 4, 4)
    for n in range(P // 4):
        full[:, n, :, n, :] = blocks[:, n]
    return full.reshape(MC, P, P).transpose(1, 0, 2)


def arrange(inputs):
    i = {k: np.asarray(v) for k, v in inputs.items()}
    f = np.float32
    c = np.ascontiguousarray
    a = {"x": i["x"].reshape(B * S, C)}
    a["w_up"] = c(i["L0_conv_W_up"].T)
    a["w_down"] = c(i["L0_conv_W_down"].T)
    wq, wk, wv = i["L0_conv_Wq"], i["L0_conv_Wk"], i["L0_conv_Wv"]
    a["blocks"] = c(np.stack([block_diagonal(w) for w in (wq, wk, wv, wv.transpose(0, 2, 1))], axis=1))
    gates = np.zeros((3 * MC, P, 40), f)
    gates[:, :, 0:NH] = i["L0_conv_W_i"].T.reshape(3 * MC, P, NH)
    gates[:, :, 32:32 + NH] = i["L0_conv_W_f"].T.reshape(3 * MC, P, NH)
    a["w_gates"] = c(gates.reshape(3, MC, P, 40).transpose(2, 0, 1, 3))
    gb = np.zeros((40, 1), f)
    gb[0:NH, 0] = i["L0_conv_b_i"]
    gb[32:32 + NH, 0] = i["L0_conv_b_f"]
    a["gate_bias"] = gb
    chan = np.concatenate([i["L0_conv_conv_w"][:, 0, :], i["L0_conv_conv_b"][:, None],
                           i["L0_conv_norm_w"][:, None], i["L0_conv_skip"][:, None]], axis=1)
    a["chan"] = c(chan.reshape(MC, P, PC_N).transpose(1, 0, 2))
    sel = np.zeros((GROW, NH, P), f)
    for slot in range(NH):
        for g in range(3):
            sel[32 * g + slot_head(slot), slot, :] = 1
    a["sel"] = sel
    pair_sel = np.zeros((NH, MC, P), f)
    for h in range(NH):
        pair_sel[h, h // 2, DH * (h % 2):DH * (h % 2) + DH] = 1
    a["pair_sel"] = pair_sel
    later = np.tril(np.ones((P, P)), -1)
    a["negmask"] = np.repeat((later * -1e30)[:, None, :], 4, axis=1).astype(f)
    a["ident"] = np.eye(P, dtype=f)
    a["ones4"] = np.ones((B, P), f)
    a["own"] = np.repeat(np.eye(B, dtype=f)[:, :, None], TOPK, axis=2)
    for layer in range(2):
        src, dst = f"L{layer}_ffn_", f"e{layer}_"
        a[dst + "wr"] = c(i[src + "Wr"].reshape(KC, P, NE).transpose(1, 0, 2))
        a[dst + "w1"], a[dst + "w2"], a[dst + "b2"] = i[src + "W1"], i[src + "W2"], i[src + "b2"]
        a[dst + "b1"] = c(i[src + "b1"].reshape(NE, FC, P).transpose(0, 2, 1))
        for name in ("br", "gamma", "beta"):
            a[dst + name] = i[src + name][None, :]
    a["adj"] = i["L1_conv_adj_w"]
    a["affine"] = c(i["L1_conv_affine_w"].T)
    for name in ("affine_b", "ln_g", "ln_b"):
        a[name] = i["L1_conv_" + name][None, :]
    return a


def kernel(**inputs):
    import concourse.bacc as bacc
    from concourse.bass_utils import run_bass_kernel_spmd as run

    nc = bacc.Bacc("TRN2", target_bir_lowering=False, num_devices=1)
    arrays, aps = {}, {}
    for name, a in arrange(inputs).items():
        arrays["in_" + name] = a
        aps[name] = nc.dram_tensor("in_" + name, a.shape, mybir.dt.from_np(a.dtype), kind="ExternalInput").ap()
    out = nc.dram_tensor("out_0", (B * S, C), F32, kind="ExternalOutput").ap()
    build(nc, aps, out)
    r = run(nc, [arrays], core_ids=[0])
    return r.results[0]["out_0"].reshape(B, S // 32, 32, C)
```

```python
from contextlib import ExitStack, contextmanager

import numpy as np

import concourse.bass as bass
from concourse import mybir

F32 = mybir.dt.float32
F16 = mybir.dt.float16
BF16 = mybir.dt.bfloat16
U32 = mybir.dt.uint32
I32 = mybir.dt.int32
ALU = mybir.AluOpType
ACT = mybir.ActivationFunctionType
AX_X = mybir.AxisListType.X

P = 128
B = 4
S = 1024
C = 256
KC = C // P
NT = S // P
HALF = S // 2
INNER = 512
MC = INNER // P
NH = 8
DH = INNER // NH
TAPS = 4
VW = DH + 1
NE = 8
TOPK = 2
FF = 512
FC = FF // P
CAPACITY = float(-(-B * S * 1.25 // NE))
GROW = 72

FILL_GATES, FILL_PARTS = 20, 12
PC_TAP, PC_CB, PC_NW, PC_SKIP = 0, TAPS, TAPS + 1, TAPS + 2
PC_N = TAPS + 3


def slot_head(slot):
    return 4 * (slot // 4) + 2 * (slot % 2) + (slot // 2) % 2


def row(t, i):
    return t[:, bass.ds(i, 1), :].rearrange("p o f -> p (o f)")


def inverse_root(dve, out, x, t):
    dve.tensor_scalar(t.bitcast(I32), x.bitcast(I32), 1, None, ALU.arith_shift_right)
    dve.drain()
    dve.tensor_scalar(out.bitcast(I32), t.bitcast(I32), -1.0, float(0x5F3759DF), ALU.mult, ALU.add)
    dve.drain()
    for _ in range(3):
        dve.tensor_tensor(t, out, out, ALU.mult)
        dve.drain()
        dve.scalar_tensor_tensor(out=t, in0=t, scalar=-0.5, in1=x, op0=ALU.mult, op1=ALU.mult)
        dve.drain()
        dve.scalar_tensor_tensor(out=out, in0=t, scalar=1.5, in1=out, op0=ALU.add, op1=ALU.mult)
        dve.drain()


def product3(pe, out, a, b, start, stop):
    pe.matmul(out, a[0], b[0], start=start, stop=False)
    pe.matmul(out, a[0], b[1], start=False, stop=False)
    return pe.matmul(out, a[1], b[0], start=False, stop=stop)


@contextmanager
def cleared(nc, sems):
    yield
    with nc.Block() as block:
        @block.sync
        def _(sp):
            for s in sems:
                sp.sem_clear(s)


def mixer0(nc, X, K, A, usum):
    sems = []
    with ExitStack() as ctx, cleared(nc, sems), ExitStack() as stage:
        def sb(name, shape, dt=F32):
            return ctx.enter_context(nc.sbuf_tensor("m0_" + name, shape, dt))

        def sem(name):
            sems.append(ctx.enter_context(nc.semaphore(name)))
            return sems[-1]

        ps = [ctx.enter_context(nc.psum_tensor(f"m0_ps{i}", [P, HALF], F32)) for i in range(8)]

        wup = sb("wup", [P, 2, KC, 2 * INNER], F16)
        wdn = sb("wdn", [P, 2, MC, C], F16)
        gk = sb("gk", [P, 2, MC, P], F16)
        wv = sb("wv", [P, 2, MC, P], F16)
        ga = sb("ga", [P, 2, MC, 40], F16)
        gv = sb("gv", [P, 2, MC, 40], F16)
        pc = sb("pc", [P, MC, PC_N])
        gb = sb("gb", [40, 1])
        sel = sb("sel", [GROW, NH, P], BF16)
        pair_sel = sb("pair_sel", [NH, MC, P])
        negmask = sb("negmask", [P, 4, P], BF16)
        ident16 = sb("ident16", [P, P], BF16)
        region_a = sb("region_a", [P, NT * NH * VW])
        region_b = sb("region_b", [P, MC * S])
        sz = sb("sz", [P, MC, S])
        xa = sb("xa", [P, MC, S])
        region_e = sb("region_e", [P, MC * S])
        region_f = sb("region_f", [P, MC * S])
        vext = sb("vext", [P, NT, NH * VW])
        region_h = sb("region_h", [P, NT * C])
        kt = sb("kt", [P, 2, 4 * DH])
        tmp = sb("tmp", [P, 4 * VW])
        state = sb("state", [P, MC, 2 * VW])
        stack = sb("stack", [P, S])
        part_a = sb("part_a", [GROW, S], BF16)
        part_n = sb("part_n", [GROW, S], BF16)
        sq_buf = sb("sq_buf", [P, S])
        cols = sb("cols", [P, NT, GROW])
        dec_row = sb("dec_row", [NH, NT])
        dec = sb("dec", [P, MC, NT])
        st6 = sb("st6", [P, NT, 6])
        mv = sb("mv", [P, NT, 2])
        rstd = sb("rstd", [P, NT])
        lnv = sb("lnv", [P, NT])
        xbias, ust, umv = sb("xbias", [P, NT]), sb("ust", [P, NT, 6]), sb("umv", [P, NT, 2])
        uvar, urstd, xneg = sb("uvar", [P, NT]), sb("urstd", [P, NT]), sb("xneg", [P, NT])
        sm = sb("sm", [P, 5, NT * NH])

        XW = TAPS - 1 + S
        xm32 = region_a[:, 0:MC * XW].rearrange("p (m t) -> p m t", m=MC)
        rows_a = region_a[0:NH, 0:4 * S].rearrange("p (r t) -> p r t", r=4)
        num = region_a[:, :].rearrange("p (n w) -> p n w", n=NT)
        num4 = region_a[:, :].rearrange("p (n v) -> p n v", v=VW)
        b16 = region_b[:, :].bitcast(F16).rearrange("p (a m t) -> p a m t", a=2, m=MC)
        ktok = region_b[:, :].rearrange("p (n c) -> p n c", n=NT)
        heads = region_b[:, :].rearrange("p (n d) -> p n d", d=DH)
        xa16 = region_e[:, :].bitcast(F16).rearrange("p (a m t) -> p a m t", a=2, m=MC)
        xn = region_f[:, KC * S:].rearrange("p (n c) -> p n c", n=NT)
        xn16 = region_f[:, 0:KC * S].bitcast(F16).rearrange("p (a k t) -> p a k t", a=2, k=KC)
        kf16 = region_f[:, :].bitcast(F16).rearrange("p (a m t) -> p a m t", a=2, m=MC)
        un = region_h[:, :].rearrange("p (n c) -> p n c", n=NT)
        args = region_h[0:GROW, 0:S]
        rest_a = region_h[32:32 + NH, S:2 * S]
        dbuf = region_h[:, 0:2 * HALF].rearrange("p (r t) -> p r t", r=2)
        pbuf = region_h[:, 2 * HALF:4 * HALF].rearrange("p (r t) -> p r t", r=2)
        hbuf = region_h[:, :].rearrange("p (r t) -> p r t", r=4)
        kf32 = sq_buf[:, :].rearrange("p (i t) -> p i t", i=2)
        rest_n = sq_buf[32:32 + NH, :]
        sq = sq_buf[:, :].rearrange("p (n d) -> p n d", d=DH)
        s_wup = xa[:, :, :].rearrange("p m t -> p (m t)")[:, 0:KC * 2 * INNER].rearrange("p (k n) -> p k n", k=KC)
        s_wdn = sz[:, 0, :].rearrange("p (m n) -> p m n", m=MC)
        s_blk = region_b[:, 0:4 * MC * P].rearrange("p (w m c) -> p w m c", w=4, m=MC)
        s_sel = region_f[0:GROW, 0:NH * P].rearrange("p (h t) -> p h t", h=NH)
        s_neg = region_f[:, NH * P:NH * P + 4 * P].rearrange("p (h t) -> p h t", h=4)
        s_wg = region_e[:, 0:3 * MC * 40].rearrange("p (w m c) -> p w m c", w=3, m=MC)

        w_in, blk_in, small_in = sem("m0_w_in"), sem("m0_blk_in"), sem("m0_small_in")
        fold_full, fold_hi, w_hi, w_ready = sem("m0_fold_full"), sem("m0_fold_hi"), sem("m0_w_hi"), sem("m0_w_ready")
        init_done, wv_centred = sem("m0_init_done"), sem("m0_wv_centred")
        x_in, x_stats, x_rstd = sem("m0_x_in"), sem("m0_x_stats"), sem("m0_x_rstd")
        xn_ready, xt_full, xt_hi, xt_lo = sem("m0_xn"), sem("m0_xt_full"), sem("m0_xt_hi"), sem("m0_xt_lo")
        up_full, up_act, up_lo = sem("m0_up_full"), sem("m0_up_act"), sem("m0_up_lo")
        conv_init, conv_done = sem("m0_conv_init"), sem("m0_conv_done")
        xa_hi, xa_lo = sem("m0_xa_hi"), sem("m0_xa_lo")
        gates_full, gates_read = sem("m0_gates_full"), sem("m0_gates_read")
        gate_abs, gate_log, gate_scan = sem("m0_gate_abs"), sem("m0_gate_log"), sem("m0_gate_scan")
        gate_args, gate_exp, hi_ready = sem("m0_gate_args"), sem("m0_gate_exp"), sem("m0_hi")
        parts_ready = sem("m0_parts")
        v_full, v_read = sem("m0_v_full"), sem("m0_v_read")
        kf_full, kf_hi, kf_lo = sem("m0_kf_full"), sem("m0_kf_hi"), sem("m0_kf_lo")
        kt_full, kt_read = sem("m0_kt_full"), sem("m0_kt_read")
        cols_full, cols_ready = sem("m0_cols_full"), sem("m0_cols")
        s_full, d_full, d_ready, p_ready = sem("m0_s_full"), sem("m0_d_full"), sem("m0_d"), sem("m0_p")
        kw_ready, av_full, comb_done = sem("m0_kw"), sem("m0_av_full"), sem("m0_comb")
        st_full, decayed, st_done = sem("m0_st_full"), sem("m0_decayed"), sem("m0_st")
        sq_ready = sem("m0_sq")
        var_ready, hn_ready, hn_last, skx_ready = sem("m0_var"), sem("m0_hn"), sem("m0_hn_last"), sem("m0_skx")
        ht_full, pre_ready, h32_ready = sem("m0_ht_full"), sem("m0_pre"), sem("m0_h32")
        h_hi, h_lo, dn_full, x_added = sem("m0_h_hi"), sem("m0_h_lo"), sem("m0_dn_full"), sem("m0_x_added")
        u_stats, u_rstd, u_added = sem("m0_u_stats"), sem("m0_u_rstd"), sem("m0_u_added")
        us_full, us_read, un_ready = sem("m0_us_full"), sem("m0_us_read"), sem("m0_un")

        UP = [(h, m) for part in (0, MC) for h in range(2) for m in range(part, part + MC)]
        NP = NT // 2
        PW = 2 * NH
        NQ = 2 * NT
        NS = NQ - 2

        def unit_cols(q):
            return q // 2, q % 2

        def gate_unit(g):
            return 2 * (g % 2), slice(g // 2 * 2 * P, (g // 2 + 1) * 2 * P)

        def gated(g):
            return hbuf[:, g % 4, :].rearrange("p (m t) -> p m t", m=2)

        block = stage.enter_context(nc.Block())

        @block.sync
        def _(sp):
            def load_batch(b):
                sp.dma_start(X[:, b * NT:(b + 1) * NT, :],
                             A["x"][b * S:(b + 1) * S, :].rearrange("(n p) c -> p n c", p=P)).then_inc(x_in, 16)

            load_batch(0)
            sp.dma_start(s_blk, A["blocks"]).then_inc(blk_in, 16)
            sp.dma_start(s_wg, A["w_gates"]).then_inc(blk_in, 16)
            sp.dma_start(s_wup, A["w_up"].rearrange("(k p) n -> p k n", p=P)).then_inc(w_in, 16)
            sp.dma_start(s_wdn, A["w_down"].rearrange("(m p) n -> p m n", p=P)).then_inc(w_in, 16)
            sp.dma_start(pc[:, :, :], A["chan"]).then_inc(small_in, 16)
            sp.dma_start(gb[:, :], A["gate_bias"]).then_inc(small_in, 16)
            sp.dma_start(s_sel, A["sel"]).then_inc(small_in, 16)
            sp.dma_start(pair_sel[:, :, :], A["pair_sel"]).then_inc(small_in, 16)
            sp.dma_start(s_neg, A["negmask"]).then_inc(small_in, 16)
            for b in range(1, B):
                sp.wait_ge(x_in, b * 16)
                load_batch(b)
            sp.wait_ge(x_in, B * 16)

        @block.tensor
        def _(pe):
            pe.wait_ge(K["ident_in"], 16)
            pe.wait_ge(blk_in, 32)
            for m in range(MC):
                pe.matmul(ps[0][:, m * P:(m + 1) * P], s_blk[:, 1, m, :], s_blk[:, 0, m, :], start=True, stop=True)
            for m in range(MC):
                o = ps[1][:, m * 40:(m + 1) * 40]
                pe.matmul(o, s_blk[:, 0, m, :], s_wg[:, 0, m, :], start=True, stop=False)
                pe.matmul(o, s_blk[:, 1, m, :], s_wg[:, 1, m, :], start=False, stop=True)
            for m in range(MC):
                last = pe.matmul(ps[2][:, m * 40:(m + 1) * 40], s_blk[:, 2, m, :], s_wg[:, 2, m, :],
                                 start=True, stop=True)
            last.then_inc(fold_full, 1)
            pe.wait_ge(w_ready, 1)
            pe.wait_ge(small_in, 80)

            def sums(b):
                pe.wait_ge(u_added, b * 3 + 3)
                for k in range(KC):
                    t = pe.matmul(ps[7][:, k:k + 1], un[:, 0, k * P:(k + 1) * P], K["ones"], start=True, stop=True)
                t.then_inc(us_full, 1)

            def keep_clock(bank, count):
                for _ in range(count):
                    pe.matmul(bank[:, :], wup[:, 0, 0, 0:P], wup[:, 0, 0, 0:HALF], start=True, stop=True)

            def turn_front(b, first):
                for g in range(4):
                    half, k = g // 2, g % 2
                    pe.wait_ge(xn_ready, b * NT + 4 * half + 4)
                    if not first:
                        pe.wait_ge(x_added, b * NT - NT + g + 1)
                    for j in range(4):
                        t = pe.transpose(ps[g][:, j * P:(j + 1) * P], xn[:, 4 * half + j, k * P:(k + 1) * P],
                                         K["ident"])
                    t.then_inc(xt_full, 1)

            def batch(b, first, last):
                for u, (half, m) in enumerate(UP):
                    if u % 4 == 0:
                        pe.wait_ge(xt_lo, b * 4 + (2 * half + 2 if u == 0 else 4))
                    if u < 4 and not first:
                        pe.wait_ge(x_added, b * NT - NT + 4 + u + 1)
                    if u >= 8:
                        pe.wait_ge(up_act, b * 16 + u - 7)
                        pe.wait_ge(up_lo, b * 8 + u - 7)
                    for k in range(KC):
                        t = product3(pe, ps[(4 + u) % 8][:, :],
                                     [wup[:, a, k, m * P:(m + 1) * P] for a in (0, 1)],
                                     [xn16[:, a, k, half * HALF:(half + 1) * HALF] for a in (0, 1)],
                                     k == 0, k == KC - 1)
                    t.then_inc(up_full, 1)
                pe.wait_ge(up_act, b * 16 + 16)
                for half in range(2):
                    t0 = slice(half * HALF, (half + 1) * HALF)
                    for m in range(MC):
                        product3(pe, ps[half][0:40, :], [gv[:, a, m, :] for a in (0, 1)],
                                 [b16[:, a, m, t0] for a in (0, 1)], m == 0, False)
                for n in range(NT):
                    if n >= 6:
                        pe.wait_ge(v_read, b * NT + n - 5)
                    for m in range(MC):
                        t = product3(pe, ps[2 + n % 6][:, m * P:(m + 1) * P],
                                     [b16[:, a, m, n * P:(n + 1) * P] for a in (0, 1)],
                                     [wv[:, a, m, :] for a in (0, 1)], True, True)
                    t.then_inc(v_full, 1)
                for m in range(MC):
                    pe.wait_ge(xa_lo, b * MC + m + 1)
                    for half in range(2):
                        t0 = slice(half * HALF, (half + 1) * HALF)
                        t = product3(pe, ps[half][0:40, :], [ga[:, a, m, :] for a in (0, 1)],
                                     [xa16[:, a, m, t0] for a in (0, 1)], False, m == MC - 1)
                        if m == MC - 1:
                            t.then_inc(gates_full, 1)
                pe.wait_ge(v_read, b * NT + NT)
                if not first:
                    sums(b - 1)
                for j in range(8):
                    m, half = j // 2, j % 2
                    if j == 5 and not first:
                        pe.wait_ge(us_read, b)
                    if j >= 6:
                        pe.wait_ge(gates_read, b * 2 + j - 5)
                    t = product3(pe, ps[(2 + j) % 8][:, :], [gk[:, a, m, :] for a in (0, 1)],
                                 [xa16[:, a, m, half * HALF:(half + 1) * HALF] for a in (0, 1)], True, True)
                    t.then_inc(kf_full, 1)
                for n in range(NT):
                    pe.wait_ge(kf_lo, b * 8 + n + 1)
                    for m in range(MC):
                        t = product3(pe, ps[(2 + n) % 8][:, m * P:(m + 1) * P],
                                     [xa16[:, a, m, n * P:(n + 1) * P] for a in (0, 1)],
                                     [gk[:, a, m, :] for a in (0, 1)], True, True)
                    t.then_inc(kt_full, 1)
                pe.wait_ge(kt_read, b * NT + 1)
                keep_clock(ps[2], FILL_GATES)
                pe.wait_ge(kt_read, b * NT + 3)
                pe.wait_ge(gate_exp, b * 2 + 2)
                for g in range(2):
                    for j in range(4):
                        n = 4 * g + j
                        t = pe.transpose(ps[2 + g][:, j * P:j * P + GROW], stack[0:GROW, n * P:(n + 1) * P],
                                         K["ident"][0:GROW, 0:GROW])
                    t.then_inc(cols_full, 1)
                for m in range(MC):
                    t = pe.matmul(ps[4][:, m * NT:(m + 1) * NT], pair_sel[:, m, :], dec_row[:, :],
                                  start=True, stop=True)
                t.then_inc(cols_full, 1)
                pe.wait_ge(kt_read, b * NT + NT)
                keep_clock(ps[5], FILL_PARTS)
                pe.wait_ge(parts_ready, b * 2 + 2)
                pe.wait_ge(cols_ready, b * 3 + 3)

                def scores(q):
                    c, hf = unit_cols(q)
                    t0 = slice(c * P, (c + 1) * P)
                    if q >= 2:
                        pe.wait_ge(p_ready, b * NQ + q - 1)
                    for pr in range(2):
                        for par in range(2):
                            rows = slice(64 * par, 64 * par + 64)
                            m = 2 * hf + pr
                            t = product3(pe, ps[2 * (q % 2) + par][:, pr * P:(pr + 1) * P],
                                         [kf16[rows, a, m, t0] for a in (0, 1)],
                                         [xa16[rows, a, m, t0] for a in (0, 1)], True, True)
                    t.then_inc(s_full, 1)

                def log_weights(q):
                    c, hf = unit_cols(q)
                    t0 = slice(c * P, (c + 1) * P)
                    if q >= 1:
                        pe.wait_ge(d_ready, b * NQ + q)
                    pe.matmul(ps[4][:, :], ident16[:, :], negmask[:, :, :].rearrange("p h t -> p (h t)"),
                              start=True, stop=False)
                    pe.matmul(ps[4][:, :], part_a[:, t0],
                              sel[:, 4 * hf:4 * hf + 4, :].rearrange("p h t -> p (h t)"), start=False, stop=False)
                    for s in range(4):
                        t = pe.matmul(ps[4][:, s * P:(s + 1) * P], sel[:, 4 * hf + s, :], part_n[:, t0],
                                      start=False, stop=(s == 3))
                    t.then_inc(d_full, 1)

                scores(0)
                log_weights(0)
                for q in range(NQ):
                    c, hf = unit_cols(q)
                    t0 = slice(c * P, (c + 1) * P)
                    if q + 1 < NQ:
                        scores(q + 1)
                        log_weights(q + 1)
                    pe.wait_ge(p_ready, b * NQ + q + 1)
                    if q >= 1:
                        pe.wait_ge(comb_done, b * NQ + q)
                    for s in range(4):
                        h = slot_head(4 * hf + s)
                        t = pe.matmul(ps[5][:, (h % 4) * VW:(h % 4 + 1) * VW], pbuf[:, q % 2, s * P:(s + 1) * P],
                                      vext[:, c, h * VW:(h + 1) * VW], start=True, stop=True)
                    if c > 0:
                        pe.wait_ge(st_done, b * NS + q - 1)
                        for pr in range(2):
                            t = pe.matmul(ps[6][:, pr * 2 * VW:(pr + 1) * 2 * VW], xa[:, 2 * hf + pr, t0],
                                          state[:, 2 * hf + pr, :], start=True, stop=True)
                    t.then_inc(av_full, 1)
                    if c < NT - 1:
                        pe.wait_ge(kw_ready, b * NS + q + 1)
                        if q >= 1:
                            pe.wait_ge(st_done, b * NS + q)
                        for pr in range(2):
                            m = 2 * hf + pr
                            t = pe.matmul(ps[7][:, pr * 2 * VW:(pr + 1) * 2 * VW], kt[:, q % 2, pr * P:(pr + 1) * P],
                                          vext[:, c, m * 2 * VW:(m + 1) * 2 * VW], start=True, stop=True)
                        t.then_inc(st_full, 1)

                def turn(p):
                    if p < NP - 1:
                        pe.wait_ge(hn_ready, b * 3 + p + 1)
                    else:
                        pe.wait_ge(hn_last, b + 1)
                    if p == 2:
                        pe.wait_ge(comb_done, b * NQ + NQ)
                    for g in (2 * p, 2 * p + 1):
                        for i in range(4):
                            m, j = 2 * (g % 2) + i // 2, i % 2
                            t = pe.transpose(ps[g][:, i * P:(i + 1) * P], ktok[:, 2 * p + j, m * P:(m + 1) * P],
                                             K["ident"])
                        t.then_inc(ht_full, 1)

                def down(p):
                    pe.wait_ge(h_lo, b * 8 + 2 * p + 2)
                    for n in (2 * p, 2 * p + 1):
                        for m in range(MC):
                            t = product3(pe, ps[n][:, 0:C], [xa16[:, a, m, n * P:(n + 1) * P] for a in (0, 1)],
                                         [wdn[:, a, m, :] for a in (0, 1)], m == 0, m == MC - 1)
                        t.then_inc(dn_full, 1)

                turn(0)
                turn(1)
                turn(2)
                down(0)
                down(1)
                turn(3)
                down(2)
                if not last:
                    turn_front(b + 1, False)
                down(3)

            turn_front(0, True)
            batch(0, True, False)
            with pe.Fori(1, B - 1) as b:
                batch(b, False, False)
            batch(B - 1, False, True)
            pe.wait_ge(un_ready, 1)
            for k in range(KC):
                for n in range(NT):
                    t = pe.matmul(ps[7][:, k:k + 1], un[:, n, k * P:(k + 1) * P], K["ones"],
                                  start=(n == 0), stop=(n == NT - 1))
            t.then_inc(us_full, 1)

        @block.scalar
        def _(act):
            def normalise(b, n):
                act.activation(xn[:, n, :], row(X, b * NT + n), ACT.Identity, scale=rstd[:, n:n + 1],
                               bias=xbias[:, n:n + 1]).then_inc(xn_ready, 1)

            def high_front(b):
                for g in range(4):
                    half, k = g // 2, g % 2
                    act.wait_ge(xt_full, b * 4 + g + 1)
                    act.activation(xn16[:, 0, k, half * HALF:(half + 1) * HALF], ps[g][:, :],
                                   ACT.Identity).then_inc(xt_hi, 1)

            def batch(b, last):
                def silu_pair(i):
                    for m in (2 * i, 2 * i + 1):
                        act.wait_ge(conv_done, b * MC + m + 1)
                        act.activation(xa16[:, 0, m, :], xa[:, m, :], ACT.Silu)
                    act.drain()
                    for m in (2 * i, 2 * i + 1):
                        act.activation(xa[:, m, :], xa[:, m, :], ACT.Silu).then_inc(xa_hi, 1)

                for u, (half, m) in enumerate(UP):
                    src = ps[(4 + u) % 8][:, :]
                    t0 = slice(half * HALF, (half + 1) * HALF)
                    act.wait_ge(up_full, b * 16 + u + 1)
                    if m < MC:
                        act.activation(xm32[:, m, TAPS - 1 + half * HALF:TAPS - 1 + (half + 1) * HALF], src,
                                       ACT.Identity)
                        if m < 2:
                            t = act.activation(xa[:, m, t0], src, ACT.Identity, bias=pc[:, m, PC_CB:PC_CB + 1],
                                               scale=pc[:, m, TAPS - 1:TAPS])
                            if half == 1:
                                t.then_inc(conv_init, 1)
                        act.activation(b16[:, 0, m, t0], src, ACT.Identity).then_inc(up_act, 1)
                    else:
                        act.activation(sz[:, m - MC, t0], src, ACT.Silu).then_inc(up_act, 1)
                    if u == 8:
                        act.drain()
                        for i in (2, 3):
                            act.activation(xa[:, i, :], xm32[:, i, TAPS - 1:TAPS - 1 + S], ACT.Identity,
                                           bias=pc[:, i, PC_CB:PC_CB + 1],
                                           scale=pc[:, i, TAPS - 1:TAPS]).then_inc(conv_init, 1)
                silu_pair(0)
                silu_pair(1)
                for n in range(NT):
                    act.wait_ge(v_full, b * NT + n + 1)
                    act.activation(vext[:, n, :].rearrange("p (h v) -> p h v", v=VW)[:, :, 0:DH],
                                   ps[2 + n % 6][:, :].rearrange("p (h v) -> p h v", v=DH),
                                   ACT.Identity).then_inc(v_read, 1)

                def keys_high(j):
                    m, half = j // 2, j % 2
                    act.wait_ge(kf_full, b * 8 + j + 1)
                    act.activation(kf16[:, 0, m, half * HALF:(half + 1) * HALF], ps[(2 + j) % 8][:, :],
                                   ACT.Identity)
                    if j >= 2:
                        act.wait_ge(kf_lo, b * 8 + j - 1)
                    act.activation(kf32[:, j % 2, :], ps[(2 + j) % 8][:, :], ACT.Identity).then_inc(kf_hi, 1)

                for j in range(2):
                    keys_high(j)
                act.wait_ge(gate_abs, b + 1)
                act.activation(rows_a[:, 1, :], rows_a[:, 1, :], ACT.Exp)
                act.drain()
                act.activation(rows_a[:, 1, :], rows_a[:, 1, :], ACT.Ln,
                               bias=K["ones"][0:NH, :]).then_inc(gate_log, 1)
                for j in range(2, 8):
                    keys_high(j)
                act.wait_ge(gate_scan, b * 2 + 1)
                act.activation(part_a[0:NH, :], rows_a[:, 3, :], ACT.Identity).then_inc(hi_ready, 1)
                act.wait_ge(gate_scan, b * 2 + 2)
                act.activation(part_n[0:NH, :], rows_a[:, 0, :], ACT.Identity, scale=-1.0).then_inc(hi_ready, 1)

                def keys_tokens(n):
                    act.wait_ge(kt_full, b * NT + n + 1)
                    act.activation(ktok[:, n, :], ps[(2 + n) % 8][:, :], ACT.Identity).then_inc(kt_read, 1)

                for n in range(4):
                    keys_tokens(n)
                act.wait_ge(gate_args, b + 1)
                act.activation(stack[0:GROW, :], args, ACT.Exp).then_inc(gate_exp, 1)
                act.activation(dec_row[:, :], dec_row[:, :], ACT.Exp).then_inc(gate_exp, 1)
                for n in range(4, NT):
                    keys_tokens(n)

                def skip_half(half):
                    act.wait_ge(av_full, b * NQ + (half + 1) * NT)
                    for m in range(MC):
                        x = xa[:, m, half * HALF:(half + 1) * HALF]
                        t = act.activation(x, x, ACT.Identity, scale=pc[:, m, PC_SKIP:PC_SKIP + 1])
                    t.then_inc(skx_ready, 1)

                def decay(q):
                    c, hf = unit_cols(q)
                    act.wait_ge(av_full, b * NQ + q + 1)
                    for m in (2 * hf, 2 * hf + 1):
                        t = act.activation(state[:, m, :], state[:, m, :], ACT.Identity, scale=dec[:, m, c:c + 1])
                    t.then_inc(decayed, 1)

                def squares(p):
                    act.wait_ge(comb_done, b * NQ + 4 * p + 4)
                    act.activation(sq, num4[:, p * PW:(p + 1) * PW, 0:DH], ACT.Square).then_inc(sq_ready, 1)

                for q in range(NQ):
                    act.wait_ge(d_full, b * NQ + q + 1)
                    if q >= 2:
                        act.wait_ge(p_ready, b * NQ + q - 1)
                    else:
                        act.wait_ge(cols_ready, b * 3 + 3)
                    act.activation(dbuf[:, q % 2, :], ps[4][:, :], ACT.Exp).then_inc(d_ready, 1)
                    if 3 <= q <= NS:
                        decay(q - 1)
                    if q in (5, 9, 13):
                        squares(q // 4 - 1)
                    if q == 11:
                        skip_half(0)
                squares(NP - 1)
                skip_half(1)
                for g in range(8):
                    m, t0 = gate_unit(g)
                    act.wait_ge(h32_ready, b * 8 + g + 1)
                    act.activation(xa16[:, 0, m:m + 2, t0], gated(g), ACT.Identity).then_inc(h_hi, 1)
                    if g < 4 and not last:
                        if g == 0:
                            act.wait_ge(x_rstd, b + 2)
                        normalise(b + 1, 2 * g)
                        normalise(b + 1, 2 * g + 1)
                if not last:
                    high_front(b + 1)

            act.wait_ge(x_rstd, 1)
            for n in range(NT):
                normalise(0, n)
            act.wait_ge(w_in, 32)
            act.activation(wup[:, 0, :, :], s_wup, ACT.Identity)
            act.activation(wdn[:, 0, :, :], s_wdn, ACT.Identity)
            act.wait_ge(blk_in, 32)
            act.wait_ge(wv_centred, 1)
            act.activation(wv[:, 0, :, :], s_blk[:, 3, :, :], ACT.Identity).then_inc(w_hi, 1)
            act.wait_ge(fold_full, 1)
            act.activation(gk[:, 0, :, :].rearrange("p m c -> p (m c)"), ps[0][:, :], ACT.Identity, scale=DH ** -0.5)
            act.activation(ga[:, 0, :, :].rearrange("p m c -> p (m c)"), ps[1][:, 0:MC * 40], ACT.Identity)
            act.activation(gv[:, 0, :, :].rearrange("p m c -> p (m c)"), ps[2][:, 0:MC * 40],
                           ACT.Identity).then_inc(fold_hi, 1)
            act.wait_ge(small_in, 80)
            act.activation(sel[:, :, :], s_sel, ACT.Identity)
            act.activation(negmask[:, :, :], s_neg, ACT.Identity)
            act.wait_ge(K["ident_in"], 16)
            act.activation(ident16[:, :], K["ident"], ACT.Identity)
            act.drain()
            act.wait_ge(init_done, 1)
            high_front(0)
            with act.Fori(0, B - 1) as b:
                batch(b, False)
            batch(B - 1, True)

        @block.gpsimd
        def _(pool):
            pool.memset(stack[:, :], 0.0)
            pool.memset(part_a[:, :], 0.0)
            pool.memset(part_n[:, :], 0.0)
            pool.memset(state[:, :, :], 0.0)
            pool.memset(vext[:, :, :], 1.0)
            pool.drain().then_inc(init_done, 1)

            def x_root(b):
                pool.wait_ge(x_stats, b + 1)
                pool.tensor_tensor(rstd[:, :], lnv[:, :], K["neg_half"], ALU.pow)
                pool.drain()
                pool.tensor_tensor(xbias[:, :], xneg[:, :], rstd[:, :], ALU.mult).then_inc(x_rstd, 1)

            def sums_add(b):
                pool.wait_ge(u_stats, b + 1)
                pool.tensor_tensor(urstd[:, :], uvar[:, :], K["neg_half"], ALU.pow).then_inc(u_rstd, 1)
                pool.drain()
                for h in (0, 4):
                    pool.tensor_tensor(un[:, h:h + 4, :], X[:, bass.ds(b * NT + h, 4), :],
                                       umv[:, h:h + 4, 0].unsqueeze(2).broadcast_to([P, 4, C]), ALU.subtract)
                pool.drain()
                for h in (0, 4):
                    pool.tensor_tensor(un[:, h:h + 4, :], un[:, h:h + 4, :],
                                       urstd[:, h:h + 4].unsqueeze(2).broadcast_to([P, 4, C]), ALU.mult)
                pool.drain()
                for h in (4, 2, 1):
                    pool.tensor_tensor(un[:, 0:h, :], un[:, 0:h, :], un[:, h:2 * h, :], ALU.add).then_inc(u_added, 1)
                    pool.drain()

            def batch(b, first, last):
                if not first:
                    sums_add(b - 1)

                def keys(q):
                    c, hf = unit_cols(q)
                    if q >= 2:
                        pool.wait_ge(st_full, b * NS + q - 1)
                    pool.tensor_tensor(kt[:, q % 2, :].rearrange("p (h d) -> p h d", h=4),
                                       ktok[:, c, hf * 4 * DH:(hf + 1) * 4 * DH].rearrange("p (h d) -> p h d", h=4),
                                       cols[:, c, 64 + 4 * hf:68 + 4 * hf].unsqueeze(2).broadcast_to([P, 4, DH]),
                                       ALU.mult).then_inc(kw_ready, 1)

                def scale(p):
                    pool.wait_ge(var_ready, b * 3 + p + 1)
                    pool.tensor_tensor(sm[:, 3, p * PW:(p + 1) * PW], sm[:, 2, p * PW:(p + 1) * PW],
                                       K["neg_half"][:, 0:1].broadcast_to([P, PW]), ALU.pow)
                    pool.drain()
                    pool.tensor_tensor(heads[:, p * PW:(p + 1) * PW, :], num4[:, p * PW:(p + 1) * PW, 0:DH],
                                       sm[:, 3, p * PW:(p + 1) * PW].unsqueeze(2).broadcast_to([P, PW, DH]),
                                       ALU.mult).then_inc(hn_ready, 1)

                for j in range(8):
                    m, half = j // 2, j % 2
                    t0 = slice(half * HALF, (half + 1) * HALF)
                    pool.wait_ge(kf_hi, b * 8 + j + 1)
                    pool.tensor_tensor(kf16[:, 1, m, t0], kf32[:, j % 2, :], kf16[:, 0, m, t0],
                                       ALU.subtract).then_inc(kf_lo, 1)
                pool.wait_ge(kt_read, b * NT + NT)
                pool.wait_ge(cols_ready, b * 3 + 3)
                for q in range(NS):
                    keys(q)
                    if q in (7, 11):
                        scale(q // 4 - 1)
                    if q == 10 and not last:
                        x_root(b + 1)
                scale(NP - 2)
                for g in range(8):
                    m, t0 = gate_unit(g)
                    pool.wait_ge(pre_ready, b * 8 + g + 1)
                    pool.tensor_tensor(gated(g), gated(g), sz[:, m:m + 2, t0], ALU.mult).then_inc(h32_ready, 1)

            x_root(0)
            batch(0, True, False)
            with pool.Fori(1, B - 1) as b:
                batch(b, False, False)
            batch(B - 1, False, True)
            pool.wait_ge(u_stats, B)
            pool.tensor_tensor(urstd[:, :], uvar[:, :], K["neg_half"], ALU.pow).then_inc(u_rstd, 1)

        @block.vector
        def _(dve):
            def x_moments(b, n):
                dve.bn_stats(st6[:, n, :], row(X, b * NT + n))

            def x_variance():
                dve.drain()
                for n in range(NT):
                    dve.bn_aggr(mv[:, n, :], st6[:, n, :])
                dve.drain()
                dve.tensor_scalar(lnv[:, :], mv[:, :, 1], 1e-6, None, ALU.add)
                dve.tensor_scalar(xneg[:, :], mv[:, :, 0], -1.0, None, ALU.mult).then_inc(x_stats, 1)

            def sums_moments(b, n):
                dve.bn_stats(ust[:, n, :], row(X, b * NT + n))

            def sums_variance():
                dve.drain()
                for n in range(NT):
                    dve.bn_aggr(umv[:, n, :], ust[:, n, :])
                dve.drain()
                dve.tensor_scalar(uvar[:, :], umv[:, :, 1], 1e-5, None, ALU.add).then_inc(u_stats, 1)

            def sums_kept(b):
                dve.wait_ge(u_rstd, b + 1)
                dve.tensor_copy(K["ln_mean"][:, bass.ds(b * NT, NT)], umv[:, :, 0])
                dve.tensor_copy(K["ln_rstd"][:, bass.ds(b * NT, NT)], urstd[:, :])

            def sums_read(b):
                dve.wait_ge(us_full, b + 1)
                dve.tensor_copy(usum[:, :, bass.ds(b, 1)].rearrange("p k o -> p (k o)"),
                                ps[7][:, 0:KC]).then_inc(us_read, 1)

            def low_front(b):
                for g in range(4):
                    half, k = g // 2, g % 2
                    t0 = slice(half * HALF, (half + 1) * HALF)
                    dve.wait_ge(xt_hi, b * 4 + g + 1)
                    dve.tensor_tensor(xn16[:, 1, k, t0], ps[g][:, :], xn16[:, 0, k, t0],
                                      ALU.subtract).then_inc(xt_lo, 1)

            def batch(b, first, last):
                for m in range(MC):
                    dve.memset(xm32[:, m, 0:TAPS - 1], 0.0)
                for u in range(8):
                    half, m = UP[u]
                    t0 = slice(half * HALF, (half + 1) * HALF)
                    dve.wait_ge(up_act, b * 16 + u + 1)
                    dve.tensor_tensor(b16[:, 1, m, t0], ps[(4 + u) % 8][:, :], b16[:, 0, m, t0],
                                      ALU.subtract).then_inc(up_lo, 1)
                    if not first:
                        sums_moments(b - 1, u)

                def low_act(m):
                    dve.wait_ge(xa_hi, b * MC + m + 1)
                    dve.tensor_tensor(xa16[:, 1, m, :], xa[:, m, :], xa16[:, 0, m, :],
                                      ALU.subtract).then_inc(xa_lo, 1)

                for i in range(2):
                    for j in range(TAPS - 1):
                        if i == 1 and j == 0 and not first:
                            sums_variance()
                        dve.drain()
                        for m in (2 * i, 2 * i + 1):
                            if j == 0:
                                dve.wait_ge(conv_init, b * MC + m + 1)
                            t = dve.scalar_tensor_tensor(out=xa[:, m, :], in0=xm32[:, m, j:j + S],
                                                         scalar=pc[:, m, j:j + 1], in1=xa[:, m, :],
                                                         op0=ALU.mult, op1=ALU.add)
                            if j == TAPS - 2:
                                t.then_inc(conv_done, 1)
                        if i == 1 and j >= 1:
                            low_act(j - 1)
                low_act(2)
                low_act(3)
                if not first:
                    sums_kept(b - 1)
                F, L, CUM, I = (rows_a[:, r, :] for r in range(4))
                for half in range(2):
                    t0 = slice(half * HALF, (half + 1) * HALF)
                    dve.wait_ge(gates_full, b * 2 + half + 1)
                    dve.tensor_scalar(F[:, t0], ps[half][32:32 + NH, :], gb[32:32 + NH, :], None, ALU.add)
                    dve.tensor_scalar(I[:, t0], ps[half][0:NH, :], gb[0:NH, :], None,
                                      ALU.add).then_inc(gates_read, 1)
                dve.drain()
                dve.scalar_tensor_tensor(out=L, in0=F, scalar=-1.0, in1=F, op0=ALU.mult,
                                         op1=ALU.min).then_inc(gate_abs, 1)

                if not first:
                    sums_read(b - 1)
                dve.drain()
                dve.tensor_scalar(F, F, 0.0, None, ALU.min)
                dve.memset(args, 0.0)
                dve.drain()
                dve.wait_ge(gate_log, b + 1)
                dve.tensor_tensor_scan(CUM, F, L, 0.0, ALU.add, ALU.subtract)
                dve.drain()
                dve.tensor_tensor(I, I, CUM, ALU.subtract)
                dve.drain().then_inc(gate_scan, 1)
                dve.tensor_tensor_scan(F, I, I, -3.0e38, ALU.max, ALU.bypass)
                dve.drain().then_inc(gate_scan, 1)
                Fc = F.rearrange("p (n t) -> p n t", n=NT)
                Ic = I.rearrange("p (n t) -> p n t", n=NT)
                ends = Fc[:, :, P - 1:P]
                dve.scalar_tensor_tensor(out=args[0:NH, :], in0=CUM, scalar=-1.0, in1=F, op0=ALU.mult,
                                         op1=ALU.subtract)
                Dc = args[32:32 + NH, :].rearrange("p (n t) -> p n t", n=NT)
                dve.tensor_tensor(Dc[:, 1:NT, :], ends[:, 0:NT - 1, :].broadcast_to([NH, NT - 1, P]), Fc[:, 1:NT, :],
                                  ALU.subtract)
                dve.tensor_tensor(args[64:64 + NH, :].rearrange("p (n t) -> p n t", n=NT), Ic,
                                  ends.broadcast_to([NH, NT, P]), ALU.subtract)
                dve.memset(dec_row[:, 0:1], 0.0)
                dve.tensor_tensor(dec_row[:, 1:NT], Fc[:, 0:NT - 1, P - 1], Fc[:, 1:NT, P - 1],
                                  ALU.subtract)
                dve.drain().then_inc(gate_args, 1)
                dve.wait_ge(kf_lo, b * 8 + 8)
                dve.wait_ge(hi_ready, b * 2 + 2)
                dve.scalar_tensor_tensor(out=rest_n, in0=F, scalar=-1.0, in1=part_n[0:NH, :], op0=ALU.mult,
                                         op1=ALU.subtract)
                dve.tensor_tensor(rest_a, I, part_a[0:NH, :], ALU.subtract)
                dve.drain()
                dve.tensor_copy(part_n[32:32 + NH, :], rest_n)
                dve.tensor_copy(part_a[32:32 + NH, :], rest_a)
                dve.drain()
                dve.tensor_tensor(part_n[64:64 + NH, :], rest_n, part_n[32:32 + NH, :],
                                  ALU.subtract).then_inc(parts_ready, 1)
                dve.tensor_tensor(part_a[64:64 + NH, :], rest_a, part_a[32:32 + NH, :],
                                  ALU.subtract).then_inc(parts_ready, 1)
                for g in range(2):
                    dve.wait_ge(cols_full, b * 3 + g + 1)
                    dve.tensor_copy(cols[:, 4 * g:4 * g + 4, :],
                                    ps[2 + g][:, :].rearrange("p (n r) -> p n r", n=4)[:, :, 0:GROW]
                                    ).then_inc(cols_ready, 1)
                dve.wait_ge(cols_full, b * 3 + 3)
                dve.tensor_copy(dec[:, :, :].rearrange("p m n -> p (m n)"), ps[4][:, 0:MC * NT]
                                ).then_inc(cols_ready, 1)
                dve.drain()
                dve.tensor_scalar(cols[:, :, 0:NH], cols[:, :, 0:NH], 1e-6, None, ALU.add)

                def weigh(q):
                    dve.wait_ge(s_full, b * NQ + q + 1)
                    dve.wait_ge(d_ready, b * NQ + q + 1)
                    if q >= 2:
                        dve.wait_ge(av_full, b * NQ + q - 1)
                    for par in range(2):
                        t1 = slice(par * 2 * P, (par + 1) * 2 * P)
                        t = dve.tensor_tensor(pbuf[:, q % 2, t1], ps[2 * (q % 2) + par][:, 0:2 * P],
                                              dbuf[:, q % 2, t1], ALU.mult)
                    t.then_inc(p_ready, 1)

                def combine(q):
                    c, hf = unit_cols(q)
                    dst = num[:, c, hf * 4 * VW:(hf + 1) * 4 * VW]
                    dve.wait_ge(av_full, b * NQ + q + 1)
                    if c == 0:
                        dve.tensor_copy(dst, ps[5][:, 0:4 * VW]).then_inc(comb_done, 1)
                    else:
                        dve.tensor_tensor(tmp[:, :].rearrange("p (h v) -> p h v", h=4),
                                          ps[6][:, 0:4 * VW].rearrange("p (h v) -> p h v", h=4),
                                          cols[:, c, 32 + 4 * hf:36 + 4 * hf].unsqueeze(2).broadcast_to([P, 4, VW]),
                                          ALU.mult)
                        dve.drain()
                        dve.tensor_tensor(dst, tmp[:, :], ps[5][:, 0:4 * VW], ALU.add).then_inc(comb_done, 1)

                def update(q):
                    c, hf = unit_cols(q)
                    dve.wait_ge(st_full, b * NS + q + 1)
                    if c > 0:
                        dve.wait_ge(decayed, b * (NS - 2) + q - 1)
                    new = ps[7][:, 0:4 * VW].rearrange("p (m h v) -> p m h v", m=2, h=2)
                    for par in range(2):
                        rows = slice(64 * par, 64 * par + 64)
                        own = state[rows, 2 * hf:2 * hf + 2, par * VW:(par + 1) * VW]
                        if c == 0:
                            t = dve.tensor_copy(own, new[rows, :, par, :])
                        else:
                            t = dve.tensor_tensor(own, own, new[rows, :, par, :], ALU.add)
                    t.then_inc(st_done, 1)

                def pair_cols(i, p):
                    return sm[:, i, p * PW:(p + 1) * PW]

                def divisor(p):
                    dve.drain()
                    den = num4[:, p * PW:(p + 1) * PW, DH]
                    dve.scalar_tensor_tensor(out=pair_cols(0, p), in0=den, scalar=-1.0, in1=den, op0=ALU.mult,
                                             op1=ALU.max)
                    dve.drain()
                    dve.scalar_tensor_tensor(out=pair_cols(0, p).rearrange("p (n h) -> p n h", n=2),
                                             in0=pair_cols(0, p).rearrange("p (n h) -> p n h", n=2), scalar=1e-6,
                                             in1=cols[:, 2 * p:2 * p + 2, 0:NH], op0=ALU.add, op1=ALU.max)
                    dve.drain()
                    dve.scalar_tensor_tensor(out=pair_cols(0, p), in0=pair_cols(0, p), scalar=1e-5,
                                             in1=pair_cols(0, p), op0=ALU.mult, op1=ALU.mult)

                def variance(p):
                    dve.wait_ge(sq_ready, b * NP + p + 1)
                    dve.tensor_reduce(pair_cols(4, p), sq, AX_X, ALU.add)
                    dve.drain()
                    t = dve.scalar_tensor_tensor(out=pair_cols(2, p), in0=pair_cols(4, p), scalar=1.0 / DH,
                                                 in1=pair_cols(0, p), op0=ALU.mult, op1=ALU.add)
                    if p < NP - 1:
                        t.then_inc(var_ready, 1)

                weigh(0)
                for q in range(NQ):
                    if q + 1 < NQ:
                        weigh(q + 1)
                    combine(q)
                    if q < NS:
                        update(q)
                    if q in (4, 8, 12):
                        divisor(q // 4 - 1)
                    if q in (5, 9, 13):
                        variance(q // 4 - 1)
                    if not last:
                        if q == 0:
                            dve.wait_ge(x_in, b * 16 + 32)
                        if q < 8:
                            x_moments(b + 1, q)
                        if q == 9:
                            x_variance()

                def gate(g):
                    m, t0 = gate_unit(g)
                    if g % 4 == 0:
                        dve.wait_ge(skx_ready, b * 2 + g // 4 + 1)
                    dve.wait_ge(ht_full, b * 8 + g + 1)
                    for i in range(2):
                        t = dve.scalar_tensor_tensor(out=gated(g)[:, i, :], in0=ps[g][:, 2 * i * P:2 * (i + 1) * P],
                                                     scalar=pc[:, m + i, PC_NW:PC_NW + 1],
                                                     in1=xa[:, m + i, t0], op0=ALU.mult, op1=ALU.add)
                    t.then_inc(pre_ready, 1)

                def low_part(g):
                    m, t0 = gate_unit(g)
                    dve.wait_ge(h_hi, b * 8 + g + 1)
                    dve.tensor_tensor(xa16[:, 1, m:m + 2, t0], gated(g), xa16[:, 0, m:m + 2, t0],
                                      ALU.subtract).then_inc(h_lo, 1)

                def add(n):
                    dve.wait_ge(dn_full, b * NT + n + 1)
                    dve.tensor_tensor(row(X, b * NT + n), row(X, b * NT + n), ps[n][:, 0:C],
                                      ALU.add).then_inc(x_added, 1)

                p = NP - 1
                divisor(p)
                gate(0)
                gate(1)
                gate(2)
                gate(3)
                low_part(0)
                low_part(1)
                variance(p)
                dve.drain()
                gate(4)
                low_part(2)
                low_part(3)
                inverse_root(dve, pair_cols(3, p), pair_cols(2, p), pair_cols(4, p))
                dve.tensor_tensor(heads[:, p * PW:(p + 1) * PW, :], num4[:, p * PW:(p + 1) * PW, 0:DH],
                                  pair_cols(3, p).unsqueeze(2).broadcast_to([P, PW, DH]),
                                  ALU.mult).then_inc(hn_last, 1)
                gate(5)
                add(0)
                add(1)
                low_part(4)
                dve.drain()
                gate(6)
                gate(7)
                low_part(5)
                add(2)
                add(3)
                low_part(6)
                low_part(7)
                if not last:
                    low_front(b + 1)
                for n in range(4, NT):
                    add(n)
                dve.drain()

            dve.wait_ge(x_in, 16)
            for n in range(NT):
                x_moments(0, n)
            x_variance()
            dve.wait_ge(blk_in, 32)
            wv_heads = s_blk[:, 3, :, :].rearrange("p m (h d) -> p (m h) d", d=DH)
            dve.tensor_reduce(sm[:, 0, 0:NH], wv_heads, AX_X, ALU.add)
            dve.drain()
            dve.tensor_scalar(sm[:, 1, 0:NH], sm[:, 0, 0:NH], 1.0 / DH, None, ALU.mult)
            dve.drain()
            dve.tensor_tensor(wv_heads, wv_heads, sm[:, 1, 0:NH].unsqueeze(2).broadcast_to([P, NH, DH]),
                              ALU.subtract).then_inc(wv_centred, 1)
            dve.wait_ge(w_hi, 1)
            dve.tensor_tensor(wup[:, 1, :, :], s_wup, wup[:, 0, :, :], ALU.subtract)
            dve.tensor_tensor(wdn[:, 1, :, :], s_wdn, wdn[:, 0, :, :], ALU.subtract)
            dve.tensor_tensor(wv[:, 1, :, :], s_blk[:, 3, :, :], wv[:, 0, :, :], ALU.subtract)
            dve.wait_ge(fold_hi, 1)
            dve.scalar_tensor_tensor(out=gk[:, 1, :, :].rearrange("p m c -> p (m c)"), in0=ps[0][:, :],
                                     scalar=DH ** -0.5, in1=gk[:, 0, :, :].rearrange("p m c -> p (m c)"),
                                     op0=ALU.mult, op1=ALU.subtract)
            dve.tensor_tensor(ga[:, 1, :, :].rearrange("p m c -> p (m c)"), ps[1][:, 0:MC * 40],
                              ga[:, 0, :, :].rearrange("p m c -> p (m c)"), ALU.subtract)
            dve.tensor_tensor(gv[:, 1, :, :].rearrange("p m c -> p (m c)"), ps[2][:, 0:MC * 40],
                              gv[:, 0, :, :].rearrange("p m c -> p (m c)"), ALU.subtract).then_inc(w_ready, 1)
            dve.wait_ge(small_in, 80)
            low_front(0)
            batch(0, True, False)
            with dve.Fori(1, B - 1) as b:
                batch(b, False, False)
            batch(B - 1, False, True)
            for n in range(NT):
                sums_moments(B - 1, n)
            sums_variance()
            dve.wait_ge(u_rstd, B)
            for n in range(NT):
                t = dve.tensor_scalar(un[:, n, :], row(X, (B - 1) * NT + n), umv[:, n, 0:1], urstd[:, n:n + 1],
                                      ALU.subtract, ALU.mult)
            t.then_inc(un_ready, 1)
            sums_kept(B - 1)
            sums_read(B - 1)


def build(nc, A, out):
    with ExitStack() as ctx:
        def sb(name, shape, dt=F32):
            return ctx.enter_context(nc.sbuf_tensor(name, shape, dt))

        def sem(name):
            return ctx.enter_context(nc.semaphore(name))

        X = sb("X", [P, B * NT, C])
        ident = sb("ident", [P, P])
        consts = sb("consts", [P, 17])
        usum = sb("usum", [P, KC, B])
        ln_mean = sb("ln_mean", [P, B * NT])
        ln_rstd = sb("ln_rstd", [P, B * NT])
        m1_wst = sb("m1_wst", [P, 2, KC, C])
        m1_in = sem("m1_in")
        wr, br = sb("wr", [P, 2, KC, NE]), sb("br", [B, 2, NE])
        ones4, own = sb("ones4", [B, P]), sb("own", [B, B, TOPK])
        router_in = sem("router_in")
        c_in = sem("c_in")
        v_st6, v_mv = sb("v_st6", [P, NT, 6]), sb("v_mv", [P, NT, 2])
        v_sm, v_neg = sb("v_sm", [P, 8, NT]), sb("v_neg", [P, NT])
        K = {"ident": ident[:, :], "ident_in": c_in, "ones": consts[:, 0:1], "neg_half": consts[:, 1:1 + NT],
             "half": consts[:, 1 + NT:1 + 2 * NT], "wr": wr, "br": br, "ones4": ones4, "own": own,
             "router_in": router_in, "ln_mean": ln_mean, "ln_rstd": ln_rstd,
             "m1_wst": m1_wst, "m1_in": m1_in, "v_stats": (v_st6, v_mv, v_sm, v_neg)}
        c_set = sem("c_set")
        with nc.Block() as block:
            @block.sync
            def _(sp):
                sp.dma_start(ident[:, :], A["ident"]).then_inc(c_in, 16)
                for layer in range(2):
                    sp.dma_start(wr[:, layer, :, :], A[f"e{layer}_wr"]).then_inc(router_in, 16)
                    sp.dma_start(br[:, layer, :], A[f"e{layer}_br"].broadcast_to([B, NE])).then_inc(router_in, 16)
                sp.dma_start(ones4[:, :], A["ones4"]).then_inc(router_in, 16)
                sp.dma_start(own[:, :, :], A["own"]).then_inc(router_in, 16)

            @block.vector
            def _(dve):
                dve.memset(consts[:, 0:1], 1.0)
                dve.memset(consts[:, 1:1 + NT], -0.5)
                dve.memset(consts[:, 1 + NT:1 + 2 * NT], 0.5).then_inc(c_set, 1)
                dve.wait_ge(c_set, 1)
        mixer0(nc, X, K, A, usum)
        experts(nc, X, K, A, usum, 0)
        mixer1(nc, X, K, A, usum)
        experts(nc, X, K, A, usum, 1, out)


def experts(nc, X, K, A, usum, layer, out=None):
    L = f"e{layer}_"
    sems = []
    with ExitStack() as ctx, cleared(nc, sems), ExitStack() as stage:
        def sb(name, shape, dt=F32):
            return ctx.enter_context(nc.sbuf_tensor(L + name, shape, dt))

        def sem(name):
            sems.append(ctx.enter_context(nc.semaphore(name)))
            return sems[-1]

        ps = [ctx.enter_context(nc.psum_tensor(f"{L}ps{i}", [P, HALF], F32)) for i in range(8)]
        wr, br, ones4, own, router_in = K["wr"], K["br"], K["ones4"], K["own"], K["router_in"]
        gam, bet = sb("gam", [P, C]), sb("bet", [P, C])
        lg, rw, ex = sb("lg", [B, NE]), sb("rw", [B, NE]), sb("ex", [B, NE])
        sc = sb("sc", [B, 12])
        top, idx = sb("top", [B, NE]), sb("idx", [B, NE], U32)
        wexp = sb("wexp", [B, B, TOPK])
        idx_row = sb("idx_row", [1, B * TOPK], U32)
        wcol = sb("wcol", [P, B, TOPK])
        s1, s2 = sb("s1", [P, TOPK, KC, FF]), sb("s2", [P, TOPK, FC, C])
        sb1, sb2 = sb("sb1", [P, TOPK, FC]), sb("sb2", [P, TOPK, C])
        w1, w2 = sb("w1", [P, TOPK, 2, KC, FF], F16), sb("w2", [P, TOPK, 2, FC, C], F16)
        b1, b2 = sb("b1", [P, TOPK, FC]), sb("b2", [P, C])
        u = sb("u", [P, NT, C])
        y = sb("y", [P, NT, C])
        uf = sb("uf", [P, 2, KC, S], F16)
        g32 = sb("g32", [P, 4, HALF])
        hp = sb("hp", [P, 2, 2, TOPK * FC, HALF], F16)
        yst, ymv = sb("yst", [P, NT, 6]), sb("ymv", [P, NT, 2])
        yvar, yrstd = sb("yvar", [P, NT]), sb("yrstd", [P, NT])

        names = ("small_in lg_full sm_max sm_exp r_rw ld_full sm_max2 sm_exp2 r_top r_exp r_wexp wc_full idx_ok "
                 "idx_in w1_in w2_in w2_scaled w1_hi w2_hi w1_split w2_split wc_read u_ready ut_full uf_hi "
                 "uf_lo h_full g_ready h_lo ub_ready y_full y_read y_stats y_rstd z_ready z_done x_out v_var v_root").split()
        (small_in, lg_full, sm_max, sm_exp, r_rw, ld_full, sm_max2, sm_exp2, r_top, r_exp, r_wexp, wc_full, idx_ok,
         idx_in, w1_in, w2_in, w2_scaled, w1_hi, w2_hi, w1_split, w2_split, wc_read, u_ready, ut_full, uf_hi,
         uf_lo, h_full, g_ready, h_lo, ub_ready, y_full, y_read, y_stats, y_rstd, z_ready, z_done,
         x_out, v_var, v_root) = (sem(L + n) for n in names)
        NU = TOPK * FC
        N2 = 2 * NU

        block = stage.enter_context(nc.Block())

        @block.sync
        def _(sp):
            sp.dma_start(gam[:, :], A[L + "gamma"].broadcast_to([P, C])).then_inc(small_in, 16)
            sp.dma_start(bet[:, :], A[L + "beta"].broadcast_to([P, C])).then_inc(small_in, 16)
            sp.wait_ge(idx_ok, 1)
            sp.dma_start(idx_row[:, :], idx[:, 0:TOPK]).then_inc(idx_in, 16)
            sp.wait_ge(idx_in, 16)

            def experts_of(b):
                return [sp.value_load(idx_row[0:1, bass.ds(b * TOPK + s, 1)], min_val=0, max_val=NE - 1)
                        for s in range(TOPK)]

            def load_first(chosen):
                for s, e in enumerate(chosen):
                    sp.dma_start(s1[:, s, :, :], A[L + "w1"][bass.ds(e, 1), :, :].rearrange(
                        "o (k p) f -> p (o k) f", p=P)).then_inc(w1_in, 16)
                    sp.dma_start(sb1[:, s, :], A[L + "b1"][bass.ds(e, 1), :, :].rearrange(
                        "o p f -> p (o f)")).then_inc(w1_in, 16)

            def load_second(chosen):
                for s, e in enumerate(chosen):
                    sp.dma_start(s2[:, s, :, :], A[L + "w2"][bass.ds(e, 1), :, :].rearrange(
                        "o (k p) f -> p (o k) f", p=P)).then_inc(w2_in, 16)
                    sp.dma_start(sb2[:, s, :], A[L + "b2"][bass.ds(e, 1), :].broadcast_to([P, C])).then_inc(w2_in, 16)

            def store(b):
                if out is not None:
                    sp.wait_ge(z_done, b * NT + NT)
                    sp.dma_start(out[bass.ds(b * S, S), :].rearrange("(n p) c -> p n c", p=P),
                                 X[:, bass.ds(b * NT, NT), :]).then_inc(x_out, 16)

            def reload(b):
                chosen = experts_of(b + 1)
                sp.wait_ge(w1_split, b + 1)
                load_first(chosen)
                sp.wait_ge(w2_split, b + 1)
                load_second(chosen)

            chosen = experts_of(0)
            load_first(chosen)
            load_second(chosen)
            if layer == 0:
                for i, w in enumerate(("adj", "affine")):
                    sp.dma_start(K["m1_wst"][:, i, :, :],
                                 A[w].rearrange("(k p) n -> p k n", p=P)).then_inc(K["m1_in"], 16)
            reload(0)
            with sp.Fori(1, B - 1) as b:
                reload(b)
                store(b - 1)
            store(B - 2)
            if out is not None:
                for n in range((B - 1) * NT, B * NT, 2):
                    sp.wait_ge(z_done, n + 2)
                    sp.dma_start(out[n * P:(n + 2) * P, :].rearrange("(n p) c -> p n c", p=P),
                                 X[:, n:n + 2, :]).then_inc(x_out, 16)
                sp.wait_ge(x_out, 16 * (B - 1 + NT // 2))

        @block.tensor
        def _(pe):
            pe.wait_ge(router_in, 96)
            for k in range(KC):
                t = pe.matmul(ps[0][0:B, 0:NE], usum[:, k, :], wr[:, layer, k, :], start=(k == 0), stop=(k == KC - 1))
            t.then_inc(lg_full, 1)
            pe.wait_ge(r_rw, 1)
            pe.matmul(ps[1][0:B, 0:NE], ones4[:, 0:B], rw[:, :], start=True, stop=True).then_inc(ld_full, 1)
            pe.wait_ge(r_wexp, 1)
            pe.matmul(ps[4][:, 0:B * TOPK], ones4[:, :], wexp[:, :, :].rearrange("b c s -> b (c s)"),
                      start=True, stop=True).then_inc(wc_full, 1)

            def turn(b, half):
                pe.wait_ge(u_ready, b * NT + 4 * half + 4)
                for k in range(KC):
                    g = 2 * half + k
                    for j in range(4):
                        t = pe.transpose(ps[g][:, j * P:(j + 1) * P], u[:, 4 * half + j, k * P:(k + 1) * P],
                                         K["ident"])
                    t.then_inc(ut_full, 1)

            def compute(b, first, last):
                pe.wait_ge(w1_split, b + 1)
                for half in range(2):
                    pe.wait_ge(uf_lo, b * 4 + (4 if half else 2))
                    for j in range(NU):
                        i = half * NU + j
                        s, f = j // FC, j % FC
                        if i == 2:
                            pe.wait_ge(uf_lo, b * 4 + 4)
                        if i >= 4:
                            pe.wait_ge(g_ready, b * N2 + i - 3)
                        for k in range(KC):
                            t = product3(pe, ps[i % 4][:, :], [w1[:, s, a, k, f * P:(f + 1) * P] for a in (0, 1)],
                                         [uf[:, a, k, half * HALF:(half + 1) * HALF] for a in (0, 1)],
                                         k == 0, k == KC - 1)
                        t.then_inc(h_full, 1)
                pe.wait_ge(w2_split, b + 1)
                for n in range(NT):
                    half = n // 4
                    if n % 4 == 0:
                        pe.wait_ge(h_lo, b * N2 + (half + 1) * NU)
                    if n >= 4 or not first:
                        pe.wait_ge(y_read, b * NT + n - 3)
                    for j in range(NU):
                        s, f = j // FC, j % FC
                        t = product3(pe, ps[4 + n % 4][:, 0:C],
                                     [hp[:, half, a, j, (n % 4) * P:(n % 4 + 1) * P] for a in (0, 1)],
                                     [w2[:, s, a, f, :] for a in (0, 1)], j == 0, j == NU - 1)
                    t.then_inc(y_full, 1)
                    if n == 3 and not last:
                        pe.wait_ge(g_ready, b * N2 + N2)
                        turn(b + 1, 0)
                    if n == 5 and not last:
                        turn(b + 1, 1)

            turn(0, 0)
            turn(0, 1)
            pe.wait_ge(wc_read, 1)
            compute(0, True, False)
            with pe.Fori(1, B - 1) as b:
                compute(b, False, False)
            compute(B - 1, False, True)

        @block.scalar
        def _(act):
            act.wait_ge(sm_max, 1)
            act.activation(ex[:, :], lg[:, :], ACT.Exp, bias=sc[:, 0:1], accum_out=sc[:, 1:2]).then_inc(sm_exp, 1)
            act.wait_ge(sm_max2, 1)
            act.activation(ex[:, :], lg[:, :], ACT.Exp, bias=sc[:, 3:4], accum_out=sc[:, 4:5]).then_inc(sm_exp2, 1)
            act.wait_ge(r_top, 1)
            act.activation(sc[:, 7:8], sc[:, 6:7], ACT.Exp).then_inc(r_exp, 1)

            def turn_parts(b, half):
                for k in range(KC):
                    act.wait_ge(ut_full, b * 4 + 2 * half + k + 1)
                    act.activation(uf[:, 0, k, half * HALF:(half + 1) * HALF], ps[2 * half + k][:, :],
                                   ACT.Identity).then_inc(uf_hi, 1)

            def first_weights(b):
                act.drain()
                act.wait_ge(w1_in, b * 64 + 64)
                act.activation(b1[:, :, :], sb1[:, :, :], ACT.Identity)
                for s in range(TOPK):
                    act.activation(w1[:, s, 0, :, :], s1[:, s, :, :], ACT.Identity).then_inc(w1_hi, 1)
                act.drain()

            def hidden(b, i):
                s, f = (i % NU) // FC, i % FC
                act.wait_ge(h_full, b * N2 + i + 1)
                if i >= 4:
                    act.wait_ge(h_lo, b * N2 + i - 3)
                act.activation(hp[:, i // NU, 0, i % NU, :], ps[i % 4][:, :], ACT.Gelu, bias=b1[:, s, f:f + 1])
                act.activation(g32[:, i % 4, :], ps[i % 4][:, :], ACT.Gelu,
                               bias=b1[:, s, f:f + 1]).then_inc(g_ready, 1)

            def compute(b, last):
                for i in range(N2):
                    hidden(b, i)
                    if i in (1, 3):
                        s = i // 2
                        act.wait_ge(w2_scaled, b * TOPK + s + 1)
                        act.activation(w2[:, s, 0, :, :], s2[:, s, :, :], ACT.Identity).then_inc(w2_hi, 1)
                if not last:
                    first_weights(b + 1)
                    for half in range(2):
                        turn_parts(b + 1, half)

            first_weights(0)
            for half in range(2):
                turn_parts(0, half)
            with act.Fori(0, B - 1) as b:
                compute(b, False)
            compute(B - 1, True)

        @block.gpsimd
        def _(pool):

            def tail(b):
                pool.wait_ge(y_stats, b + 1)
                pool.tensor_tensor(yrstd[:, :], yvar[:, :], K["neg_half"], ALU.pow).then_inc(y_rstd, 1)
                for n in range(NT):
                    pool.wait_ge(z_ready, b * NT + n + 1)
                    pool.tensor_tensor(y[:, n, :], y[:, n, :], gam[:, :], ALU.mult)
                for n in range(NT):
                    if n == 0:
                        pool.drain()
                    pool.tensor_tensor(y[:, n, :], y[:, n, :], bet[:, :], ALU.add)
                pool.drain()
                for n in range(NT):
                    pool.tensor_tensor(row(X, b * NT + n), row(X, b * NT + n), y[:, n, :], ALU.add).then_inc(z_done, 1)
                pool.drain()

            def with_bias(b):
                pool.wait_ge(w2_split, b + 1)
                for n in range(NT):
                    pool.tensor_tensor(y[:, n, :], u[:, n, :], b2[:, :], ALU.add).then_inc(ub_ready, 1)

            with_bias(0)
            pool.wait_ge(small_in, 32)
            with pool.Fori(1, B - 1) as b:
                tail(b - 1)
                with_bias(b)
            tail(B - 2)
            with_bias(B - 1)
            if layer == 0:
                sm = K["v_stats"][2]
                pool.wait_ge(v_var, 1)
                pool.tensor_tensor(sm[:, 1, :], sm[:, 0, :], K["neg_half"], ALU.pow).then_inc(v_root, 1)
                pool.wait_ge(v_var, 2)
                pool.tensor_tensor(sm[:, 4, :], sm[:, 2, :], K["neg_half"], ALU.pow).then_inc(v_root, 1)
                pool.tensor_tensor(sm[:, 5, :], sm[:, 2, :], K["half"], ALU.pow).then_inc(v_root, 1)
            pool.wait_ge(y_stats, B)
            pool.tensor_tensor(yrstd[:, :], yvar[:, :], K["neg_half"], ALU.pow).then_inc(y_rstd, 1)
            for n in range(NT):
                pool.wait_ge(z_ready, (B - 1) * NT + n + 1)
                pool.tensor_tensor(row(X, (B - 1) * NT + n), row(X, (B - 1) * NT + n), y[:, n, :],
                                   ALU.add).then_inc(z_done, 1)

        @block.vector
        def _(dve):
            dve.wait_ge(router_in, 96)
            dve.wait_ge(lg_full, 1)
            dve.scalar_tensor_tensor(out=lg[:, :], in0=ps[0][0:B, 0:NE], scalar=1.0 / S, in1=br[:, layer, :],
                                     op0=ALU.mult, op1=ALU.add)
            dve.drain()
            dve.tensor_reduce(sc[:, 8:9], lg[:, :], AX_X, ALU.max)
            dve.drain()
            dve.tensor_scalar(sc[:, 0:1], sc[:, 8:9], -1.0, None, ALU.mult).then_inc(sm_max, 1)
            dve.wait_ge(sm_exp, 1)
            dve.reciprocal(sc[:, 2:3], sc[:, 1:2])
            dve.drain()
            dve.tensor_scalar(rw[:, :], ex[:, :], sc[:, 2:3], None, ALU.mult).then_inc(r_rw, 1)
            dve.wait_ge(ld_full, 1)
            dve.tensor_scalar(lg[:, :], ps[1][0:B, 0:NE], float(S), None, ALU.mult)
            dve.drain()
            dve.reciprocal(lg[:, :], lg[:, :])
            dve.drain()
            dve.tensor_scalar(lg[:, :], lg[:, :], CAPACITY, 1.0, ALU.mult, ALU.min)
            dve.drain()
            dve.tensor_tensor(lg[:, :], lg[:, :], rw[:, :], ALU.mult)
            dve.drain()
            dve.tensor_reduce(sc[:, 9:10], lg[:, :], AX_X, ALU.max)
            dve.drain()
            dve.tensor_scalar(sc[:, 3:4], sc[:, 9:10], -1.0, None, ALU.mult).then_inc(sm_max2, 1)
            dve.wait_ge(sm_exp2, 1)
            dve.reciprocal(sc[:, 5:6], sc[:, 4:5])
            dve.drain()
            dve.tensor_scalar(rw[:, :], ex[:, :], sc[:, 5:6], None, ALU.mult)
            dve.drain()
            dve.max(top[:, :], rw[:, :])
            dve.drain()
            dve.max_index(idx[:, :], top[:, :], rw[:, :]).then_inc(idx_ok, 1)
            dve.tensor_tensor(sc[:, 6:7], top[:, 1:2], top[:, 0:1], ALU.subtract).then_inc(r_top, 1)
            dve.wait_ge(r_exp, 1)
            dve.tensor_scalar(sc[:, 8:9], sc[:, 7:8], 1.0, None, ALU.add)
            dve.drain()
            dve.reciprocal(sc[:, 10:11], sc[:, 8:9])
            dve.drain()
            dve.tensor_tensor(sc[:, 11:12], sc[:, 10:11], sc[:, 7:8], ALU.mult)
            dve.drain()
            dve.tensor_tensor(wexp[:, :, :], own[:, :, :],
                              sc[:, 10:12].unsqueeze(1).broadcast_to([B, B, TOPK]), ALU.mult).then_inc(r_wexp, 1)
            dve.wait_ge(wc_full, 1)
            dve.tensor_copy(wcol[:, :, :].rearrange("p b s -> p (b s)"), ps[4][:, 0:B * TOPK]).then_inc(wc_read, 1)
            dve.drain()

            def weight(b, s):
                return wcol[:, bass.ds(b, 1), s:s + 1].rearrange("p o s -> p (o s)")

            def front_norm(b):
                for n in range(NT):
                    dve.tensor_scalar(u[:, n, :], row(X, b * NT + n), K["ln_mean"][:, bass.ds(b * NT + n, 1)],
                                      K["ln_rstd"][:, bass.ds(b * NT + n, 1)],
                                      ALU.subtract, ALU.mult).then_inc(u_ready, 1)

            def first_weights(b, s):
                dve.wait_ge(w1_hi, b * TOPK + s + 1)
                t = dve.tensor_tensor(w1[:, s, 1, :, :], s1[:, s, :, :], w1[:, s, 0, :, :], ALU.subtract)
                if s == TOPK - 1:
                    t.then_inc(w1_split, 1)

            def turn_parts(b, half):
                t0 = slice(half * HALF, (half + 1) * HALF)
                for k in range(KC):
                    dve.wait_ge(uf_hi, b * 4 + 2 * half + k + 1)
                    dve.tensor_tensor(uf[:, 1, k, t0], ps[2 * half + k][:, :], uf[:, 0, k, t0],
                                      ALU.subtract).then_inc(uf_lo, 1)

            def scale_second(b):
                dve.wait_ge(w2_in, b * 64 + 64)
                for s in range(TOPK):
                    dve.tensor_scalar(s2[:, s, :, :], s2[:, s, :, :], weight(b, s), None,
                                      ALU.mult).then_inc(w2_scaled, 1)
                dve.tensor_scalar(b2[:, :], sb2[:, 0, :], weight(b, 0), None, ALU.mult)
                dve.drain()
                dve.scalar_tensor_tensor(out=b2[:, :], in0=sb2[:, 1, :], scalar=weight(b, 1), in1=b2[:, :],
                                         op0=ALU.mult, op1=ALU.add)

            def second_weights(b, s):
                dve.wait_ge(w2_hi, b * TOPK + s + 1)
                t = dve.tensor_tensor(w2[:, s, 1, :, :], s2[:, s, :, :], w2[:, s, 0, :, :], ALU.subtract)
                if s == TOPK - 1:
                    t.then_inc(w2_split, 1)

            def low_hidden(b, i):
                half, j = i // NU, i % NU
                dve.wait_ge(g_ready, b * N2 + i + 1)
                dve.tensor_tensor(hp[:, half, 1, j, :], g32[:, i % 4, :], hp[:, half, 0, j, :],
                                  ALU.subtract).then_inc(h_lo, 1)

            def sum_rows(b, n):
                dve.wait_ge(ub_ready, b * NT + n + 1)
                dve.wait_ge(y_full, b * NT + n + 1)
                dve.tensor_tensor(y[:, n, :], y[:, n, :], ps[4 + n % 4][:, 0:C], ALU.add).then_inc(y_read, 1)
                dve.drain()
                dve.bn_stats(yst[:, n, :], y[:, n, :])

            def sum_stats(b):
                dve.drain()
                for n in range(NT):
                    dve.bn_aggr(ymv[:, n, :], yst[:, n, :])
                dve.drain()
                dve.tensor_scalar(yvar[:, :], ymv[:, :, 1], 1e-5, None, ALU.add).then_inc(y_stats, 1)

            def sum_norm(b, n):
                dve.tensor_scalar(y[:, n, :], y[:, n, :], ymv[:, n, 0:1], yrstd[:, n:n + 1],
                                  ALU.subtract, ALU.mult).then_inc(z_ready, 1)

            st6, mv, sm, xneg = K["v_stats"]

            def v_variance():
                dve.wait_ge(z_done, NT)
                for n in range(NT):
                    dve.bn_stats(st6[:, n, :], X[:, n, :])
                dve.drain()
                for n in range(NT):
                    dve.bn_aggr(mv[:, n, :], st6[:, n, :])
                dve.drain()
                dve.tensor_scalar(sm[:, 0, :], mv[:, :, 1], 1e-6, None, ALU.add).then_inc(v_var, 1)

            def v_square():
                dve.wait_ge(v_root, 1)
                dve.tensor_tensor(sm[:, 2, :], mv[:, :, 1], sm[:, 1, :], ALU.mult)
                dve.drain()
                dve.tensor_tensor(sm[:, 2, :], sm[:, 2, :], sm[:, 1, :], ALU.mult)
                dve.drain()
                dve.tensor_scalar(sm[:, 2, :], sm[:, 2, :], float(C), 1e-24, ALU.mult, ALU.max).then_inc(v_var, 1)

            def v_scale():
                dve.wait_ge(v_root, 3)
                dve.tensor_tensor(sm[:, 4, :], sm[:, 4, :], sm[:, 1, :], ALU.mult)
                dve.tensor_scalar(xneg[:, :], mv[:, :, 0], -1.0, None, ALU.mult)
                dve.drain()
                dve.tensor_tensor(sm[:, 6, :], sm[:, 4, :], xneg[:, :], ALU.mult)

            def compute(b, first, last):
                scale_second(b)
                for i in range(N2):
                    low_hidden(b, i)
                    if i == 0 and not first:
                        dve.wait_ge(y_rstd, b)
                        for n in range(NT):
                            sum_norm(b - 1, n)
                    if i in (3, 5):
                        second_weights(b, (i - 3) // 2)
                if not last:
                    dve.wait_ge(ub_ready, b * NT + NT)
                    front_norm(b + 1)
                v_front = last and layer == 0
                if v_front:
                    v_variance()
                for n in range(NT):
                    sum_rows(b, n)
                    if v_front and n == 5:
                        v_square()
                    if not last:
                        if n in (1, 2):
                            first_weights(b + 1, n - 1)
                        if n in (4, 6):
                            turn_parts(b + 1, n // 2 - 2)
                sum_stats(b)

            front_norm(0)
            for s in range(TOPK):
                first_weights(0, s)
            for half in range(2):
                turn_parts(0, half)
            compute(0, True, False)
            with dve.Fori(1, B - 1) as b:
                compute(b, False, False)
            compute(B - 1, False, True)
            if layer == 0:
                v_scale()
            for n in range(NT):
                if n == 0:
                    dve.wait_ge(small_in, 32)
                dve.scalar_tensor_tensor(out=y[:, n, :], in0=y[:, n, :], scalar=ymv[:, n, 0:1], in1=gam[:, :],
                                         op0=ALU.subtract, op1=ALU.mult)
            dve.drain()
            dve.wait_ge(y_rstd, B)
            for n in range(NT):
                dve.scalar_tensor_tensor(out=y[:, n, :], in0=y[:, n, :], scalar=yrstd[:, n:n + 1], in1=bet[:, :],
                                         op0=ALU.mult, op1=ALU.add).then_inc(z_ready, 1)


def mixer1(nc, X, K, A, usum):
    sems = []
    with ExitStack() as ctx, cleared(nc, sems), ExitStack() as stage:
        def sb(name, shape, dt=F32):
            return ctx.enter_context(nc.sbuf_tensor("m1_" + name, shape, dt))

        def sem(name):
            sems.append(ctx.enter_context(nc.semaphore(name)))
            return sems[-1]

        ps = [ctx.enter_context(nc.psum_tensor(f"m1_ps{i}", [P, HALF], F32)) for i in range(4)]
        pa = [ctx.enter_context(nc.psum_tensor(f"m1_pa{i}", [P, 2 * HALF], F32)) for i in range(2)]
        wst = K["m1_wst"]
        wadj, waff = sb("wadj", [P, 2, KC, C], F16), sb("waff", [P, 2, KC, C], F16)
        aff_b, ln_g, ln_b = sb("aff_b", [P, C]), sb("ln_g", [P, C]), sb("ln_b", [P, C])
        nf = sb("nf", [P, NT, C])
        nf16 = sb("nf16", [P, 2, KC, S], F16)
        g16 = sb("g16", [P, 2, KC, S], F16)
        h32 = sb("h32", [P, 3, C])
        h16 = sb("h16", [P, 2, NT, C], F16)
        pr = sb("pr", [P, 2, S])
        pt16 = sb("pt16", [P, 2, 2, NT, P], F16)
        y = sb("y", [P, 2, C])
        un = sb("un", [P, NT, C])
        st6, mv, sm, xneg = K["v_stats"]
        ust, umv, uvar, urstd = sb("ust", [P, NT, 6]), sb("umv", [P, NT, 2]), sb("uvar", [P, NT]), sb("urstd", [P, NT])
        uneg, ubias = sb("uneg", [P, NT]), sb("ubias", [P, NT])
        mx, nmx = sb("mx", [P, 2]), sb("nmx", [P, 2])
        ssum = sb("ssum", [P, 2])
        yst, ymv, ys = sb("yst", [P, 2, 6]), sb("ymv", [P, 2, 2]), sb("ys", [P, 2, 4])
        names = ("w_in w_hi w_ready x_stats x_rstd n2_ready n_scale nf_scale nf_ready nt_full nf_hi nf_lo "
                 "gf_full gf_hi gf_lo hf_full h_ready h_hi h_lo a_full mx_ready p_ready pt_full pt_hi pt_lo o_full "
                 "y_stats y_rstd y_norm y_aff u_stats u_rstd u_ready u_added us_full us_read").split()
        (w_in, w_hi, w_ready, x_stats, x_rstd, n2_ready, n_scale, nf_scale, nf_ready, nt_full, nf_hi, nf_lo,
         gf_full, gf_hi, gf_lo, hf_full, h_ready, h_hi, h_lo, a_full, mx_ready, p_ready, pt_full, pt_hi, pt_lo,
         o_full, y_stats, y_rstd, y_norm, y_aff, u_stats, u_rstd, u_ready, u_added,
         us_full, us_read) = (sem("m1_" + n) for n in names)
        block = stage.enter_context(nc.Block())

        @block.sync
        def _(sp):
            sp.dma_start(aff_b[:, :], A["affine_b"].broadcast_to([P, C])).then_inc(w_in, 16)
            sp.dma_start(ln_g[:, :], A["ln_g"].broadcast_to([P, C])).then_inc(w_in, 16)
            sp.dma_start(ln_b[:, :], A["ln_b"].broadcast_to([P, C])).then_inc(w_in, 16)
            sp.wait_ge(w_in, 48)

        @block.tensor
        def _(pe):

            def front(b, first):
                for g in range(4):
                    half, k = g // 2, g % 2
                    pe.wait_ge(nf_ready, b * NT + 4 * half + 4)
                    for j in range(4):
                        t = pe.transpose(pa[half][:, k * HALF + j * P:k * HALF + (j + 1) * P],
                                         nf[:, 4 * half + j, k * P:(k + 1) * P], K["ident"])
                    t.then_inc(nt_full, 1)
                for i in range(4):
                    half, d = i // 2, i % 2
                    pe.wait_ge(nf_lo, b * 4 + (2 * half + 2 if i < 2 else 4))
                    if i == 0 and first:
                        pe.wait_ge(w_ready, 1)
                    if i >= 2 and not first:
                        pe.wait_ge(y_norm, b * NT + i - 3)
                    for k in range(KC):
                        t = product3(pe, ps[i][:, :], [wadj[:, a, k, d * P:(d + 1) * P] for a in (0, 1)],
                                     [nf16[:, a, k, half * HALF:(half + 1) * HALF] for a in (0, 1)],
                                     k == 0, k == KC - 1)
                    t.then_inc(gf_full, 1)
                for n in range(NT):
                    if n < 4:
                        pe.wait_ge(gf_lo, b * 4 + n + 1)
                    else:
                        pe.wait_ge(h_ready, b * NT + n - 3)
                    for k in range(KC):
                        t = product3(pe, ps[n % 4][:, 0:C], [nf16[:, a, k, n * P:(n + 1) * P] for a in (0, 1)],
                                     [waff[:, a, k, :] for a in (0, 1)], k == 0, k == KC - 1)
                    t.then_inc(hf_full, 1)

            def sums(b):
                pe.wait_ge(u_added, b * 3 + 3)
                for k in range(KC):
                    t = pe.matmul(ps[3][:, k:k + 1], un[:, 0, k * P:(k + 1) * P], K["ones"], start=True, stop=True)
                t.then_inc(us_full, 1)

            def attention(b, first):
                def logits(n):
                    if n >= 2:
                        pe.wait_ge(p_ready, b * NT + n - 1)
                    for half in range(2):
                        for k in range(KC):
                            t = product3(pe, pa[n % 2][:, half * HALF:(half + 1) * HALF],
                                         [g16[:, a, k, n * P:(n + 1) * P] for a in (0, 1)],
                                         [nf16[:, a, k, half * HALF:(half + 1) * HALF] for a in (0, 1)],
                                         k == 0, k == KC - 1)
                    t.then_inc(a_full, 1)

                def turn(n):
                    pe.wait_ge(p_ready, b * NT + n + 1)
                    for g in range(2):
                        if n >= 1:
                            pe.wait_ge(pt_lo, b * 2 * NT + 2 * n + g - 1)
                        for j in range(4):
                            t = pe.transpose(ps[g][:, j * P:(j + 1) * P], pr[:, n % 2, (4 * g + j) * P:(4 * g + j + 1) * P],
                                             K["ident"])
                        t.then_inc(pt_full, 1)

                def mix(n):
                    pe.wait_ge(pt_lo, b * 2 * NT + 2 * n + 2)
                    if n == 0:
                        pe.wait_ge(h_lo, b * NT + NT)
                    if n == 1 and not first:
                        pe.wait_ge(us_read, b)
                    if n >= 2:
                        pe.wait_ge(y_norm, b * NT + n - 1)
                    for m in range(NT):
                        t = product3(pe, ps[2 + n % 2][:, 0:C], [pt16[:, n % 2, a, m, :] for a in (0, 1)],
                                     [h16[:, a, m, :] for a in (0, 1)], m == 0, m == NT - 1)
                    t.then_inc(o_full, 1)

                logits(0)
                pe.wait_ge(h_ready, b * NT + NT)
                for n in range(NT):
                    if n + 1 < NT:
                        logits(n + 1)
                    if n == 1 and not first:
                        sums(b - 1)
                    turn(n)
                    if n >= 1:
                        mix(n - 1)
                mix(NT - 1)

            front(0, True)
            attention(0, True)
            with pe.Fori(1, B) as b:
                front(b, False)
                attention(b, False)
            pe.wait_ge(u_ready, B)
            for k in range(KC):
                for n in range(NT):
                    t = pe.matmul(ps[3][:, k:k + 1], un[:, n, k * P:(k + 1) * P], K["ones"],
                                  start=(n == 0), stop=(n == NT - 1))
            t.then_inc(us_full, 1)

        @block.scalar
        def _(act):
            def normalise(b, n, first=False):
                if n == 0 and not first:
                    act.wait_ge(nf_scale, b)
                act.activation(nf[:, n, :], row(X, b * NT + n), ACT.Identity, scale=sm[:, 4, n:n + 1],
                               bias=sm[:, 6, n:n + 1]).then_inc(nf_ready, 1)

            def sums_norm(b, rows):
                if rows[0] == 0:
                    act.wait_ge(u_rstd, b + 1)
                for n in rows:
                    t = act.activation(un[:, n, :], row(X, b * NT + n), ACT.Identity, scale=urstd[:, n:n + 1],
                                       bias=ubias[:, n:n + 1])
                if rows[-1] == NT - 1:
                    t.then_inc(u_ready, 1)

            def compute(b, first, last):
                for g in range(4):
                    half, k = g // 2, g % 2
                    act.wait_ge(nt_full, b * 4 + g + 1)
                    act.activation(nf16[:, 0, k, half * HALF:(half + 1) * HALF],
                                   pa[half][:, k * HALF:(k + 1) * HALF], ACT.Identity).then_inc(nf_hi, 1)
                for i in range(4):
                    half, d = i // 2, i % 2
                    act.wait_ge(gf_full, b * 4 + i + 1)
                    act.activation(g16[:, 0, d, half * HALF:(half + 1) * HALF], ps[i][:, :],
                                   ACT.Identity).then_inc(gf_hi, 1)
                for n in range(NT):
                    act.wait_ge(h_ready, b * NT + n + 1)
                    act.activation(h16[:, 0, n, :], h32[:, n % 3, :], ACT.Identity).then_inc(h_hi, 1)
                    if n >= 4 and not first:
                        sums_norm(b - 1, [n - 4])
                if not first:
                    sums_norm(b - 1, range(4, NT))
                for n in range(NT):
                    act.wait_ge(mx_ready, b * NT + n + 1)
                    if n >= 2:
                        act.wait_ge(pt_full, b * 2 * NT + 2 * n - 2)
                        act.wait_ge(y_stats, b * NT + n - 1)
                    act.activation(pr[:, n % 2, :], pa[n % 2][:, :], ACT.Exp, bias=nmx[:, n % 2:n % 2 + 1],
                                   scale=5.0, accum_out=ssum[:, n % 2:n % 2 + 1]).then_inc(p_ready, 1)
                    if n >= 2:
                        act.wait_ge(o_full, b * NT + n - 1)
                    for g in range(2):
                        act.wait_ge(pt_full, b * 2 * NT + 2 * n + g + 1)
                        act.activation(pt16[:, n % 2, 0, 4 * g:4 * g + 4, :].rearrange("p m t -> p (m t)"),
                                       ps[g][:, :], ACT.Identity).then_inc(pt_hi, 1)
                    if n in (5, 6) and not last:
                        for r in range(4 * (n - 5), 4 * (n - 5) + 4):
                            normalise(b + 1, r)

            for n in range(NT):
                normalise(0, n, first=True)
            act.wait_ge(K["m1_in"], 32)
            act.activation(wadj[:, 0, :, :], wst[:, 0, :, :], ACT.Identity)
            act.activation(waff[:, 0, :, :], wst[:, 1, :, :], ACT.Identity).then_inc(w_hi, 1)
            compute(0, True, False)
            with act.Fori(1, B - 1) as b:
                compute(b, False, False)
            compute(B - 1, False, True)
            sums_norm(B - 1, range(NT))

        @block.gpsimd
        def _(pool):
            def x_root(b):
                pool.wait_ge(x_stats, b)
                pool.tensor_tensor(sm[:, 1, :], sm[:, 0, :], K["neg_half"], ALU.pow).then_inc(x_rstd, 1)

            def norm_root(b, i):
                if i == 0:
                    pool.wait_ge(n2_ready, b)
                power = K["half"] if i else K["neg_half"]
                pool.tensor_tensor(sm[:, 4 + i, :], sm[:, 2, :], power, ALU.pow).then_inc(n_scale, 1)

            def sums_root(b):
                pool.wait_ge(u_stats, b + 1)
                pool.tensor_tensor(urstd[:, :], uvar[:, :], K["neg_half"], ALU.pow)
                pool.drain()
                pool.tensor_tensor(ubias[:, :], uneg[:, :], urstd[:, :], ALU.mult).then_inc(u_rstd, 1)

            def sums_add(b):
                pool.wait_ge(u_ready, b + 1)
                for h in (4, 2, 1):
                    pool.tensor_tensor(un[:, 0:h, :], un[:, 0:h, :], un[:, h:2 * h, :], ALU.add).then_inc(u_added, 1)
                    pool.drain()

            def attention(b, first, last):
                if not first:
                    sums_add(b - 1)
                for n in range(NT):
                    pool.wait_ge(y_stats, b * NT + n + 1)
                    pool.tensor_tensor(ys[:, n % 2, 3:4], ys[:, n % 2, 1:2], K["neg_half"][:, 0:1],
                                       ALU.pow).then_inc(y_rstd, 1)
                    pool.wait_ge(y_norm, b * NT + n + 1)
                    pool.tensor_tensor(y[:, n % 2, :], y[:, n % 2, :], ln_g[:, :], ALU.mult)
                    pool.drain()
                    pool.tensor_tensor(y[:, n % 2, :], y[:, n % 2, :], ln_b[:, :], ALU.add).then_inc(y_aff, 1)
                    if n == 1 and not last:
                        x_root(b + 1)
                    if n in (2, 3) and not last:
                        norm_root(b + 1, n - 2)
                sums_root(b)

            pool.wait_ge(w_in, 48)
            attention(0, True, False)
            with pool.Fori(1, B - 1) as b:
                attention(b, False, False)
            attention(B - 1, False, True)

        @block.vector
        def _(dve):
            def x_moments(b, rows):
                for n in rows:
                    dve.bn_stats(st6[:, n, :], row(X, b * NT + n))

            def x_variance():
                dve.drain()
                for n in range(NT):
                    dve.bn_aggr(mv[:, n, :], st6[:, n, :])
                dve.drain()
                dve.tensor_scalar(sm[:, 0, :], mv[:, :, 1], 1e-6, None, ALU.add).then_inc(x_stats, 1)

            def norm_square(b):
                dve.wait_ge(x_rstd, b)
                dve.tensor_tensor(sm[:, 2, :], mv[:, :, 1], sm[:, 1, :], ALU.mult)
                dve.drain()
                dve.tensor_tensor(sm[:, 2, :], sm[:, 2, :], sm[:, 1, :], ALU.mult)
                dve.drain()
                dve.tensor_scalar(sm[:, 2, :], sm[:, 2, :], float(C), 1e-24, ALU.mult, ALU.max).then_inc(n2_ready, 1)

            def norm_scale(b):
                dve.wait_ge(n_scale, b * 2)
                dve.tensor_tensor(sm[:, 4, :], sm[:, 4, :], sm[:, 1, :], ALU.mult)
                dve.tensor_scalar(xneg[:, :], mv[:, :, 0], -1.0, None, ALU.mult)
                dve.drain()
                dve.tensor_tensor(sm[:, 6, :], sm[:, 4, :], xneg[:, :], ALU.mult).then_inc(nf_scale, 1)

            def sums_variance(b):
                dve.drain()
                for n in range(NT):
                    dve.bn_aggr(umv[:, n, :], ust[:, n, :])
                dve.drain()
                dve.tensor_scalar(uvar[:, :], umv[:, :, 1], 1e-5, None, ALU.add)
                dve.tensor_scalar(uneg[:, :], umv[:, :, 0], -1.0, None, ALU.mult).then_inc(u_stats, 1)

            def sums_kept(b):
                dve.wait_ge(u_rstd, b + 1)
                dve.tensor_copy(K["ln_mean"][:, bass.ds(b * NT, NT)], umv[:, :, 0])
                dve.tensor_copy(K["ln_rstd"][:, bass.ds(b * NT, NT)], urstd[:, :])

            def sums_read(b):
                dve.wait_ge(us_full, b + 1)
                dve.tensor_copy(usum[:, :, bass.ds(b, 1)].rearrange("p k o -> p (k o)"),
                                ps[3][:, 0:KC]).then_inc(us_read, 1)

            def out_add(b, n):
                i = n % 2
                dve.wait_ge(y_aff, b * NT + n + 1)
                dve.scalar_tensor_tensor(out=y[:, i, :], in0=y[:, i, :], scalar=0.01, in1=y[:, i, :],
                                         op0=ALU.mult, op1=ALU.max)
                dve.drain()
                dve.tensor_tensor(row(X, b * NT + n), row(X, b * NT + n), y[:, i, :], ALU.add)

            def sums_moments(b, n):
                dve.bn_stats(ust[:, n, :], row(X, b * NT + n))

            def front(b, first):
                for g in range(4):
                    half, k = g // 2, g % 2
                    t0 = slice(half * HALF, (half + 1) * HALF)
                    dve.wait_ge(nf_hi, b * 4 + g + 1)
                    dve.tensor_tensor(nf16[:, 1, k, t0], pa[half][:, k * HALF:(k + 1) * HALF], nf16[:, 0, k, t0],
                                      ALU.subtract).then_inc(nf_lo, 1)
                    if g == 1 and not first:
                        out_add(b - 1, NT - 2)
                        sums_moments(b - 1, NT - 3)
                for i in range(4):
                    half, d = i // 2, i % 2
                    t0 = slice(half * HALF, (half + 1) * HALF)
                    if i == 1 and not first:
                        out_add(b - 1, NT - 1)
                        sums_moments(b - 1, NT - 2)
                    if i == 2 and not first:
                        dve.drain()
                        sums_moments(b - 1, NT - 1)
                    if i == 3 and not first:
                        sums_variance(b - 1)
                    dve.wait_ge(gf_hi, b * 4 + i + 1)
                    dve.tensor_tensor(g16[:, 1, d, t0], ps[i][:, :], g16[:, 0, d, t0],
                                      ALU.subtract).then_inc(gf_lo, 1)
                for n in range(NT + 1):
                    if n < NT:
                        dve.wait_ge(hf_full, b * NT + n + 1)
                        if n >= 3:
                            dve.wait_ge(h_lo, b * NT + n - 2)
                        dve.scalar_tensor_tensor(out=h32[:, n % 3, :], in0=ps[n % 4][:, 0:C], scalar=sm[:, 5, n:n + 1],
                                                 in1=aff_b[:, :], op0=ALU.mult, op1=ALU.add).then_inc(h_ready, 1)
                    if n >= 1:
                        dve.wait_ge(h_hi, b * NT + n)
                        dve.tensor_tensor(h16[:, 1, n - 1, :], h32[:, (n - 1) % 3, :], h16[:, 0, n - 1, :],
                                          ALU.subtract).then_inc(h_lo, 1)
                if not first:
                    sums_kept(b - 1)

            def attention(b, first, last):
                def row_max(n):
                    dve.wait_ge(a_full, b * NT + n + 1)
                    if n >= 2:
                        dve.wait_ge(p_ready, b * NT + n - 1)
                    dve.tensor_reduce(mx[:, n % 2:n % 2 + 1], pa[n % 2][:, :], AX_X, ALU.max)
                    dve.drain()
                    dve.tensor_scalar(nmx[:, n % 2:n % 2 + 1], mx[:, n % 2:n % 2 + 1], -5.0, None,
                                      ALU.mult).then_inc(mx_ready, 1)

                def low_weights(n):
                    for g in range(2):
                        dve.wait_ge(pt_hi, b * 2 * NT + 2 * n + g + 1)
                        dve.tensor_tensor(pt16[:, n % 2, 1, 4 * g:4 * g + 4, :].rearrange("p m t -> p (m t)"),
                                          ps[g][:, :],
                                          pt16[:, n % 2, 0, 4 * g:4 * g + 4, :].rearrange("p m t -> p (m t)"),
                                          ALU.subtract).then_inc(pt_lo, 1)

                def out_stats(n):
                    i = n % 2
                    dve.wait_ge(o_full, b * NT + n + 1)
                    dve.bn_stats(yst[:, i, :], ps[2 + i][:, 0:C])
                    dve.tensor_scalar(ys[:, i, 0:1], ssum[:, i:i + 1], ssum[:, i:i + 1], 1e-5, ALU.mult, ALU.mult)
                    dve.drain()
                    dve.bn_aggr(ymv[:, i, :], yst[:, i, :])
                    dve.drain()
                    dve.tensor_tensor(ys[:, i, 1:2], ymv[:, i, 1:2], ys[:, i, 0:1], ALU.add).then_inc(y_stats, 1)

                def out_norm(n):
                    i = n % 2
                    dve.wait_ge(y_rstd, b * NT + n + 1)
                    dve.tensor_scalar(y[:, i, :], ps[2 + i][:, 0:C], ymv[:, i, 0:1], ys[:, i, 3:4],
                                      ALU.subtract, ALU.mult).then_inc(y_norm, 1)

                row_max(0)
                for n in range(NT):
                    if n + 1 < NT:
                        row_max(n + 1)
                    low_weights(n)
                    if n == 1 and not first:
                        sums_read(b - 1)
                    if not last:
                        if n in (0, 1):
                            x_moments(b + 1, range(4 * n, 4 * n + 4))
                        if n == 2:
                            x_variance()
                        if n == 3:
                            norm_square(b + 1)
                        if n == 5:
                            norm_scale(b + 1)
                    if n >= 1:
                        out_stats(n - 1)
                        if n >= 3:
                            sums_moments(b, n - 3)
                        out_norm(n - 1)
                    if n >= 2:
                        out_add(b, n - 2)
                out_stats(NT - 1)
                out_norm(NT - 1)

            dve.wait_ge(w_in, 48)
            dve.wait_ge(K["m1_in"], 32)
            dve.wait_ge(w_hi, 1)
            dve.tensor_tensor(wadj[:, 1, :, :], wst[:, 0, :, :], wadj[:, 0, :, :], ALU.subtract)
            dve.tensor_tensor(waff[:, 1, :, :], wst[:, 1, :, :], waff[:, 0, :, :], ALU.subtract).then_inc(w_ready, 1)
            front(0, True)
            attention(0, True, False)
            with dve.Fori(1, B - 1) as b:
                front(b, False)
                attention(b, False, False)
            front(B - 1, False)
            attention(B - 1, False, True)
            for n in (NT - 2, NT - 1):
                out_add(B - 1, n)
            dve.drain()
            for n in (NT - 3, NT - 2, NT - 1):
                sums_moments(B - 1, n)
            sums_variance(B - 1)
            sums_kept(B - 1)
            sums_read(B - 1)


def block_diagonal(w):
    w = np.asarray(w)
    full = np.zeros((MC, P // 4, 4, P // 4, 4), w.dtype)
    blocks = w.reshape(MC, P // 4, 4, 4)
    for n in range(P // 4):
        full[:, n, :, n, :] = blocks[:, n]
    return full.reshape(MC, P, P).transpose(1, 0, 2)


def arrange(inputs):
    i = {k: np.asarray(v) for k, v in inputs.items()}
    f = np.float32
    c = np.ascontiguousarray
    a = {"x": i["x"].reshape(B * S, C)}
    a["w_up"] = c(i["L0_conv_W_up"].T)
    a["w_down"] = c(i["L0_conv_W_down"].T)
    wq, wk, wv = i["L0_conv_Wq"], i["L0_conv_Wk"], i["L0_conv_Wv"]
    a["blocks"] = c(np.stack([block_diagonal(w) for w in (wq, wk, wv, wv.transpose(0, 2, 1))], axis=1))
    gates = np.zeros((3 * MC, P, 40), f)
    gates[:, :, 0:NH] = i["L0_conv_W_i"].T.reshape(3 * MC, P, NH)
    gates[:, :, 32:32 + NH] = i["L0_conv_W_f"].T.reshape(3 * MC, P, NH)
    a["w_gates"] = c(gates.reshape(3, MC, P, 40).transpose(2, 0, 1, 3))
    gb = np.zeros((40, 1), f)
    gb[0:NH, 0] = i["L0_conv_b_i"]
    gb[32:32 + NH, 0] = i["L0_conv_b_f"]
    a["gate_bias"] = gb
    chan = np.concatenate([i["L0_conv_conv_w"][:, 0, :], i["L0_conv_conv_b"][:, None],
                           i["L0_conv_norm_w"][:, None], i["L0_conv_skip"][:, None]], axis=1)
    a["chan"] = c(chan.reshape(MC, P, PC_N).transpose(1, 0, 2))
    sel = np.zeros((GROW, NH, P), f)
    for slot in range(NH):
        for g in range(3):
            sel[32 * g + slot_head(slot), slot, :] = 1
    a["sel"] = sel
    pair_sel = np.zeros((NH, MC, P), f)
    for h in range(NH):
        pair_sel[h, h // 2, DH * (h % 2):DH * (h % 2) + DH] = 1
    a["pair_sel"] = pair_sel
    later = np.tril(np.ones((P, P)), -1)
    a["negmask"] = np.repeat((later * -1e30)[:, None, :], 4, axis=1).astype(f)
    a["ident"] = np.eye(P, dtype=f)
    a["ones4"] = np.ones((B, P), f)
    a["own"] = np.repeat(np.eye(B, dtype=f)[:, :, None], TOPK, axis=2)
    for layer in range(2):
        src, dst = f"L{layer}_ffn_", f"e{layer}_"
        a[dst + "wr"] = c(i[src + "Wr"].reshape(KC, P, NE).transpose(1, 0, 2))
        a[dst + "w1"], a[dst + "w2"], a[dst + "b2"] = i[src + "W1"], i[src + "W2"], i[src + "b2"]
        a[dst + "b1"] = c(i[src + "b1"].reshape(NE, FC, P).transpose(0, 2, 1))
        for name in ("br", "gamma", "beta"):
            a[dst + name] = i[src + name][None, :]
    a["adj"] = i["L1_conv_adj_w"]
    a["affine"] = c(i["L1_conv_affine_w"].T)
    for name in ("affine_b", "ln_g", "ln_b"):
        a[name] = i["L1_conv_" + name][None, :]
    return a


def kernel(**inputs):
    import concourse.bacc as bacc
    from concourse.bass_utils import run_bass_kernel_spmd as run

    nc = bacc.Bacc("TRN2", target_bir_lowering=False, num_devices=1)
    arrays, aps = {}, {}
    for name, a in arrange(inputs).items():
        arrays["in_" + name] = a
        aps[name] = nc.dram_tensor("in_" + name, a.shape, mybir.dt.from_np(a.dtype), kind="ExternalInput").ap()
    out = nc.dram_tensor("out_0", (B * S, C), F32, kind="ExternalOutput").ap()
    build(nc, aps, out)
    r = run(nc, [arrays], core_ids=[0])
    return r.results[0]["out_0"].reshape(B, S // 32, 32, C)
```
